# Optimizing a Trainium2 kernel written in Bass

```python
import numpy as np
import jax
import jax.numpy as jnp

def _softmax(x, axis=-1):
    return jax.nn.softmax(x, axis=axis)

def _gelu(x):
    return jax.nn.gelu(x, approximate=True)

def _silu(x):
    return jax.nn.silu(x)

def _sigmoid(x):
    return jax.nn.sigmoid(x)

def _layernorm(x, axis=-1, eps=1e-05):
    m = jnp.mean(x, axis=axis, keepdims=True)
    v = jnp.var(x, axis=axis, keepdims=True)
    return (x - m) / jnp.sqrt(v + eps)

def _scatter_add(tgt, idx, src, axis=0):
    return tgt.at[idx].add(src)

def _segment_sum(src, seg, n):
    return jax.ops.segment_sum(src, seg, n)
kernel_name = 'mk_recurrent_d2_jaxref_r4_14fd29'

def setup_inputs(seed: int=0):
    np.random.seed(seed)
    _w = jnp.asarray

    def _L0_attn_setup():
        import jax, jax.numpy as jnp
        import numpy as np
        import math
        D_MODEL = 256
        LN_EPS = 1e-05

        def _layer_norm(x):
            mu = jnp.mean(x, axis=-1, keepdims=True)
            var = jnp.var(x, axis=-1, keepdims=True)
            return (x - mu) * jax.lax.rsqrt(var + LN_EPS)
        key = jax.random.key(seed)
        ks = jax.random.split(key, 5)
        B, S, D = (4, 512, D_MODEL)
        scale = 1.0 / math.sqrt(D)
        x = jax.random.normal(ks[0], (B, S, D), dtype=jnp.float32)
        Wq = jax.random.normal(ks[1], (D, D), dtype=jnp.float32) * scale
        Wk = jax.random.normal(ks[2], (D, D), dtype=jnp.float32) * scale
        Wv = jax.random.normal(ks[3], (D, D), dtype=jnp.float32) * scale
        Wo = jax.random.normal(ks[4], (D, D), dtype=jnp.float32) * scale
        b = jnp.zeros((D,), dtype=jnp.float32)
        layerscale = 0.0001 * jnp.ones((D,), dtype=jnp.float32)
        return {'x': x, 'Wq': Wq, 'bq': b, 'Wk': Wk, 'bk': b, 'Wv': Wv, 'bv': b, 'Wo': Wo, 'bo': b, 'layerscale': layerscale}
    _L0_attn_in = _L0_attn_setup()

    def _L0_ffn_setup():
        import jax, jax.numpy as jnp
        import numpy as np
        B, S, H = (1, 512, 256)
        E, K = (16, 4)
        G, TG = (4, 2)
        I_MOE = 128
        N_SH = 2
        SCALE = 2.5

        def _mlp(x, gw, uw, dw):
            return jax.nn.silu(x @ gw.T) * (x @ uw.T) @ dw.T

        def _route(x2d, router_weight, e_bias):
            T = x2d.shape[0]
            scores = jax.nn.sigmoid(x2d @ router_weight.T)
            sc = scores + e_bias[None, :]
            group_scores = jnp.sum(jax.lax.top_k(sc.reshape(T, G, E // G), 2)[0], axis=-1)
            _, gidx = jax.lax.top_k(group_scores, TG)
            gmask = jnp.zeros((T, G), sc.dtype).at[jnp.arange(T)[:, None], gidx].set(1.0)
            smask = jnp.repeat(gmask, E // G, axis=1)
            masked = jnp.where(smask > 0, sc, 0.0)
            _, tidx = jax.lax.top_k(masked, K)
            tw = jnp.take_along_axis(scores, tidx, axis=1)
            tw = tw / (jnp.sum(tw, axis=-1, keepdims=True) + 1e-20)
            tw = tw * SCALE
            return (tidx, tw)

        def _moe_forward(hidden_states, router_weight, e_bias, gate_w, up_w, down_w, sh_gate_w, sh_up_w, sh_down_w):
            orig_shape = hidden_states.shape
            x = hidden_states.reshape(-1, H)
            T = x.shape[0]
            tidx, tw = _route(x, router_weight, e_bias)
            g = jnp.einsum('th,eih->tei', x, gate_w)
            u = jnp.einsum('th,eih->tei', x, up_w)
            h = jax.nn.silu(g) * u
            yo = jnp.einsum('tei,ehi->teh', h, down_w)
            combine = jnp.zeros((T, E), tw.dtype).at[jnp.arange(T)[:, None], tidx].add(tw)
            routed = jnp.einsum('te,teh->th', combine, yo)
            shared = _mlp(hidden_states.reshape(-1, H), sh_gate_w, sh_up_w, sh_down_w)
            return (routed + shared).reshape(orig_shape)
        key = jax.random.key(seed)
        ks = jax.random.split(key, 9)
        s = 0.02
        return {'hidden_states': jax.random.normal(ks[0], (B, S, H), jnp.float32), 'router_weight': jax.random.normal(ks[1], (E, H), jnp.float32) * s, 'e_bias': jnp.zeros((E,), jnp.float32), 'gate_w': jax.random.normal(ks[2], (E, I_MOE, H), jnp.float32) * s, 'up_w': jax.random.normal(ks[3], (E, I_MOE, H), jnp.float32) * s, 'down_w': jax.random.normal(ks[4], (E, H, I_MOE), jnp.float32) * s, 'sh_gate_w': jax.random.normal(ks[5], (N_SH * I_MOE, H), jnp.float32) * s, 'sh_up_w': jax.random.normal(ks[6], (N_SH * I_MOE, H), jnp.float32) * s, 'sh_down_w': jax.random.normal(ks[7], (H, N_SH * I_MOE), jnp.float32) * s}
    _L0_ffn_in = _L0_ffn_setup()

    def _L1_attn_setup():
        import jax, jax.numpy as jnp
        import numpy as np
        import math
        IN_FEATURES = 256
        OUT_FEATURES = 256
        N_BANK = 2048
        N_LAYER = 12
        N_EMBD = 256
        key = jax.random.key(seed)
        kq, kk, kv = jax.random.split(key, 3)
        q = jax.random.normal(kq, (4, 512, IN_FEATURES), dtype=jnp.float32)
        k = 0.02 * jax.random.normal(kk, (N_BANK, IN_FEATURES), dtype=jnp.float32)
        v_std = 2.0 / N_LAYER / math.sqrt(N_EMBD)
        v = v_std * jax.random.normal(kv, (N_BANK, OUT_FEATURES), dtype=jnp.float32)
        return {'q': q, 'k': k, 'v': v}
    _L1_attn_in = _L1_attn_setup()

    def _L1_ffn_setup():
        import jax, jax.numpy as jnp
        import numpy as np
        EMB = 256
        FF = 4 * EMB

        def _ternary(w):
            scale = jnp.maximum(jnp.mean(jnp.abs(w)), 1e-08)
            w_t = jnp.clip(jnp.round(w / scale), -1.0, 1.0)
            return w + jax.lax.stop_gradient(w_t - w)
        key = jax.random.key(seed)
        kx, k1, k2, kb1, kb2 = jax.random.split(key, 5)
        x = jax.random.normal(kx, (4, 512, EMB), dtype=jnp.float32)
        lim1 = 1.0 / np.sqrt(EMB)
        lim2 = 1.0 / np.sqrt(FF)
        W1 = jax.random.uniform(k1, (FF, EMB), jnp.float32, -lim1, lim1)
        b1 = jax.random.uniform(kb1, (FF,), jnp.float32, -lim1, lim1)
        W2 = jax.random.uniform(k2, (EMB, FF), jnp.float32, -lim2, lim2)
        b2 = jax.random.uniform(kb2, (EMB,), jnp.float32, -lim2, lim2)
        return {'x': x, 'W1': W1, 'b1': b1, 'W2': W2, 'b2': b2}
    _L1_ffn_in = _L1_ffn_setup()
    _d = {'L0_attn_x': _L0_attn_in['x'], 'L0_attn_Wq': _L0_attn_in['Wq'], 'L0_attn_bq': _L0_attn_in['bq'], 'L0_attn_Wk': _L0_attn_in['Wk'], 'L0_attn_bk': _L0_attn_in['bk'], 'L0_attn_Wv': _L0_attn_in['Wv'], 'L0_attn_bv': _L0_attn_in['bv'], 'L0_attn_Wo': _L0_attn_in['Wo'], 'L0_attn_bo': _L0_attn_in['bo'], 'L0_attn_layerscale': _L0_attn_in['layerscale'], 'L0_ffn_router_weight': _L0_ffn_in['router_weight'], 'L0_ffn_e_bias': _L0_ffn_in['e_bias'], 'L0_ffn_gate_w': _L0_ffn_in['gate_w'], 'L0_ffn_up_w': _L0_ffn_in['up_w'], 'L0_ffn_down_w': _L0_ffn_in['down_w'], 'L0_ffn_sh_gate_w': _L0_ffn_in['sh_gate_w'], 'L0_ffn_sh_up_w': _L0_ffn_in['sh_up_w'], 'L0_ffn_sh_down_w': _L0_ffn_in['sh_down_w'], 'L1_attn_k': _L1_attn_in['k'], 'L1_attn_v': _L1_attn_in['v'], 'L1_ffn_W1': _L1_ffn_in['W1'], 'L1_ffn_b1': _L1_ffn_in['b1'], 'L1_ffn_W2': _L1_ffn_in['W2'], 'L1_ffn_b2': _L1_ffn_in['b2']}
    _x0 = _d['L0_attn_x']
    _d['L0_attn_x'] = jax.random.normal(jax.random.fold_in(jax.random.key(seed), 1), (2, 2048, 256), dtype=_x0.dtype)
    del _x0
    return _d

def reference(L0_attn_x, L0_attn_Wq, L0_attn_bq, L0_attn_Wk, L0_attn_bk, L0_attn_Wv, L0_attn_bv, L0_attn_Wo, L0_attn_bo, L0_attn_layerscale, L0_ffn_router_weight, L0_ffn_e_bias, L0_ffn_gate_w, L0_ffn_up_w, L0_ffn_down_w, L0_ffn_sh_gate_w, L0_ffn_sh_up_w, L0_ffn_sh_down_w, L1_attn_k, L1_attn_v, L1_ffn_W1, L1_ffn_b1, L1_ffn_W2, L1_ffn_b2):

    def _L0_attn_ref(x, Wq, bq, Wk, bk, Wv, bv, Wo, bo, layerscale):
        import jax, jax.numpy as jnp
        import numpy as np
        import math
        D_MODEL = 256
        LN_EPS = 1e-05

        def _layer_norm(x):
            mu = jnp.mean(x, axis=-1, keepdims=True)
            var = jnp.var(x, axis=-1, keepdims=True)
            return (x - mu) * jax.lax.rsqrt(var + LN_EPS)
        B, S, D = x.shape
        q = jnp.einsum('bsd,ed->bse', x, Wq) + bq
        k = jnp.einsum('bsd,ed->bse', x, Wk) + bk
        v = jnp.einsum('bsd,ed->bse', x, Wv) + bv
        qn = _layer_norm(q)
        kn = _layer_norm(k)
        scores = jnp.einsum('bse,bte->bst', qn, kn) / jnp.sqrt(jnp.float32(D))
        attn = jax.nn.sigmoid(scores - jnp.log(jnp.float32(S)))
        out = jnp.einsum('bst,bte->bse', attn, v)
        proj = jnp.einsum('bsd,ed->bse', out, Wo) + bo
        return proj * layerscale

    def _L0_ffn_ref(hidden_states, router_weight, e_bias, gate_w, up_w, down_w, sh_gate_w, sh_up_w, sh_down_w):
        import jax, jax.numpy as jnp
        import numpy as np
        B, S, H = (1, 512, 256)
        E, K = (16, 4)
        G, TG = (4, 2)
        I_MOE = 128
        N_SH = 2
        SCALE = 2.5

        def _mlp(x, gw, uw, dw):
            return jax.nn.silu(x @ gw.T) * (x @ uw.T) @ dw.T

        def _route(x2d, router_weight, e_bias):
            T = x2d.shape[0]
            scores = jax.nn.sigmoid(x2d @ router_weight.T)
            sc = scores + e_bias[None, :]
            group_scores = jnp.sum(jax.lax.top_k(sc.reshape(T, G, E // G), 2)[0], axis=-1)
            _, gidx = jax.lax.top_k(group_scores, TG)
            gmask = jnp.zeros((T, G), sc.dtype).at[jnp.arange(T)[:, None], gidx].set(1.0)
            smask = jnp.repeat(gmask, E // G, axis=1)
            masked = jnp.where(smask > 0, sc, 0.0)
            _, tidx = jax.lax.top_k(masked, K)
            tw = jnp.take_along_axis(scores, tidx, axis=1)
            tw = tw / (jnp.sum(tw, axis=-1, keepdims=True) + 1e-20)
            tw = tw * SCALE
            return (tidx, tw)

        def _moe_forward(hidden_states, router_weight, e_bias, gate_w, up_w, down_w, sh_gate_w, sh_up_w, sh_down_w):
            orig_shape = hidden_states.shape
            x = hidden_states.reshape(-1, H)
            T = x.shape[0]
            tidx, tw = _route(x, router_weight, e_bias)
            g = jnp.einsum('th,eih->tei', x, gate_w)
            u = jnp.einsum('th,eih->tei', x, up_w)
            h = jax.nn.silu(g) * u
            yo = jnp.einsum('tei,ehi->teh', h, down_w)
            combine = jnp.zeros((T, E), tw.dtype).at[jnp.arange(T)[:, None], tidx].add(tw)
            routed = jnp.einsum('te,teh->th', combine, yo)
            shared = _mlp(hidden_states.reshape(-1, H), sh_gate_w, sh_up_w, sh_down_w)
            return (routed + shared).reshape(orig_shape)
        return _moe_forward(hidden_states, router_weight, e_bias, gate_w, up_w, down_w, sh_gate_w, sh_up_w, sh_down_w)

    def _L1_attn_ref(q, k, v):
        import jax, jax.numpy as jnp
        import numpy as np
        import math
        IN_FEATURES = 256
        OUT_FEATURES = 256
        N_BANK = 2048
        N_LAYER = 12
        N_EMBD = 256
        scores = jnp.einsum('btd,nd->btn', q, k)
        sqrt_n = jnp.sqrt(jnp.asarray(scores.shape[-1], scores.dtype))
        norm = jnp.linalg.norm(scores, axis=-1, keepdims=True)
        gated = jax.nn.gelu(scores / norm * sqrt_n, approximate=False)
        return jnp.einsum('btn,no->bto', gated, v)

    def _L1_ffn_ref(x, W1, b1, W2, b2):
        import jax, jax.numpy as jnp
        import numpy as np
        EMB = 256
        FF = 4 * EMB

        def _ternary(w):
            scale = jnp.maximum(jnp.mean(jnp.abs(w)), 1e-08)
            w_t = jnp.clip(jnp.round(w / scale), -1.0, 1.0)
            return w + jax.lax.stop_gradient(w_t - w)
        h = jnp.einsum('bsd,fd->bsf', x, _ternary(W1)) + b1
        h = jax.nn.gelu(h, approximate=False)
        out = jnp.einsum('bsf,df->bsd', h, _ternary(W2)) + b2
        return out
    x = L0_attn_x
    xn = _layernorm(x, axis=-1)
    s = _L0_attn_ref(xn, L0_attn_Wq, L0_attn_bq, L0_attn_Wk, L0_attn_bk, L0_attn_Wv, L0_attn_bv, L0_attn_Wo, L0_attn_bo, L0_attn_layerscale)
    g = _silu(_L0_ffn_ref(xn, L0_ffn_router_weight, L0_ffn_e_bias, L0_ffn_gate_w, L0_ffn_up_w, L0_ffn_down_w, L0_ffn_sh_gate_w, L0_ffn_sh_up_w, L0_ffn_sh_down_w))
    x = x + s * g
    xn = _layernorm(x, axis=-1)
    s = _L1_attn_ref(xn, L1_attn_k, L1_attn_v)
    g = _silu(_L1_ffn_ref(xn, L1_ffn_W1, L1_ffn_b1, L1_ffn_W2, L1_ffn_b2))
    x = x + s * g
    return x

_drawn_inputs = setup_inputs


def setup_inputs(seed=0):
    import zlib

    import numpy as np

    out = dict(_drawn_inputs(seed))
    spreads = {'L0_attn_bq': (0.0, 2.0),
     'L0_attn_bk': (0.0, 2.0),
     'L0_attn_bv': (0.0, 2.0),
     'L0_attn_bo': (0.0, 2.0),
     'L0_attn_layerscale': (9.999999747378752e-05, 0.6),
     'L0_ffn_e_bias': (0.0, 2.0)}
    factors = {'L0_attn_Wq': 26.06,
     'L0_attn_Wk': 26.167,
     'L0_attn_Wv': 24.749,
     'L0_attn_Wo': 8.0,
     'L0_ffn_router_weight': 39.102,
     'L0_ffn_gate_w': 26.92,
     'L0_ffn_up_w': 23.814,
     'L0_ffn_down_w': 24.147,
     'L0_ffn_sh_gate_w': 29.041,
     'L0_ffn_sh_up_w': 25.884,
     'L0_ffn_sh_down_w': 26.128,
     'L1_ffn_b1': 23.744,
     'L1_ffn_b2': 64.0}
    for name, (base, spread) in spreads.items():
        noise = np.random.default_rng([zlib.crc32(name.encode()), seed]).standard_normal(out[name].shape)
        drawn = base * np.exp(spread * noise) if base else spread * noise
        out[name] = jnp.asarray(drawn.astype(out[name].dtype))
    for name, factor in factors.items():
        out[name] = (out[name] * factor).astype(out[name].dtype)
    return out
```

```python
from contextlib import ExitStack
import math

import concourse.bass as bass
from concourse import mybir

P = 128
D = 256
KC = D // P
B, S = 2, 2048
T = B * S
TT = T // P
G4 = 4
NCH = TT // G4
CW = G4 * P
E = 16
TOPK, GROUPS, GTOP = 4, 4, 2
EPG = E // GROUPS
NE = E + 2
IM = 128
NP2 = NE // 2
NB = 2048
FF = 1024
EPS = 1e-5

F32 = mybir.dt.float32
F16 = mybir.dt.float16
ALU = mybir.AluOpType
ACT = mybir.ActivationFunctionType
AXX = mybir.AxisListType.X

X_S = 64.0
WQK_S = 16.0
WO_S = 64.0
WP_S = 4.0
V_S = 0.25
ATT_S = 2.0 ** 14
H_S = 0.25
K_S = 1024.0
GRAM_S = 64.0
QS_S = 16.0
GE_S = 64.0
QK_PS = X_S * WQK_S
VP_PS = X_S * WP_S


def build(nc, a, out):
    with ExitStack() as ctx:
        def sb(name, shape, dt=F32):
            return ctx.enter_context(nc.sbuf_tensor(name, shape, dt))

        def sem(name):
            return ctx.enter_context(nc.semaphore(name))

        def dram(name, shape, dt=F32):
            return nc.dram_tensor(name, shape, dt, kind="Internal").ap()

        s0_d = dram("s0_d", [T, D])
        moe_d = dram("moe_d", [T, D])
        x1_d = dram("x1_d", [T, D])
        f_d = dram("f_d", [T, D])

        def chunks(ap):
            return ap.rearrange("(n m p) d -> n p m d", m=G4, p=P)

        x_rows = a["L0_attn_x"].rearrange("b s d -> (b s) d")
        x_c, s0_c, moe_c, x1_c, f_c = (chunks(v) for v in (x_rows, s0_d, moe_d, x1_d, f_d))
        out_c = chunks(out.rearrange("b s d -> (b s) d"))
        moe_t = moe_d.rearrange("(n p) d -> n p d", p=P)

        reg_x = sb("reg_x", [P, 8192])
        reg_qk = sb("reg_qk", [P, 8192])
        reg_v = sb("reg_v", [P, 4096])
        reg_e = sb("reg_e", [P, NE * 512 + NE * D])
        reg_w = sb("reg_w", [P, 3072])

        def f16(r, lo, n):
            return r[:, lo:lo + n].bitcast(F16)

        xT = [f16(reg_x, h * 4096, 4096).rearrange("p (k t) -> p k t", k=KC) for h in range(2)]
        qkT = [f16(reg_qk, h * 4096, 4096).rearrange("p (k t) -> p k t", k=2 * KC) for h in range(2)]
        qsT = [f16(reg_qk, h * 4096, 4096).rearrange("p (k t) -> p k t", k=KC) for h in range(2)]
        vp = [f16(reg_v, h * 2048, 2048).rearrange("p (t e) -> p t e", e=D) for h in range(2)]
        vb = vp
        gu = [f16(reg_e, h * NE * 256, NE * 256).rearrange("p (e k c) -> p e k c", k=KC, c=D) for h in range(2)]
        dn = [f16(reg_e, NE * 512 + h * NE * 128, NE * 128).rearrange("p (e h) -> p e h", h=D) for h in range(2)]

        wqkT = [sb(f"wqkT{h}", [P, KC, 2 * D], F16) for h in range(2)]
        woT = [sb(f"woT{h}", [P, KC, D], F16) for h in range(2)]
        wv = [sb(f"wv{h}", [P, KC, D], F16) for h in range(2)]
        wpT = [sb(f"wpT{h}", [P, KC, D], F16) for h in range(2)]
        kbT = [sb(f"kbT{h}", [P, KC, NB], F16) for h in range(2)]
        gram = [sb(f"gram{h}", [P, KC, D], F16) for h in range(2)]
        w1T = sb("w1T", [P, KC, FF], F16)
        w2T = sb("w2T", [P, FF // P, D], F16)
        rwT = [sb(f"rwT{h}", [P, KC, E], F16) for h in range(2)]
        bvf = sb("bvf", [P, KC])
        bvc = [sb(f"bvc{h}", [P, KC, 33], F16) for h in range(2)]
        bias3 = sb("bias3", [33, 3 * D])
        biasz = sb("biasz", [33, 3 * D], F16)
        ones33 = sb("ones33", [33, P], F16)
        onesf = sb("onesf", [P, P])
        ident = sb("ident", [P, P])
        b1c = sb("b1c", [P, FF // P])
        bo_b = sb("bo_b", [P, D])
        ls_b = sb("ls_b", [P, D])
        b2_b = sb("b2_b", [P, D])
        eb_b = sb("eb_b", [P, E])
        nlogs = sb("nlogs", [P, 1])
        mhalf = sb("mhalf", [P, G4])
        thr = sb("thr", [P, 8])
        comb = sb("comb", [P, TT, NE])

        xin = sb("xin", [P, 2, G4, D])
        stat = sb("stat", [P, 2, G4, 6])
        mv = sb("mv", [P, 2, G4, 2])
        ve = sb("ve", [P, 2, G4])
        rstd = sb("rstd", [P, 2, G4])
        nmr = sb("nmr", [P, 2, G4])
        nn2 = sb("nn2", [P, 2, G4])
        rn2 = sb("rn2", [P, 2, G4])
        att = reg_w[:, 0:1024].rearrange("p (r c) -> p r c", c=CW)
        ah = f16(reg_w, 1024, 1024).rearrange("p (r c) -> p r c", c=CW)
        al = f16(reg_w, 2048, 1024).rearrange("p (r c) -> p r c", c=CW)
        xn = reg_w[:, 0:2048].rearrange("p (b m d) -> p b m d", b=2, d=D)
        sg, t1, hh, mres = (reg_w[:, 512 * i:512 * (i + 1)].rearrange("p (r c) -> p r c", c=D) for i in range(4))
        hT = [f16(reg_w, 2048 + 256 * h, 256).rearrange("p (r c) -> p r c", c=D) for h in range(2)]
        qkn = reg_w[:, 0:1024].rearrange("p (r c) -> p r c", c=2 * D)
        buf_e = [reg_e[:, i * 1024:(i + 1) * 1024].rearrange("p (m d) -> p m d", d=D) for i in range(8)]
        sin, gin, sgb, qsb = buf_e[0:2], buf_e[2:4], buf_e[4:6], buf_e[6:8]
        fbuf, tbuf, gl, xl = buf_e[0:2], buf_e[2:4], buf_e[4:6], buf_e[6:8]
        junk = reg_e[:, 8192:8192 + G4 * D].rearrange("p (m d) -> p m d", d=D)
        st_vb = reg_e[:, 9216:9216 + 4096].rearrange("p (n d) -> p n d", d=D)

        scores, biased, masked, erank = (reg_w[:, 512 * i:512 * (i + 1)] for i in range(4))
        pair_s = reg_w[:, 2048:2816].rearrange("p (n q) -> p n q", q=6)
        xin_f = xin[:, :, :, :].rearrange("p a b c -> p (a b c)")
        gs, grank, gsel = (xin_f[:, 128 * i:128 * (i + 1)] for i in range(3))
        esum = xin_f[:, 384:448]
        gbeat = xin_f[:, 512:1024].rearrange("p (t x) -> p t x", x=GROUPS * GROUPS)
        ebeat = reg_qk[:, :].rearrange("p (t x) -> p t x", x=E * E)

        bank = [ctx.enter_context(nc.psum_tensor(f"bank{i}", [P, 512], F32)) for i in range(8)]
        s_bank, a_bank = bank[:4], bank[4:]
        h_bank = (bank[3], bank[6])

        st_gate = reg_qk[:, 0:4096].rearrange("p (e d) -> p e d", d=D)
        st_up = reg_qk[:, 4096:8192].rearrange("p (e d) -> p e d", d=D)
        st_down = reg_v[:, :].rearrange("p (t e i) -> p t e i", t=KC, e=E)
        st_sg = reg_x[:, 0:512].rearrange("p (t d) -> p t d", d=D)
        st_su = reg_x[:, 512:1024].rearrange("p (t d) -> p t d", d=D)
        st_sd = reg_x[:, 1024:1536].rearrange("p (t i) -> p t i", i=D)
        st_wq, st_wk, st_wv, st_wo = (reg_x[:, 1536 + 512 * i:2048 + 512 * i].rearrange("p (t d) -> p t d", d=D)
                                      for i in range(4))
        st_rw = reg_x[0:E, 3584:3840]
        st_k = reg_x[:, 4096:8192].rearrange("p (n d) -> p n d", d=D)
        kn = [f16(reg_qk, h * 2048, 2048).rearrange("p (n d) -> p n d", d=D) for h in range(2)]
        st_w = [reg_v[:, 0:2048], reg_v[:, 2048:4096]]
        tern = [reg_w[:, 0:2048], xin[:, :, :, :].rearrange("p a b c -> p (a b c)")]
        below = reg_qk[:, 4096:6144]

        def rows(ap):
            return ap.rearrange("(t p) d -> p t d", p=P)

        def row1(ap):
            return ap.rearrange("(o d) -> o d", o=1)

        def spread(ap, axis, n):
            shape = list(ap.shape)
            shape[axis] = n
            return ap.broadcast_to(shape)

        def one(ap, n):
            return ap[bass.ds(n, 1)].rearrange("o p m d -> p (o m) d")

        def by(eng, n, m, body):
            if n > m:
                with eng.Fori(0, n // m - 1) as g:
                    for i in range(m):
                        body(m * g + i, i, g, True)
            for i in range(m):
                body(n - m + i, i, n // m - 1, False)

        CR = 4

        def at(k):
            return k + 1 + CR

        def open_(eng, *sems):
            for q in sems:
                eng.sem_inc(q, CR)

        def gate(eng, waits):
            for q, count in waits:
                eng.wait_ge(q, count)

        ld = {n: sem("ld_" + n) for n in ("qk", "o_v", "rw", "gate", "up", "down", "sh", "bank", "w12", "small", "vb")}
        ident_zero = sem("ident_zero")
        ready_id = sem("ready_id")
        consts = sem("consts")
        w_turned = sem("w_turned")
        w_hi = sem("w_hi")
        w_lo = sem("w_lo")
        nat_hi = sem("nat_hi")
        nat_lo = sem("nat_lo")
        wp_mm, wp_hi, wp_lo = sem("wp_mm"), sem("wp_hi"), sem("wp_lo")
        bias_step = sem("bias_step")
        gram_mm, gram_hi, gram_lo = sem("gram_mm"), sem("gram_hi"), sem("gram_lo")
        tn_sum, tn_tot, tn_step, tn_made = sem("tn_sum"), sem("tn_tot"), sem("tn_step"), sem("tn_made")
        rw_mm, rw_hi, rw_lo = sem("rw_mm"), sem("rw_hi"), sem("rw_lo")

        jobs = []

        def job(need, blocks, hi, lo, scale):
            jobs.append((need, blocks, hi, lo, scale))

        def blk(x3, t, k):
            return x3[:, t, k * P:(k + 1) * P]

        for n, w in enumerate((st_wq, st_wk)):
            job(("qk",), [blk(w, r, k) for k in range(KC) for r in range(KC)],
                wqkT[0][:, :, n * D:(n + 1) * D], wqkT[1][:, :, n * D:(n + 1) * D], WQK_S)
        job(("o_v",), [blk(st_wo, r, k) for k in range(KC) for r in range(KC)],
            woT[0][:, :, :], woT[1][:, :, :], WO_S)
        WO_JOBS = len(jobs)
        for e in range(NE):
            g, u, t = (st_gate, st_up, e) if e < E else (st_sg, st_su, e - E)
            job(("gate", "up") if e < E else ("sh",), [blk(w, t, k) for k in range(KC) for w in (g, u)],
                gu[0][:, e, :, :], gu[1][:, e, :, :], WQK_S)
        for e in range(0, NE, 2):
            src = ([st_down[:, t, x, :] for x in (e, e + 1) for t in range(KC)] if e < E else
                   [st_sd[:, t, x * P:(x + 1) * P] for x in range(2) for t in range(KC)])
            job(("down",) if e < E else ("sh",), src, dn[0][:, e:e + 2, :], dn[1][:, e:e + 2, :], WQK_S)
        DN_JOBS = len(jobs)
        for n in range(0, NB // P, 2):
            job(("bank",), [blk(st_k, n + r, k) for k in range(KC) for r in range(2)],
                kbT[0][:, :, n * P:(n + 2) * P], kbT[1][:, :, n * P:(n + 2) * P], K_S)
        LO_JOBS = len(jobs)
        tern1 = tern[0].rearrange("p (n d) -> p n d", d=D)
        tern2 = tern[1].rearrange("p (t f) -> p t f", f=FF)
        for n in range(0, FF // P, 2):
            job((), [blk(tern1, n + r, k) for k in range(KC) for r in range(2)],
                w1T[:, :, n * P:(n + 2) * P], None, 1.0)
        W1_JOBS = len(jobs)
        for n in range(0, FF // P, 2):
            job((), [tern2[:, t, (n + r) * P:(n + r + 1) * P] for r in range(2) for t in range(KC)],
                w2T[:, n:n + 2, :], None, 1.0)

        def job_ps(j):
            return bank[j % 8][:, :].rearrange("p (k c) -> p k c", k=2)

        bvt = sb("bvt", [P, KC, 33])
        bv_step = sem("bv_step")
        x_ld = [sem(f"x_ld{i}") for i in range(2)]
        ln = {n: sem("ln_" + n) for n in ("mv", "ve", "rs", "xn", "mm", "hi", "lo")}
        rt_mm, rt_sig, rt_step, rt_done = sem("rt_mm"), sem("rt_sig"), sem("rt_step"), sem("rt_done")
        proj = [{n: sem(f"pj{b}_{n}") for n in ("mm", "mv", "ve", "rs", "nmr", "qkn", "vhi", "vlo",
                                               "tr", "thi", "tlo")} for b in range(B)]
        mo = {n: sem("mo_" + n) for n in ("gu", "sig", "t1", "h", "tr", "hi", "lo", "dn", "ev")}
        mo_st = [sem(f"mo_st{i}") for i in range(2)]
        q4 = {n: sem("q4_" + n) for n in ("sig", "m1", "m2", "x1", "mv", "ve", "rs", "xn", "t1", "h1", "l1",
                                         "gm", "nn", "rn", "qs", "t2", "h2", "l2")}
        q4_ld = [sem(f"q4_ld{i}") for i in range(2)]
        q4_st = [sem(f"q4_st{i}") for i in range(2)]
        vb_hi, vb_lo = sem("vb_hi"), sem("vb_lo")
        bk_ld = [sem(f"bk_ld{i}") for i in range(2)]

        class Mix:
            def __init__(self, name, nch, nt, stat, mov, pass1, second, pass2, func, scale, bias, split):
                self.name, self.nch, self.nt = name, nch, nt
                self.stat, self.mov, self.pass1 = stat, mov, pass1
                self.second, self.pass2 = second, pass2
                self.func, self.scale, self.bias, self.split = func, scale, bias, split
                self.first_done = sem(name + "_first")
                self.act_done = sem(name + "_act")
                self.hi_done = sem(name + "_hi")
                self.lo_done = sem(name + "_lo")
                self.second_done = sem(name + "_second")
                self.evac_mid = sem(name + "_mid")
                self.evac_read = sem(name + "_read")
                self.evac_done = sem(name + "_evac")
                self.stored = [sem(name + f"_st{i}") for i in range(2)]

        THREE = ((0, 0), (1, 0), (0, 1))
        at_mix = [Mix(f"at{b}", S // CW, S // P,
                      lambda part, k, j: qkT[part][:, KC + k, j * P:(j + 1) * P],
                      lambda part, k, c: qkT[part][:, k, bass.ds(c * CW, CW)],
                      THREE, lambda part, j: vp[part][:, j, :], THREE,
                      ACT.Sigmoid, 1.0 / (X_S * X_S * math.sqrt(D)), lambda j: nlogs[:, 0:1], ATT_S)
                  for b in range(B)]
        ff_mix = Mix("ff", NCH, FF // P,
                     lambda part, k, j: w1T[:, k, j * P:(j + 1) * P],
                     lambda part, k, c: xT[part][:, k, bass.ds(c * CW, CW)],
                     ((0, 0), (0, 1)), lambda part, j: w2T[:, j, :], ((0, 0), (1, 0)),
                     ACT.Gelu, 1.0 / X_S, lambda j: b1c[:, j:j + 1], GE_S)
        bk_mix = Mix("bk", NCH, NB // P,
                     lambda part, k, j: kbT[part][:, k, j * P:(j + 1) * P],
                     lambda part, k, c: qsT[part][:, k, bass.ds(c * CW, CW)],
                     THREE, lambda part, j: vb[part][:, j, :], THREE,
                     ACT.Gelu, 1.0 / (QS_S * K_S), None, GE_S)
        bk_tanh, bk_silu = sem("bk_tanh"), sem("bk_silu")

        block = ctx.enter_context(nc.Block())

        @block.sync
        def _(sp):
            def load(dst, src, name, **how):
                sp.dma_start(dst, src, **how).then_inc(ld[name], 16)

            for q in mo_st + [q for m in at_mix + [ff_mix, bk_mix] for q in m.stored]:
                sp.sem_inc(q, 16)
            load(st_wq, rows(a["L0_attn_Wq"]), "qk")
            load(st_wk, rows(a["L0_attn_Wk"]), "qk")
            load(st_wo, rows(a["L0_attn_Wo"]), "o_v")
            load(st_wv, rows(a["L0_attn_Wv"]), "o_v")
            load(st_gate, a["L0_ffn_gate_w"].rearrange("e i d -> i e d"), "gate")
            load(st_up, a["L0_ffn_up_w"].rearrange("e i d -> i e d"), "up")
            load(st_sg, rows(a["L0_ffn_sh_gate_w"]), "sh")
            load(st_su, rows(a["L0_ffn_sh_up_w"]), "sh")
            load(st_sd, rows(a["L0_ffn_sh_down_w"]), "sh")
            for t in range(KC):
                load(st_down[:, t, :, :], a["L0_ffn_down_w"][:, t * P:(t + 1) * P, :].rearrange("e h i -> h e i"),
                     "down")
            load(st_rw, a["L0_ffn_router_weight"], "rw")
            load(st_k, rows(a["L1_attn_k"]), "bank")
            sp.wait_ge(consts, 1)
            for n, name in enumerate(("L0_attn_bq", "L0_attn_bk")):
                for r in (0, 32):
                    load(bias3[r:r + 1, n * D:(n + 1) * D], row1(a[name]), "small")
            for dst, name in ((bo_b, "L0_attn_bo"), (ls_b, "L0_attn_layerscale"), (b2_b, "L1_ffn_b2"),
                              (eb_b, "L0_ffn_e_bias")):
                load(dst[:, :], spread(row1(a[name]), 0, P), "small")
            load(bvf[:, :], a["L0_attn_bv"].rearrange("(t p) -> p t", p=P), "small", allow_slow_non_contiguous=True)
            load(b1c[:, :], a["L1_ffn_b1"].rearrange("(t p) -> p t", p=P), "small", allow_slow_non_contiguous=True)
            sp.wait_ge(w_turned, DN_JOBS)
            load(st_w[0].rearrange("p (n d) -> p n d", d=D), rows(a["L1_ffn_W1"]), "w12")
            load(st_w[1].rearrange("p (t f) -> p t f", f=FF), rows(a["L1_ffn_W2"]), "w12")

            sp.wait_ge(w_turned, len(jobs))
            for i in range(2):
                sp.dma_start(xin[:, i, :, :], x_c[i]).then_inc(x_ld[i], 16)

            def next_x(c, i, g, more):
                if more:
                    sp.wait_ge(ln["xn"], at(c))
                    sp.dma_start(xin[:, i, :, :], one(x_c, c + 2)).then_inc(x_ld[i], 16)
            by(sp, NCH, 2, next_x)

            def store_experts(c, i, g, more):
                sp.wait_ge(mo["ev"], at(c))
                sp.dma_start(moe_t[bass.ds(c, 1)].rearrange("o p d -> p (o d)"), mres[:, i, :]
                             ).then_inc(mo_st[i], 16)
            by(sp, TT, 2, store_experts)

            def store_mix(m, dst_c, base, res):
                def store(c, i, g, more):
                    sp.wait_ge(m.evac_done, at(c))
                    sp.dma_start(one(dst_c, base + c), res(i)).then_inc(m.stored[i], 16)
                return store
            for b in range(B):
                by(sp, S // CW, 2, store_mix(at_mix[b], s0_c, b * (S // CW), lambda i: xin[:, i, :, :]))
            for i in range(2):
                sp.wait_ge(mo_st[i], 16 * (TT // 2) + 16)
                for b in range(B):
                    sp.wait_ge(at_mix[b].stored[i], 16 * (S // CW // 2) + 16)

            def load3(n, i):
                sp.dma_start(xin[:, i, :, :], one(x_c, n)).then_inc(q4_ld[i], 16)
                sp.dma_start(sin[i], one(s0_c, n)).then_inc(q4_ld[i], 16)
                sp.dma_start(gin[i], one(moe_c, n)).then_inc(q4_ld[i], 16)
            load3(0, 0)
            load3(1, 1)
            sp.dma_start(st_vb, rows(a["L1_attn_v"])).then_inc(ld["vb"], 16)

            def x1_out(c, i, g, more):
                sp.wait_ge(q4["x1"], at(c))
                sp.dma_start(one(x1_c, c), xin[:, i, :, :]).then_inc(q4_st[i], 16)
                if more:
                    sp.wait_ge(q4["xn"], at(c))
                    sp.wait_ge(q4_st[i], 16 * g + 16)
                    load3(c + 2, i)
            by(sp, NCH, 2, x1_out)
            for i in range(2):
                sp.wait_ge(q4_st[i], 16 * (NCH // 2))

            by(sp, NCH, 2, store_mix(ff_mix, f_c, 0, lambda i: fbuf[i]))
            for i in range(2):
                sp.wait_ge(ff_mix.stored[i], 16 * (NCH // 2) + 16)

            def load2(n, i):
                sp.dma_start(gl[i], one(f_c, n)).then_inc(bk_ld[i], 16)
                sp.dma_start(xl[i], one(x1_c, n)).then_inc(bk_ld[i], 16)
            load2(0, 0)
            load2(1, 1)
            final = store_mix(bk_mix, out_c, 0, lambda i: fbuf[i])

            def out_rows(c, i, g, more):
                final(c, i, g, more)
                if more:
                    load2(c + 2, i)
            by(sp, NCH, 2, out_rows)
            for i in range(2):
                sp.wait_ge(bk_mix.stored[i], 16 * (NCH // 2) + 16)

        end_w = [(w_hi, len(jobs)), (w_lo, LO_JOBS), (wp_lo, 1), (gram_lo, 1), (rw_lo, 1), (bias_step, 4)]
        end_x = [(ln["lo"], at(2 * NCH - 1))]
        end_rt = [(rt_done, 1)]
        end_pj = [[(p["tlo"], at(S // P - 1)), (p["vlo"], at(S // P - 1))] for p in proj]
        end_mo = [(mo["ev"], at(TT - 1))] + [(q, 16 * (TT // 2) + 16) for q in mo_st]
        end_q4 = [(q4["l2"], at(2 * NCH - 1)), (vb_lo, 1)]

        def end_mix(m):
            return [(m.evac_done, at(m.nch - 1))] + [(q, 16 * (m.nch // 2) + 16) for q in m.stored]

        @block.gpsimd
        def _(pool):
            pool.memset(ident[:, :], 0.0).then_inc(ident_zero, 1)
            pool.wait_ge(ident_zero, 1)
            pool.affine_select(out=ident[:, :], in_=ident[:, :], compare_op=ALU.not_equal, fill=1.0, base=0,
                               pattern=[[-1, P]], channel_multiplier=1).then_inc(ready_id, 1)
            pool.memset(mhalf[:, :], -0.5).then_inc(ready_id, 1)
            pool.wait_ge(ready_id, 2)
            open_(pool, ln["rs"], q4["rs"], q4["rn"], *(p["rs"] for p in proj))

            def ln_rows(c, i, g, more):
                pool.wait_ge(ln["ve"], at(c))
                pool.wait_ge(ln["xn"], at(c - 2))
                pool.tensor_tensor(rstd[:, i, :], ve[:, i, :], mhalf[:, :], ALU.pow).then_inc(ln["rs"], 1)
            by(pool, NCH, 2, ln_rows)

            for b in range(B):
                pj = proj[b]

                def qk_rows(c, i, g, more):
                    pool.wait_ge(pj["ve"], at(c))
                    pool.wait_ge(pj["qkn"], at(c - 2))
                    pool.tensor_tensor(rstd[:, i, 0:2], ve[:, i, 0:2], mhalf[:, 0:2], ALU.pow
                                       ).then_inc(pj["rs"], 1)
                by(pool, S // P, 2, qk_rows)

            def second_block(c, i, g, more):
                pool.wait_ge(q4["ve"], at(c))
                pool.wait_ge(q4["xn"], at(c - 2))
                pool.tensor_tensor(rstd[:, i, :], ve[:, i, :], mhalf[:, :], ALU.pow).then_inc(q4["rs"], 1)

            def query_norms(c, i, g, more):
                pool.wait_ge(q4["nn"], at(c))
                pool.wait_ge(q4["qs"], at(c - 2))
                pool.tensor_tensor(rn2[:, i, :], nn2[:, i, :], mhalf[:, :], ALU.pow).then_inc(q4["rn"], 1)

            second_block(0, 0, 0, True)

            def both(c, i, g, more):
                if more or i == 0:
                    second_block(c + 1, 1 - i, None, None)
                query_norms(c, i, g, more)
            by(pool, NCH, 2, both)

        @block.tensor
        def _(pe):
            pe.wait_ge(ready_id, 2)
            pe.wait_ge(consts, 1)
            open_(pe, ln["mm"], mo["gu"], mo["tr"], mo["dn"], q4["t1"], q4["gm"], q4["t2"],
                  *(p[n] for p in proj for n in ("mm", "tr")),
                  *(q for m in at_mix + [ff_mix, bk_mix] for q in (m.first_done, m.second_done)))

            totals = bank[LO_JOBS % 8][:, 0:2]
            loaded = set()
            for j, (need, blocks, hi, lo, scale) in enumerate(jobs):
                for n in need:
                    if n not in loaded:
                        pe.wait_ge(ld[n], 16 * {"qk": 2, "o_v": 2, "sh": 3, "down": KC}.get(n, 1))
                        loaded.add(n)
                if j >= 8:
                    if j - 8 < LO_JOBS:
                        pe.wait_ge(w_lo, j - 7)
                    else:
                        pe.wait_ge(w_hi, j - 7)
                if j == LO_JOBS:
                    pe.wait_ge(tn_sum, 2)
                    pe.matmul(totals, onesf[:, :], thr[:, 0:2], start=True, stop=True).then_inc(tn_tot, 1)
                    pe.wait_ge(tn_made, 1)
                if j == W1_JOBS:
                    pe.wait_ge(tn_made, 2)
                for n, b in enumerate(blocks):
                    mm = pe.transpose(bank[j % 8][:, n * P:(n + 1) * P], b, ident[:, :])
                mm.then_inc(w_turned, 1)

            pe.wait_ge(w_hi, len(jobs))
            pe.wait_ge(w_lo, LO_JOBS)
            pe.wait_ge(nat_lo, 2)
            pe.wait_ge(bv_step, 4)
            pe.wait_ge(ld["rw"], 16)
            for k in range(KC):
                for n, (m, (x, y)) in enumerate([(m, p) for m in range(KC) for p in THREE]):
                    mm = pe.matmul(bank[0][:, k * D:(k + 1) * D], wv[x][:, m, k * P:(k + 1) * P], woT[y][:, m, :],
                                   start=(n == 0), stop=(n == 5))
            mm.then_inc(wp_mm, 1)
            for n, (m, (x, y)) in enumerate([(m, p) for m in range(KC) for p in THREE]):
                mm = pe.matmul(bank[1][0:33, 0:D], bvc[x][:, m, :], woT[y][:, m, :], start=(n == 0), stop=(n == 5))
            mm.then_inc(wp_mm, 1)
            for k in range(KC):
                mm = pe.transpose(bank[2][:, k * E:(k + 1) * E], st_rw[:, k * P:(k + 1) * P], ident[0:E, 0:E])
            mm.then_inc(rw_mm, 1)
            for k in range(KC):
                seq = [(m, p) for m in range(NB // P) for p in THREE]
                for n, (m, (x, y)) in enumerate(seq):
                    mm = pe.matmul(bank[3][:, k * D:(k + 1) * D], kn[x][:, m, k * P:(k + 1) * P], kn[y][:, m, :],
                                   start=(n == 0), stop=(n == len(seq) - 1))
            mm.then_inc(gram_mm, 1)

            gate(pe, end_w)

            def turn(c, i, b, src, banks, done, free, ready):
                pe.wait_ge(ready[0], ready[1])
                pe.wait_ge(free[0], free[1])
                for m in range(2):
                    for k in range(KC):
                        mm = pe.transpose(banks[b][:, k * D + m * P:k * D + (m + 1) * P],
                                          src[:, 2 * b + m, k * P:(k + 1) * P], ident[:, :])
                mm.then_inc(done, 1)

            def turn_x(c, i, g, more):
                for b in range(2):
                    turn(c, i, b, xn[:, i, :, :], s_bank[2 * i:2 * i + 2], ln["mm"],
                         (ln["lo"], at(2 * (c - 2) + b)), (ln["xn"], at(c)))
            by(pe, NCH, 2, turn_x)

            gate(pe, end_x)
            with pe.Fori(0, TT) as t:
                for n, (k, (x, y)) in enumerate([(k, p) for k in range(KC) for p in THREE]):
                    mm = pe.matmul(a_bank[0][:, bass.ds(t * E, E)], xT[x][:, k, bass.ds(t * P, P)], rwT[y][:, k, :],
                                   start=(n == 0), stop=(n == 5))
                mm.then_inc(rt_mm, 1)

            gate(pe, end_rt)

            def gate_up(c, i, p):
                k = c * NP2 + p
                pe.wait_ge(mo["h"], at(k - 3))
                for n, (kc, (x, y)) in enumerate([(kc, q) for kc in range(KC) for q in THREE]):
                    mm = pe.matmul(s_bank[p % 3][:, :].rearrange("p (e c) -> p e c", e=2),
                                   xT[x][:, kc, bass.ds(c * P, P)], gu[y][:, 2 * p:2 * p + 2, kc, :],
                                   start=(n == 0), stop=(n == 5))
                mm.then_inc(mo["gu"], 1)

            def turn_h(c, i, p):
                k = c * NP2 + p
                r = (i * NP2 + p) % 2
                pe.wait_ge(mo["h"], at(k))
                pe.wait_ge(mo["lo"], at(k - 2))
                for e in range(2):
                    mm = pe.transpose(h_bank[r][:, e * P:(e + 1) * P], hh[:, r, e * P:(e + 1) * P],
                                      ident[:, :])
                mm.then_inc(mo["tr"], 1)

            def down(c, i, p):
                k = c * NP2 + p
                r = (i * NP2 + p) % 2
                pe.wait_ge(mo["lo"], at(k))
                if p == 0:
                    pe.wait_ge(mo["ev"], at(c - 2))
                for e in range(2):
                    for n, (x, y) in enumerate(THREE):
                        mm = pe.matmul(a_bank[i][:, 0:D], hT[x][:, r, e * P:(e + 1) * P], dn[y][:, 2 * p + e, :],
                                       start=(p == 0 and e == 0 and n == 0),
                                       stop=(p == NP2 - 1 and e == 1 and n == 2))
                mm.then_inc(mo["dn"], 1)

            def experts(c, i, g, more):
                for p in range(NP2):
                    for lead, what in ((2, gate_up), (1, turn_h), (0, down)):
                        q = p + lead
                        if q < NP2:
                            what(c, i, q)
                        elif more or i == 0:
                            what(c + 1, 1 - i, q - NP2)
            gate_up(0, 0, 0)
            gate_up(0, 0, 1)
            turn_h(0, 0, 0)
            by(pe, TT, 2, experts)

            def mix(m):
                def first(c, j):
                    k = c * m.nt + j
                    pe.wait_ge(m.act_done, at(k - 4))
                    seq = [(kc, q) for kc in range(KC) for q in m.pass1]
                    for n, (kc, (x, y)) in enumerate(seq):
                        mm = pe.matmul(s_bank[j % 4][:, :], m.stat(x, kc, j), m.mov(y, kc, c),
                                       start=(n == 0), stop=(n == len(seq) - 1))
                    mm.then_inc(m.first_done, 1)

                def second(c, i, j):
                    k = c * m.nt + j
                    pe.wait_ge(m.lo_done, at(k))
                    if j == 0:
                        pe.wait_ge(m.evac_read, at(c - 2))
                    for q in range(G4):
                        for n, (x, y) in enumerate(m.pass2):
                            part = (ah, al)[x]
                            mm = pe.matmul(a_bank[2 * i + q // 2][:, (q % 2) * D:(q % 2 + 1) * D],
                                           part[:, j % 4, q * P:(q + 1) * P], m.second(y, j),
                                           start=(j == 0 and n == 0 and q % 2 == 0),
                                           stop=(j == m.nt - 1 and n == len(m.pass2) - 1 and q % 2 == 1),
                                           skip_group_check=True)
                    mm.then_inc(m.second_done, 1)

                def chunk(c, i, g, more):
                    for j in range(m.nt):
                        if j + 2 < m.nt:
                            first(c, j + 2)
                        elif more or i == 0:
                            first(c + 1, j + 2 - m.nt)
                        second(c, i, j)
                first(0, 0)
                first(0, 1)
                by(pe, m.nch, 2, chunk)

            before = end_mo
            for b in range(B):
                pj = proj[b]
                gate(pe, before)

                def project(t, i):
                    pe.wait_ge(pj["qkn"], at(t - 4))
                    pe.matmul(s_bank[i % 4][:, :], ones33[:, :], biasz[:, 0:2 * D], start=True, stop=False)
                    for n, (k, (x, y)) in enumerate([(k, p) for k in range(KC) for p in THREE]):
                        mm = pe.matmul(s_bank[i % 4][:, :], xT[x][:, k, bass.ds(b * S + t * P, P)], wqkT[y][:, k, :],
                                       start=False, stop=(n == 5))
                    pe.wait_ge(pj["vlo"], at(t - 2))
                    v_ps = a_bank[2 + i % 2][:, 0:D]
                    pe.matmul(v_ps, ones33[:, :], biasz[:, 2 * D:3 * D], start=True, stop=False)
                    for n, (k, (x, y)) in enumerate([(k, p) for k in range(KC) for p in THREE]):
                        mm = pe.matmul(v_ps, xT[x][:, k, bass.ds(b * S + t * P, P)], wpT[y][:, k, :],
                                       start=False, stop=(n == 5))
                    mm.then_inc(pj["mm"], 1)

                def turn_qk(t, i, g, more):
                    if more or i == 0:
                        project(t + 3, i + 3)
                    pe.wait_ge(pj["qkn"], at(t))
                    pe.wait_ge(pj["tlo"], at(t - 2))
                    for n in range(2 * KC):
                        mm = pe.transpose(a_bank[i % 2][:, n * P:(n + 1) * P], qkn[:, i % 2, n * P:(n + 1) * P],
                                          ident[:, :])
                    mm.then_inc(pj["tr"], 1)
                for t in range(3):
                    project(t, t)
                by(pe, S // P, 4, turn_qk)
                gate(pe, end_pj[b])
                mix(at_mix[b])
                before = end_mix(at_mix[b])

            gate(pe, before)

            def turn1(c, i):
                for b in range(2):
                    turn(c, i, b, xn[:, i, :, :], s_bank[0:2], q4["t1"],
                         (q4["l1"], at(2 * (c - 1) + b)), (q4["xn"], at(c)))

            def second_block(c, i, g, more):
                if more or i == 0:
                    turn1(c + 1, 1 - i)
                pe.wait_ge(q4["l1"], at(2 * c + 1))
                pe.wait_ge(q4["nn"], at(c - 1))
                for m in range(G4):
                    for n, (k, (x, y)) in enumerate([(k, p) for k in range(KC) for p in THREE]):
                        mm = pe.matmul(a_bank[m][:, 0:D], xT[x][:, k, bass.ds(c * CW + m * P, P)], gram[y][:, k, :],
                                       start=(n == 0), stop=(n == 5))
                mm.then_inc(q4["gm"], 1)
                for b in range(2):
                    turn(c, i, b, qsb[i], s_bank[2:4], q4["t2"],
                         (q4["l2"], at(2 * (c - 1) + b)), (q4["qs"], at(c)))
            turn1(0, 0)
            by(pe, NCH, 2, second_block)

            gate(pe, end_q4)
            mix(ff_mix)
            gate(pe, end_mix(ff_mix))
            mix(bk_mix)

        @block.scalar
        def _(act):
            open_(act, ln["hi"], mo["sig"], mo["hi"], q4["sig"], q4["h1"], q4["qs"], q4["h2"], bk_tanh,
                  *(p[n] for p in proj for n in ("qkn", "vhi", "thi")),
                  *(m.act_done for m in at_mix + [ff_mix, bk_mix]))

            def copy(out_ap, in_ap, scale, done):
                act.activation(out_ap, in_ap, ACT.Copy, scale=scale).then_inc(done, 1)

            for j, (need, blocks, hi, lo, scale) in enumerate(jobs):
                act.wait_ge(w_turned, j + 1)
                copy(hi, job_ps(j), scale, w_hi)
                if j == WO_JOBS:
                    act.wait_ge(ld["o_v"], 32)
                    copy(wv[0][:, :, :], st_wv, WQK_S, nat_hi)
                if j == DN_JOBS:
                    act.wait_ge(ld["bank"], 16)
                    copy(kn[0], st_k, K_S, nat_hi)
            act.wait_ge(wp_mm, 1)
            copy(wpT[0][:, :, :], bank[0][:, :].rearrange("p (k c) -> p k c", k=KC), WP_S / (WQK_S * WO_S), wp_hi)
            act.wait_ge(rw_mm, 1)
            copy(rwT[0][:, :, :], bank[2][:, 0:2 * E].rearrange("p (k c) -> p k c", k=KC), WQK_S, rw_hi)
            act.wait_ge(gram_mm, 1)
            copy(gram[0][:, :, :], bank[3][:, :].rearrange("p (k c) -> p k c", k=KC), GRAM_S / (K_S * K_S), gram_hi)

            def hi_of(c, i, b, banks, dst, scale, turned, done):
                act.wait_ge(turned, at(2 * c + b))
                copy(dst[0][:, :, bass.ds(c * CW + b * D, D)], banks[b][:, :].rearrange("p (k c) -> p k c", k=KC),
                     scale, done)

            gate(act, end_w)

            def hi_x(c, i, g, more):
                for b in range(2):
                    hi_of(c, i, b, s_bank[2 * i:2 * i + 2], xT, X_S, ln["mm"], ln["hi"])
            by(act, NCH, 2, hi_x)

            gate(act, end_x)
            act.wait_ge(rt_mm, TT)
            act.activation(scores[:, :], a_bank[0][:, :], ACT.Sigmoid, scale=1.0 / QK_PS).then_inc(rt_sig, 1)

            gate(act, end_rt)

            def sigmoid_gate(c, i, p):
                k = c * NP2 + p
                r = (i * NP2 + p) % 2
                act.wait_ge(mo["gu"], at(k))
                act.wait_ge(mo["t1"], at(k - 2))
                act.activation(sg[:, r, :].rearrange("p (e c) -> p e c", e=2),
                               s_bank[p % 3][:, :].rearrange("p (e c) -> p e c", e=2)[:, :, 0:IM],
                               ACT.Sigmoid, scale=1.0 / QK_PS).then_inc(mo["sig"], 1)

            def experts(c, i, g, more):
                for p in range(NP2):
                    if p + 1 < NP2:
                        sigmoid_gate(c, i, p + 1)
                    elif more or i == 0:
                        sigmoid_gate(c + 1, 1 - i, 0)
                    k = c * NP2 + p
                    r = (i * NP2 + p) % 2
                    act.wait_ge(mo["tr"], at(k))
                    act.wait_ge(mo["dn"], at(k - 2))
                    copy(hT[0][:, r, :], h_bank[r][:, 0:D], 1.0, mo["hi"])
            sigmoid_gate(0, 0, 0)
            by(act, TT, 2, experts)

            def mix(m, at_chunk=None):
                def chunk(c, i, g, more):
                    for j in range(m.nt):
                        if j == 2 and at_chunk:
                            at_chunk(c, i, g)
                        k = c * m.nt + j
                        act.wait_ge(m.first_done, at(k))
                        act.wait_ge(m.lo_done, at(k - 2))
                        act.activation(att[:, j % 2, :], s_bank[j % 4][:, :], m.func,
                                       bias=m.bias(j) if m.bias else 0.0, scale=m.scale).then_inc(m.act_done, 1)
                by(act, m.nch, 2, chunk)

            before = end_mo
            for b in range(B):
                pj = proj[b]
                gate(act, before)

                def norm_rows(t, i):
                    act.wait_ge(pj["mm"], at(t))
                    copy(vp[0][:, bass.ds(t, 1), :].rearrange("p o e -> p (o e)"), a_bank[2 + i % 2][:, 0:D],
                         V_S / VP_PS, pj["vhi"])
                    act.wait_ge(pj["nmr"], at(t))
                    act.wait_ge(pj["tr"], at(t - 2))
                    for n in range(2):
                        ins = act.activation(qkn[:, i % 2, n * D:(n + 1) * D], s_bank[i % 4][:, n * D:(n + 1) * D],
                                             ACT.Identity, bias=nmr[:, i % 2, n:n + 1], scale=rstd[:, i % 2, n:n + 1])
                    ins.then_inc(pj["qkn"], 1)

                def rows_hi(t, i, g, more):
                    if more or i < 3:
                        norm_rows(t + 1, i + 1)
                    act.wait_ge(pj["tr"], at(t))
                    copy(qkT[0][:, :, bass.ds(t * P, P)], a_bank[i % 2][:, :].rearrange("p (k c) -> p k c", k=2 * KC),
                         X_S, pj["thi"])
                norm_rows(0, 0)
                by(act, S // P, 4, rows_hi)
                gate(act, end_pj[b])
                mix(at_mix[b])
                before = end_mix(at_mix[b])

            gate(act, before)
            act.wait_ge(ld["vb"], 16)
            copy(vb[0], st_vb, K_S, vb_hi)

            def front(c, i, g):
                act.wait_ge(q4_ld[i], 48 * g + 48)
                act.wait_ge(q4["m1"], at(c - 2))
                act.activation(sgb[i], gin[i], ACT.Sigmoid).then_inc(q4["sig"], 1)
                for b in range(2):
                    hi_of(c, i, b, s_bank[0:2], xT, X_S, q4["t1"], q4["h1"])

            def second_block(c, i, g, more):
                if more or i == 0:
                    front(c + 1, 1 - i, g + i)
                act.wait_ge(q4["rn"], at(c))
                act.wait_ge(q4["t2"], at(2 * (c - 2) + 1))
                for m in range(G4):
                    ins = act.activation(qsb[i][:, m, :], xn[:, i, m, :], ACT.Copy, scale=rn2[:, i, m:m + 1])
                ins.then_inc(q4["qs"], 1)
                for b in range(2):
                    hi_of(c, i, b, s_bank[2:4], qsT, QS_S, q4["t2"], q4["h2"])
            front(0, 0, 0)
            by(act, NCH, 2, second_block)

            gate(act, end_q4)
            mix(ff_mix)
            gate(act, end_mix(ff_mix))

            def tanh_half(c, i, g):
                act.wait_ge(bk_ld[i], 32 * g + 32)
                act.wait_ge(bk_silu, at(c - 2))
                act.activation(tbuf[i], gl[i], ACT.Tanh, scale=0.5).then_inc(bk_tanh, 1)
            mix(bk_mix, tanh_half)

        @block.vector
        def _(dve):
            dve.memset(bias3[:, :], 0.0)
            dve.memset(ones33[:, :], X_S)
            dve.memset(onesf[:, :], 1.0)
            dve.memset(nlogs[:, :], -math.log(S)).then_inc(consts, 1)
            open_(dve, *(ln[n] for n in ("mv", "ve", "xn", "lo")),
                  *(p[n] for p in proj for n in ("mv", "ve", "nmr", "vlo", "tlo")),
                  *(mo[n] for n in ("t1", "h", "lo", "ev")),
                  *(q4[n] for n in ("m1", "m2", "x1", "mv", "ve", "xn", "l1", "nn", "l2")), bk_silu,
                  *(q for m in at_mix + [ff_mix, bk_mix] for q in (m.hi_done, m.lo_done, m.evac_mid, m.evac_read,
                                                                  m.evac_done)))

            def low(out_ap, in_ap, scale, hi_ap, done=None):
                ins = dve.scalar_tensor_tensor(out=out_ap, in0=in_ap, scalar=scale, in1=hi_ap, op0=ALU.mult,
                                               op1=ALU.subtract)
                if done is not None:
                    ins.then_inc(done, 1)

            dve.wait_ge(consts, 1)
            dve.wait_ge(ld["small"], 16 * 10)
            for t in range(KC):
                dve.tensor_scalar(bvt[:, t, :], onesf[:, 0:33], bvf[:, t:t + 1], WQK_S, ALU.mult, ALU.mult
                                  ).then_inc(bv_step, 1)
            dve.wait_ge(bv_step, 2)
            dve.tensor_copy(bvc[0][:, :, :], bvt[:, :, :]).then_inc(bv_step, 1)
            dve.wait_ge(bv_step, 3)
            low(bvc[1][:, :, :], bvt[:, :, :], 1.0, bvc[0][:, :, :], bv_step)

            def signs():
                dve.wait_ge(ld["w12"], 32)
                for n in range(2):
                    dve.tensor_reduce(thr[:, n:n + 1], st_w[n], AXX, ALU.add, apply_absolute_value=True
                                      ).then_inc(tn_sum, 1)
                dve.wait_ge(tn_tot, 1)
                dve.tensor_scalar(thr[:, 2:4], bank[LO_JOBS % 8][:, 0:2], 1.0 / (FF * D), 1e-8, ALU.mult, ALU.max
                                  ).then_inc(tn_step, 1)
                dve.wait_ge(tn_step, 1)
                dve.tensor_scalar(thr[:, 4:6], thr[:, 2:4], 0.5, None, ALU.mult)
                dve.tensor_scalar(thr[:, 6:8], thr[:, 2:4], -0.5, None, ALU.mult).then_inc(tn_step, 1)
                dve.wait_ge(tn_step, 2)
                for n in range(2):
                    if n:
                        dve.wait_ge(tn_made, 1)
                    dve.tensor_scalar(below, st_w[n], thr[:, 6 + n:7 + n], None, ALU.is_lt).then_inc(tn_step, 1)
                    dve.wait_ge(tn_step, 3 + n)
                    dve.scalar_tensor_tensor(out=tern[n], in0=st_w[n], scalar=thr[:, 4 + n:5 + n], in1=below,
                                             op0=ALU.is_gt, op1=ALU.subtract).then_inc(tn_made, 1)

            for j, (need, blocks, hi, lo, scale) in enumerate(jobs[:LO_JOBS]):
                dve.wait_ge(w_hi, j + 1)
                low(lo, job_ps(j), scale, hi, w_lo)
                if j == WO_JOBS:
                    dve.wait_ge(nat_hi, 1)
                    low(wv[1][:, :, :], st_wv, WQK_S, wv[0][:, :, :], nat_lo)
                if j == DN_JOBS:
                    dve.wait_ge(nat_hi, 2)
                    low(kn[1], st_k, K_S, kn[0], nat_lo)
            signs()
            dve.wait_ge(wp_hi, 1)
            low(wpT[1][:, :, :], bank[0][:, :].rearrange("p (k c) -> p k c", k=KC), WP_S / (WQK_S * WO_S),
                wpT[0][:, :, :], wp_lo)
            dve.wait_ge(wp_mm, 2)
            for r in (0, 32):
                dve.tensor_scalar(bias3[r:r + 1, 2 * D:3 * D], bank[1][r:r + 1, 0:D],
                                  WP_S / (WQK_S * WQK_S * WO_S), None, ALU.mult).then_inc(bias_step, 1)
            dve.wait_ge(bias_step, 2)
            dve.tensor_scalar(biasz[:, :], bias3[:, :], WQK_S, None, ALU.mult).then_inc(bias_step, 1)
            dve.wait_ge(bias_step, 3)
            low(biasz[32:33, :], bias3[32:33, :], WQK_S, biasz[32:33, :], bias_step)
            dve.wait_ge(rw_hi, 1)
            low(rwT[1][:, :, :], bank[2][:, 0:2 * E].rearrange("p (k c) -> p k c", k=KC), WQK_S, rwT[0][:, :, :],
                rw_lo)
            dve.wait_ge(gram_hi, 1)
            low(gram[1][:, :, :], bank[3][:, :].rearrange("p (k c) -> p k c", k=KC), GRAM_S / (K_S * K_S),
                gram[0][:, :, :], gram_lo)

            def low_of(c, i, b, banks, dst, scale, his, done):
                dve.wait_ge(his, at(2 * c + b))
                cols = bass.ds(c * CW + b * D, D)
                low(dst[1][:, :, cols], banks[b][:, :].rearrange("p (k c) -> p k c", k=KC), scale,
                    dst[0][:, :, cols], done)

            gate(dve, end_w)

            def moments(src, n, i, c, q, eps):
                for m in range(n):
                    dve.bn_stats(stat[:, i, m, :], src(m))
                dve.drain()
                for m in range(n):
                    ins = dve.bn_aggr(mv[:, i, m, :], stat[:, i, m, :])
                ins.then_inc(q["mv"], 1)
                dve.wait_ge(q["mv"], at(c))
                dve.tensor_scalar(ve[:, i, 0:n], mv[:, i, 0:n, 1], eps, None, ALU.add).then_inc(q["ve"], 1)

            def norm(src, i, c, q):
                dve.wait_ge(q["rs"], at(c))
                for m in range(G4):
                    ins = dve.tensor_scalar(xn[:, i, m, :], src[:, i, m, :], mv[:, i, m, 0:1], rstd[:, i, m:m + 1],
                                            ALU.subtract, ALU.mult)
                ins.then_inc(q["xn"], 1)

            def x_moments(c, i, g):
                dve.wait_ge(x_ld[i], 16 * g + 16)
                moments(lambda m: xin[:, i, m, :], G4, i, c, ln, EPS)

            def x_norm(c, i, g, more):
                if more or i == 0:
                    x_moments(c + 1, 1 - i, g + i)
                dve.wait_ge(ln["mm"], at(2 * (c - 2) + 1))
                norm(xin, i, c, ln)
                for b in range(2):
                    low_of(c, i, b, s_bank[2 * i:2 * i + 2], xT, X_S, ln["hi"], ln["lo"])
            x_moments(0, 0, 0)
            by(dve, NCH, 2, x_norm)

            gate(dve, end_x)
            dve.wait_ge(rt_sig, 1)
            count = [0]

            def step(ins):
                count[0] += 1
                ins.then_inc(rt_step, 1)
                dve.wait_ge(rt_step, count[0])

            sc3 = scores[:, :].rearrange("p (t e) -> p t e", e=E)
            b3 = biased[:, :].rearrange("p (t e) -> p t e", e=E)
            step(dve.tensor_tensor(b3, sc3, spread(eb_b[:, :].rearrange("p (o e) -> p o e", o=1), 1, TT), ALU.add))
            b4 = biased[:, :].rearrange("p (n e) -> p n e", e=EPG)
            pairs = [(x, y) for x in range(EPG) for y in range(x + 1, EPG)]
            for n, (x, y) in enumerate(pairs):
                ins = dve.tensor_tensor(pair_s[:, :, n], b4[:, :, x], b4[:, :, y], ALU.add)
            step(ins)
            step(dve.tensor_reduce(gs[:, :], pair_s[:, :, :], AXX, ALU.max))

            def ranks(vals, n, beat, rank):
                dve.memset(beat[:, :, 0:n * n:n + 1], 0.0)
                bt = beat[:, :, :].rearrange("p t (x y) -> p t x y", x=n)
                for x in range(n):
                    for lo_, hi_, op in ((0, x, ALU.is_ge), (x + 1, n, ALU.is_gt)):
                        if hi_ > lo_:
                            ins = dve.tensor_tensor(bt[:, :, x, lo_:hi_], vals[:, :, lo_:hi_],
                                                    spread(vals[:, :, x:x + 1], 2, hi_ - lo_), op)
                step(ins)
                step(dve.tensor_reduce(rank, bt, AXX, ALU.add))

            ranks(gs[:, :].rearrange("p (t g) -> p t g", g=GROUPS), GROUPS, gbeat,
                  grank[:, :].rearrange("p (t g) -> p t g", g=GROUPS))
            step(dve.tensor_scalar(gsel[:, :], grank[:, :], GTOP - 0.5, None, ALU.is_lt))
            step(dve.tensor_tensor(masked[:, :].rearrange("p (n e) -> p n e", e=EPG), b4,
                                   spread(gsel[:, :].rearrange("p (n o) -> p n o", o=1), 2, EPG), ALU.mult))
            m3 = masked[:, :].rearrange("p (t e) -> p t e", e=E)
            ranks(m3, E, ebeat, erank[:, :].rearrange("p (t e) -> p t e", e=E))
            step(dve.scalar_tensor_tensor(out=masked[:, :], in0=erank[:, :], scalar=TOPK - 0.5, in1=scores[:, :],
                                          op0=ALU.is_lt, op1=ALU.mult))
            step(dve.tensor_reduce(esum[:, 0:TT], m3, AXX, ALU.add))
            step(dve.tensor_scalar(esum[:, 0:TT], esum[:, 0:TT], 1e-20, None, ALU.add))
            step(dve.reciprocal(esum[:, TT:2 * TT], esum[:, 0:TT]))
            unit = H_S / (QK_PS * QK_PS)
            dve.memset(comb[:, :, E:NE], unit)
            dve.scalar_tensor_tensor(out=comb[:, :, 0:E], in0=m3, scalar=2.5 * unit,
                                     in1=spread(esum[:, TT:2 * TT].rearrange("p (t o) -> p t o", o=1), 2, E),
                                     op0=ALU.mult, op1=ALU.mult).then_inc(rt_done, 1)

            gate(dve, end_rt)

            def inner(c, i, p):
                k = c * NP2 + p
                r = (i * NP2 + p) % 2
                ps = s_bank[p % 3][:, :].rearrange("p (e c) -> p e c", e=2)
                dve.wait_ge(mo["sig"], at(k))
                dve.tensor_tensor(t1[:, r, :].rearrange("p (e c) -> p e c", e=2),
                                  sg[:, r, :].rearrange("p (e c) -> p e c", e=2), ps[:, :, 0:IM], ALU.mult
                                  ).then_inc(mo["t1"], 1)
                dve.wait_ge(mo["t1"], at(k))
                dve.wait_ge(mo["tr"], at(k - 2))
                for e in range(2):
                    x = 2 * p + e
                    ins = dve.scalar_tensor_tensor(
                        out=hh[:, r, e * IM:(e + 1) * IM], in0=t1[:, r, e * IM:(e + 1) * IM],
                        scalar=comb[:, bass.ds(c, 1), x:x + 1].rearrange("p o e -> p (o e)"), in1=ps[:, e, IM:2 * IM],
                        op0=ALU.mult, op1=ALU.mult)
                ins.then_inc(mo["h"], 1)

            def experts(c, i, g, more):
                for p in range(NP2):
                    if p + 1 < NP2:
                        inner(c, i, p + 1)
                    elif more or i == 0:
                        inner(c + 1, 1 - i, 0)
                    r = (i * NP2 + p) % 2
                    dve.wait_ge(mo["hi"], at(c * NP2 + p))
                    low(hT[1][:, r, :], h_bank[r][:, 0:D], 1.0, hT[0][:, r, :], mo["lo"])
                dve.wait_ge(mo["dn"], at(c * NP2 + NP2 - 1))
                dve.wait_ge(mo_st[i], 16 * g + 16)
                dve.tensor_scalar(mres[:, i, :], a_bank[i][:, 0:D], 1.0 / (H_S * WQK_S), None, ALU.mult
                                  ).then_inc(mo["ev"], 1)
            inner(0, 0, 0)
            by(dve, TT, 2, experts)

            def mix(m, evac, at_chunk=None):
                def split(c, j):
                    k = c * m.nt + j
                    dve.wait_ge(m.act_done, at(k))
                    dve.wait_ge(m.second_done, at(k - 4))
                    dve.tensor_scalar(ah[:, j % 4, :], att[:, j % 2, :], m.split, None, ALU.mult
                                      ).then_inc(m.hi_done, 1)
                    dve.wait_ge(m.hi_done, at(k))
                    low(al[:, j % 4, :], att[:, j % 2, :], m.split, ah[:, j % 4, :], m.lo_done)

                def chunk(c, i, g, more):
                    for j in range(2, m.nt):
                        if j == 4 and at_chunk:
                            at_chunk(c, i, g)
                        split(c, j)
                    if more or i == 0:
                        split(c + 1, 0)
                        split(c + 1, 1)
                    dve.wait_ge(m.second_done, at(c * m.nt + m.nt - 1))
                    dve.wait_ge(m.stored[i], 16 * g + 16)
                    evac(m, c, i)
                split(0, 0)
                split(0, 1)
                by(dve, m.nch, 2, chunk)

            def two(ap):
                return spread(ap[:, :].rearrange("p (o d) -> p o d", o=1), 1, 2)

            def half(h, i):
                return a_bank[2 * i + h][:, :].rearrange("p (o d) -> p o d", o=2)

            def evac_attention(m, c, i):
                for h in range(2):
                    ins = dve.scalar_tensor_tensor(out=xin[:, i, 2 * h:2 * h + 2, :], in0=half(h, i),
                                                   scalar=1.0 / (ATT_S * V_S), in1=two(bo_b), op0=ALU.mult,
                                                   op1=ALU.add)
                ins.then_inc(m.evac_read, 1)
                dve.wait_ge(m.evac_read, at(c))
                for h in range(2):
                    ins = dve.tensor_tensor(xin[:, i, 2 * h:2 * h + 2, :], xin[:, i, 2 * h:2 * h + 2, :], two(ls_b),
                                            ALU.mult)
                ins.then_inc(m.evac_done, 1)

            before = end_mo
            for b in range(B):
                pj = proj[b]
                gate(dve, before)

                def rows_norm(t, i):
                    dve.wait_ge(pj["mm"], at(t))
                    dve.wait_ge(pj["qkn"], at(t - 2))
                    moments(lambda m: s_bank[i % 4][:, m * D:(m + 1) * D], 2, i % 2, t, pj, EPS * QK_PS * QK_PS)
                    dve.wait_ge(pj["vhi"], at(t))
                    rows_t = bass.ds(t, 1)
                    low(vp[1][:, rows_t, :].rearrange("p o e -> p (o e)"), a_bank[2 + i % 2][:, 0:D], V_S / VP_PS,
                        vp[0][:, rows_t, :].rearrange("p o e -> p (o e)"), pj["vlo"])
                    dve.wait_ge(pj["rs"], at(t))
                    dve.scalar_tensor_tensor(out=nmr[:, i % 2, 0:2], in0=mv[:, i % 2, 0:2, 0], scalar=-1.0,
                                             in1=rstd[:, i % 2, 0:2], op0=ALU.mult, op1=ALU.mult
                                             ).then_inc(pj["nmr"], 1)

                def rows_lo(t, i, g, more):
                    if more or i < 3:
                        rows_norm(t + 1, i + 1)
                    dve.wait_ge(pj["thi"], at(t))
                    cols = bass.ds(t * P, P)
                    low(qkT[1][:, :, cols], a_bank[i % 2][:, :].rearrange("p (k c) -> p k c", k=2 * KC), X_S,
                        qkT[0][:, :, cols], pj["tlo"])
                rows_norm(0, 0)
                by(dve, S // P, 4, rows_lo)
                gate(dve, end_pj[b])
                mix(at_mix[b], evac_attention)
                before = end_mix(at_mix[b])

            gate(dve, before)
            dve.wait_ge(vb_hi, 1)
            low(vb[1], st_vb, K_S, vb[0], vb_lo)

            def front(c, i, g):
                dve.wait_ge(q4["sig"], at(c))
                dve.wait_ge(q4_ld[i], 48 * g + 48)
                dve.tensor_tensor(gin[i], gin[i], sgb[i], ALU.mult).then_inc(q4["m1"], 1)
                dve.wait_ge(q4["m1"], at(c))
                dve.tensor_tensor(gin[i], gin[i], sin[i], ALU.mult).then_inc(q4["m2"], 1)
                dve.wait_ge(q4["m2"], at(c))
                dve.tensor_tensor(xin[:, i, :, :], xin[:, i, :, :], gin[i], ALU.add).then_inc(q4["x1"], 1)
                dve.wait_ge(q4["x1"], at(c))
                moments(lambda m: xin[:, i, m, :], G4, i, c, q4, EPS)
                dve.wait_ge(q4["t1"], at(2 * (c - 2) + 1))
                dve.wait_ge(q4["qs"], at(c - 2))
                norm(xin, i, c, q4)
                for b in range(2):
                    low_of(c, i, b, s_bank[0:2], xT, X_S, q4["h1"], q4["l1"])

            def second_block(c, i, g, more):
                if more or i == 0:
                    front(c + 1, 1 - i, g + i)
                dve.wait_ge(q4["gm"], at(c))
                dve.wait_ge(q4["rn"], at(c - 2))
                for m in range(G4):
                    ins = dve.tensor_tensor_reduce(out=junk[:, m, :], in0=a_bank[m][:, 0:D], in1=xn[:, i, m, :],
                                                   scale=1.0 / (X_S * GRAM_S * NB), scalar=0.0, op0=ALU.mult,
                                                   op1=ALU.add, accum_out=nn2[:, i, m:m + 1])
                ins.then_inc(q4["nn"], 1)
                for b in range(2):
                    low_of(c, i, b, s_bank[2:4], qsT, QS_S, q4["h2"], q4["l2"])
            front(0, 0, 0)
            by(dve, NCH, 2, second_block)

            def evac_ffn(m, c, i):
                for h in range(2):
                    ins = dve.scalar_tensor_tensor(out=fbuf[i][:, 2 * h:2 * h + 2, :], in0=half(h, i),
                                                   scalar=1.0 / GE_S, in1=two(b2_b), op0=ALU.mult, op1=ALU.add)
                ins.then_inc(m.evac_read, 1)
                dve.wait_ge(m.evac_read, at(c))
                dve.sem_inc(m.evac_done, 1)
            gate(dve, end_q4)
            mix(ff_mix, evac_ffn)
            gate(dve, end_mix(ff_mix))

            def silu2(c, i, g):
                dve.wait_ge(bk_tanh, at(c))
                dve.wait_ge(bk_ld[i], 32 * g + 32)
                dve.scalar_tensor_tensor(out=gl[i], in0=tbuf[i], scalar=1.0, in1=gl[i], op0=ALU.add, op1=ALU.mult
                                         ).then_inc(bk_silu, 1)

            def evac_bank(m, c, i):
                dve.wait_ge(bk_silu, at(c))
                for h in range(2):
                    ins = dve.scalar_tensor_tensor(out=gl[i][:, 2 * h:2 * h + 2, :], in0=half(h, i),
                                                   scalar=0.5 / (GE_S * K_S), in1=gl[i][:, 2 * h:2 * h + 2, :],
                                                   op0=ALU.mult, op1=ALU.mult)
                ins.then_inc(m.evac_read, 1)
                dve.wait_ge(m.evac_read, at(c))
                dve.tensor_tensor(fbuf[i], gl[i], xl[i], ALU.add).then_inc(m.evac_done, 1)
            mix(bk_mix, evac_bank, silu2)


_INS = ["L0_attn_x", "L0_attn_Wq", "L0_attn_bq", "L0_attn_Wk", "L0_attn_bk", "L0_attn_Wv", "L0_attn_bv",
        "L0_attn_Wo", "L0_attn_bo", "L0_attn_layerscale", "L0_ffn_router_weight", "L0_ffn_e_bias",
        "L0_ffn_gate_w", "L0_ffn_up_w", "L0_ffn_down_w", "L0_ffn_sh_gate_w", "L0_ffn_sh_up_w",
        "L0_ffn_sh_down_w", "L1_attn_k", "L1_attn_v", "L1_ffn_W1", "L1_ffn_b1", "L1_ffn_W2", "L1_ffn_b2"]


def kernel(**inputs):
    import numpy as _np
    import concourse.bacc as _bacc
    from concourse import mybir as _mybir
    from concourse.bass_utils import run_bass_kernel_spmd as _run

    nc = _bacc.Bacc("TRN2", target_bir_lowering=False, num_devices=1)
    arrays, args = {}, {}
    for name in _INS:
        v = _np.ascontiguousarray(inputs[name])
        arrays[f"in_{name}_dram"] = v
        args[name] = nc.dram_tensor(f"in_{name}_dram", v.shape, _mybir.dt.from_np(v.dtype), kind="ExternalInput").ap()
    result = nc.dram_tensor("out_0_dram", (B, S, D), F32, kind="ExternalOutput").ap()
    build(nc, args, result)
    r = _run(nc, [arrays], core_ids=[0])
    return r.results[0]["out_0_dram"]
```

```python
from contextlib import ExitStack
import math

import concourse.bass as bass
from concourse import mybir

P = 128
D = 256
KC = D // P
B, S = 2, 2048
T = B * S
TT = T // P
G4 = 4
NCH = TT // G4
CW = G4 * P
E = 16
TOPK, GROUPS, GTOP = 4, 4, 2
ROUTE_SCALE = 2.5
EPG = E // GROUPS
NE = E + 2
IM = 128
NSLOT_T = TOPK * T // P + E
NSLOT = NSLOT_T * P
ROUND = 12582912.0
NB = 2048
FF = 1024
EPS = 1e-5

F32 = mybir.dt.float32
F16 = mybir.dt.float16
I32 = mybir.dt.int32
ALU = mybir.AluOpType
ACT = mybir.ActivationFunctionType
AXX = mybir.AxisListType.X

X_S = 64.0
WQK_S = 16.0
WO_S = 64.0
WP_S = 4.0
V_S = 0.25
ATT_S = 2.0 ** 14
H_S = 0.25
K_S = 1024.0
GRAM_S = 64.0
QS_S = 16.0
GE_S = 64.0
QK_PS = X_S * WQK_S
VP_PS = X_S * WP_S


def build(nc, a, out):
    with ExitStack() as ctx:
        def sb(name, shape, dt=F32):
            return ctx.enter_context(nc.sbuf_tensor(name, shape, dt))

        def sem(name):
            return ctx.enter_context(nc.semaphore(name))

        def dram(name, shape, dt=F32):
            return nc.dram_tensor(name, shape, dt, kind="Internal").ap()

        s0_d = dram("s0_d", [T, D])
        xn_d = dram("xn_d", [T, D])
        xg_d = dram("xg_d", [NSLOT, D])
        yg_d = dram("yg_d", [NSLOT, D])
        sh_d = dram("sh_d", [T, D])
        moe_d = dram("moe_d", [T, D])
        x1_d = dram("x1_d", [T, D])
        f_d = dram("f_d", [T, D])
        sums_d = dram("sums_d", [P, 2])

        def chunks(ap):
            return ap.rearrange("(n m p) d -> n p m d", m=G4, p=P)

        x_rows = a["L0_attn_x"].rearrange("b s d -> (b s) d")
        x_c, s0_c, xn_c, moe_c, x1_c, f_c = (chunks(v) for v in (x_rows, s0_d, xn_d, moe_d, x1_d, f_d))
        out_c = chunks(out.rearrange("b s d -> (b s) d"))
        xn_t, sh_t, moe_t = (v.rearrange("(n p) d -> n p d", p=P) for v in (xn_d, sh_d, moe_d))
        xg_p, yg_p = (v.rearrange("(n m p) d -> n p m d", m=2, p=P) for v in (xg_d, yg_d))

        reg_x = sb("reg_x", [P, 8192])
        reg_qk = sb("reg_qk", [P, 8192])
        reg_v = sb("reg_v", [P, 4096])
        reg_e = sb("reg_e", [P, NE * 512 + NE * D])
        reg_w = sb("reg_w", [P, 3072])

        def f16(r, lo, n):
            return r[:, lo:lo + n].bitcast(F16)

        xT = [f16(reg_x, h * 4096, 4096).rearrange("p (k t) -> p k t", k=KC) for h in range(2)]
        qkT = [f16(reg_qk, h * 4096, 4096).rearrange("p (k t) -> p k t", k=2 * KC) for h in range(2)]
        qsT = [f16(reg_qk, h * 4096, 4096).rearrange("p (k t) -> p k t", k=KC) for h in range(2)]
        vp = [f16(reg_v, h * 2048, 2048).rearrange("p (t e) -> p t e", e=D) for h in range(2)]
        vb = vp
        gu = [f16(reg_e, h * NE * 256, NE * 256).rearrange("p (e k c) -> p e k c", k=KC, c=D) for h in range(2)]
        dn = [f16(reg_e, NE * 512 + h * NE * 128, NE * 128).rearrange("p (e h) -> p e h", h=D) for h in range(2)]

        wqkT = [sb(f"wqkT{h}", [P, KC, 2 * D], F16) for h in range(2)]
        woT = [sb(f"woT{h}", [P, KC, D], F16) for h in range(2)]
        wv = [sb(f"wv{h}", [P, KC, D], F16) for h in range(2)]
        wpT = [sb(f"wpT{h}", [P, KC, D], F16) for h in range(2)]
        kbT = [sb(f"kbT{h}", [P, KC, NB], F16) for h in range(2)]
        gram = [sb(f"gram{h}", [P, KC, D], F16) for h in range(2)]
        w1T = sb("w1T", [P, KC, FF], F16)
        w2T = sb("w2T", [P, FF // P, D], F16)
        rwT = [sb(f"rwT{h}", [P, KC, E], F16) for h in range(2)]
        bvf = sb("bvf", [P, KC])
        bvc = [sb(f"bvc{h}", [P, KC, 33], F16) for h in range(2)]
        bias3 = sb("bias3", [33, 3 * D])
        biasz = sb("biasz", [33, 3 * D], F16)
        ones33 = sb("ones33", [33, P], F16)
        onesf = sb("onesf", [P, P])
        ident = sb("ident", [P, P])
        b1c = sb("b1c", [P, FF // P])
        bo_b = sb("bo_b", [P, D])
        ls_b = sb("ls_b", [P, D])
        b2_b = sb("b2_b", [P, D])
        eb_b = sb("eb_b", [P, E])
        nlogs = sb("nlogs", [P, 1])
        mhalf = sb("mhalf", [P, G4])
        thr = sb("thr", [P, 8])
        slot_i = sb("slot_i", [P, TOPK, TT], I32)
        w4 = sb("w4", [P, TOPK, TT])
        expert_of = sb("expert_of", [1, NSLOT_T], I32)
        before_h = sb("before_h", [P, P], F16)
        ones_h = sb("ones_h", [P, P], F16)
        sel_h = sb("sel_h", [P, TT * E], F16)
        tile_no = sb("tile_no", [1, NSLOT_T], I32)
        xr = sb("xr", [P, 4, D])
        icol = sb("icol", [P, 4, TOPK], I32)

        xin = sb("xin", [P, 2, G4, D])
        stat = sb("stat", [P, 2, G4, 6])
        mv = sb("mv", [P, 2, G4, 2])
        ve = sb("ve", [P, 2, G4])
        rstd = sb("rstd", [P, 2, G4])
        nmr = sb("nmr", [P, 2, G4])
        nn2 = sb("nn2", [P, 2, G4])
        rn2 = sb("rn2", [P, 2, G4])
        att = reg_w[:, 0:1024].rearrange("p (r c) -> p r c", c=CW)
        ah = f16(reg_w, 1024, 1024).rearrange("p (r c) -> p r c", c=CW)
        al = f16(reg_w, 2048, 1024).rearrange("p (r c) -> p r c", c=CW)
        xn = reg_w[:, 0:2048].rearrange("p (b m d) -> p b m d", b=2, d=D)
        sg, t1, hh = (reg_w[:, 512 * i:512 * (i + 1)].rearrange("p (r c) -> p r c", c=D) for i in range(3))
        hT = [f16(reg_w, 1536 + 256 * h, 256).rearrange("p (r c) -> p r c", c=D) for h in range(2)]
        xgT = [f16(reg_w, 2048 + 512 * h, 512).rearrange("p (r k c) -> p r k c", r=2, k=KC) for h in range(2)]
        xs = xin[:, :, :, :].rearrange("p a (b m) d -> p (a b) m d", m=2)
        yres = reg_qk[:, 0:1024].rearrange("p (r m d) -> p r m d", r=2, d=D)
        yg = reg_e[:, 0:2560].rearrange("p (r k d) -> p r k d", r=2, d=D)
        cres = reg_e[:, 2560:3072].rearrange("p (r d) -> p r d", d=D)
        qkn = reg_w[:, 0:1024].rearrange("p (r c) -> p r c", c=2 * D)
        buf_e = [reg_e[:, i * 1024:(i + 1) * 1024].rearrange("p (m d) -> p m d", d=D) for i in range(8)]
        sin, gin, sgb, qsb = buf_e[0:2], buf_e[2:4], buf_e[4:6], buf_e[6:8]
        fbuf, tbuf, gl, xl = buf_e[0:2], buf_e[2:4], buf_e[4:6], buf_e[6:8]
        junk = reg_e[:, 8192:8192 + G4 * D].rearrange("p (m d) -> p m d", d=D)
        st_vb = reg_e[:, 9216:9216 + 4096].rearrange("p (n d) -> p n d", d=D)

        scores, biased, masked, erank = (reg_w[:, 512 * i:512 * (i + 1)] for i in range(4))
        pair_s = reg_w[:, 2048:2816].rearrange("p (n q) -> p n q", q=6)
        xin_f = xin[:, :, :, :].rearrange("p a b c -> p (a b c)")
        gs, grank, gsel = (xin_f[:, 128 * i:128 * (i + 1)] for i in range(3))
        esum = xin_f[:, 384:448]
        gbeat = xin_f[:, 512:1024].rearrange("p (t x) -> p t x", x=GROUPS * GROUPS)
        ebeat = reg_qk[:, :].rearrange("p (t x) -> p t x", x=E * E)
        cnt = [reg_qk[:, 512 * i:512 * (i + 1)].rearrange("p (t e) -> p t e", e=E) for i in range(3)]
        picks = [reg_qk[:, 2048 + 2048 * i:4096 + 2048 * i].rearrange("p (k t e) -> p k t e", k=TOPK, e=E)
                 for i in range(2)]
        slot_f = reg_qk[:, 6144:6272]
        small = [reg_qk[:, 6272 + 16 * i:6288 + 16 * i] for i in range(8)]
        upto = reg_qk[0:1, 2048:2048 + NSLOT_T * E].rearrange("p (j e) -> p j e", e=E)
        tile_f = reg_qk[0:1, 6400:6400 + NSLOT_T]
        exp_f = reg_qk[0:1, 6560:6560 + NSLOT_T]

        bank = [ctx.enter_context(nc.psum_tensor(f"bank{i}", [P, 512], F32)) for i in range(8)]
        s_bank, a_bank = bank[:4], bank[4:]
        h_bank = bank[6:]

        st_gate = reg_qk[:, 0:4096].rearrange("p (e d) -> p e d", d=D)
        st_up = reg_qk[:, 4096:8192].rearrange("p (e d) -> p e d", d=D)
        st_down = reg_v[:, :].rearrange("p (t e i) -> p t e i", t=KC, e=E)
        st_sg = reg_x[:, 0:512].rearrange("p (t d) -> p t d", d=D)
        st_su = reg_x[:, 512:1024].rearrange("p (t d) -> p t d", d=D)
        st_sd = reg_x[:, 1024:1536].rearrange("p (t i) -> p t i", i=D)
        st_wq, st_wk, st_wv, st_wo = (reg_x[:, 1536 + 512 * i:2048 + 512 * i].rearrange("p (t d) -> p t d", d=D)
                                      for i in range(4))
        st_rw = reg_x[0:E, 3584:3840]
        st_k = reg_v[:, :].rearrange("p (n d) -> p n d", d=D)
        KN = NB // P // 2
        kn = [[f16(reg_x, h * 4096 + k * 2048, 1024).rearrange("p (n d) -> p n d", d=D) for k in range(KC)]
              for h in range(2)]
        st_w = [reg_qk[:, 1024:3072], reg_qk[:, 3072:5120]]
        below = reg_qk[:, 5120:7168]
        w_sums = reg_qk[:, 7168:7168 + 2 * P].rearrange("p (q n) -> p q n", n=2)

        def rows(ap):
            return ap.rearrange("(t p) d -> p t d", p=P)

        def row1(ap):
            return ap.rearrange("(o d) -> o d", o=1)

        def spread(ap, axis, n):
            shape = list(ap.shape)
            shape[axis] = n
            return ap.broadcast_to(shape)

        def one(ap, n):
            return ap[bass.ds(n, 1)].rearrange("o p m d -> p (o m) d")

        def first_step(c):
            return isinstance(c, int) and c == 0

        def by(eng, n, m, body, head=0):
            for c in range(head):
                body(c, c % m, c // m, True)
            if n - head > m:
                with eng.Fori(head // m, n // m - 1) as g:
                    for i in range(m):
                        body(m * g + i, i, g, True)
            for i in range(m):
                body(n - m + i, i, n // m - 1, False)

        CR = 4

        def at(k):
            return k + 1 + CR

        def open_(eng, *sems):
            for q in sems:
                eng.sem_inc(q, CR)

        def gate(eng, waits):
            for q, count in waits:
                eng.wait_ge(q, count)

        ld = {n: sem("ld_" + n) for n in ("qk", "o_v", "gate_up", "down", "sh", "bank", "w12", "small", "vb")}
        ident_zero = sem("ident_zero")
        ready_id = sem("ready_id")
        consts = sem("consts")
        w_turned = sem("w_turned")
        w_hi = sem("w_hi")
        w_lo = sem("w_lo")
        nat_hi = sem("nat_hi")
        nat_lo = sem("nat_lo")
        ex = {n: sem("ex_" + n) for n in ("turned", "hi", "lo")}
        kn_step = sem("kn_step")
        wp_mm, wp_hi, wp_lo = sem("wp_mm"), sem("wp_hi"), sem("wp_lo")
        bias_step = sem("bias_step")
        gram_mm, gram_hi, gram_lo = sem("gram_mm"), sem("gram_hi"), sem("gram_lo")
        tn_step, tn_sum, tn_dma, tn_made = sem("tn_step"), sem("tn_sum"), sem("tn_dma"), sem("tn_made")
        rw_mm, rw_hi, rw_lo = sem("rw_mm"), sem("rw_hi"), sem("rw_lo")

        jobs = []

        def job(need, blocks, hi, lo, scale):
            jobs.append((need, blocks, hi, lo, scale))

        def blk(x3, t, k):
            return x3[:, t, k * P:(k + 1) * P]

        for n, w in enumerate((st_wq, st_wk)):
            job(("qk",), [blk(w, r, k) for k in range(KC) for r in range(KC)],
                wqkT[0][:, :, n * D:(n + 1) * D], wqkT[1][:, :, n * D:(n + 1) * D], WQK_S)
        job(("o_v",), [blk(st_wo, r, k) for k in range(KC) for r in range(KC)],
            woT[0][:, :, :], woT[1][:, :, :], WO_S)
        WO_JOBS = len(jobs)
        for e in range(2):
            job(("sh",), [blk(w, e, k) for k in range(KC) for w in (st_sg, st_su)],
                gu[0][:, E + e, :, :], gu[1][:, E + e, :, :], WQK_S)
        job(("sh",), [st_sd[:, t, x * P:(x + 1) * P] for x in range(2) for t in range(KC)],
            dn[0][:, E:NE, :], dn[1][:, E:NE, :], WQK_S)

        def ex_job(c, n):
            def e1(ap, e):
                return ap[:, bass.ds(e, 1)]
            if n < 2:
                return ([e1(w, 2 * c + n)[:, 0, k * P:(k + 1) * P] for k in range(KC) for w in (st_gate, st_up)],
                        [gu[h][:, bass.ds(2 * c + n, 1), :, :].rearrange("p o k c -> p (o k) c") for h in range(2)])
            return ([st_down[:, t, bass.ds(2 * c + x, 1), :].rearrange("p o i -> p (o i)")
                     for x in range(2) for t in range(KC)],
                    [dn[h][:, bass.ds(2 * c, 2), :] for h in range(2)])

        late_jobs = []
        for n in range(0, NB // P, 2):
            late_jobs.append(([blk(st_k, n + r, k) for k in range(KC) for r in range(2)],
                              kbT[0][:, :, n * P:(n + 2) * P], kbT[1][:, :, n * P:(n + 2) * P], 1.0))
        LATE_LO = len(late_jobs)
        tern1 = st_w[0].rearrange("p (n d) -> p n d", d=D)
        tern2 = st_w[1].rearrange("p (t f) -> p t f", f=FF)
        for n in range(0, FF // P, 2):
            late_jobs.append(([blk(tern1, n + r, k) for k in range(KC) for r in range(2)],
                              w1T[:, :, n * P:(n + 2) * P], None, 1.0))
        for n in range(0, FF // P, 2):
            late_jobs.append(([tern2[:, t, (n + r) * P:(n + r + 1) * P] for r in range(2) for t in range(KC)],
                              w2T[:, n:n + 2, :], None, 1.0))

        def job_ps(j):
            return bank[j % 8][:, :].rearrange("p (k c) -> p k c", k=2)

        bvt = sb("bvt", [P, KC, 33])
        bv_step = sem("bv_step")
        x_ld = [sem(f"x_ld{i}") for i in range(2)]
        ln = {n: sem("ln_" + n) for n in ("mv", "ve", "rs", "xn", "mm", "hi", "lo")}
        rt_mm, rt_sig, rt_step, rt_done = sem("rt_mm"), sem("rt_sig"), sem("rt_step"), sem("rt_done")
        pj = {n: sem(f"pj_{n}") for n in ("mm", "mv", "ve", "rs", "nmr", "qkn", "vhi", "vlo", "tr", "thi", "tlo")}
        steps = ("xt", "xh", "xl", "gu", "sig", "t1", "h", "tr", "hi", "lo", "dn", "ev")
        shx = {n: sem("shx_" + n) for n in steps[3:]}
        rex = {n: sem("rex_" + n) for n in steps}
        shx_st = [sem(f"shx_st{i}") for i in range(2)]
        rex_st = [sem(f"rex_st{i}") for i in range(2)]
        rex_ld = [sem(f"rex_ld{i}") for i in range(4)]
        xn_st = [sem(f"xn_st{i}") for i in range(2)]
        zero_st = sem("zero_st")
        xr_ld = [sem(f"xr_ld{i}") for i in range(4)]
        xr_st = [sem(f"xr_st{i}") for i in range(4)]
        sh_ld = [sem(f"sh_ld{i}") for i in range(2)]
        y_ld = [sem(f"y_ld{i}") for i in range(2)]
        cb_step, cb_done = sem("cb_step"), sem("cb_done")
        cb_st = [sem(f"cb_st{i}") for i in range(2)]
        pool_col, pool_turn = sem("pool_col"), sem("pool_turn")
        rt_sel, rt_cnt = sem("rt_sel"), sem("rt_cnt")
        q4 = {n: sem("q4_" + n) for n in ("sig", "m1", "m2", "x1", "mv", "ve", "rs", "xn", "t1", "h1", "l1",
                                         "gm", "nn", "rn", "qs", "t2", "h2", "l2")}
        g_ld = [sem(f"g_ld{i}") for i in range(2)]
        q4_ld = [sem(f"q4_ld{i}") for i in range(2)]
        q4_st = [sem(f"q4_st{i}") for i in range(2)]
        vb_hi, vb_lo = sem("vb_hi"), sem("vb_lo")
        bk_ld = [sem(f"bk_ld{i}") for i in range(2)]

        mixes = []
        mx_first, mx_act, mx_hi, mx_lo, mx_second, mx_read, mx_evac = (
            sem("mx_" + n) for n in ("first", "act", "hi", "lo", "second", "read", "evac"))
        mx_st = [[sem(f"mx_st{n}{i}") for i in range(2)] for n in ("a", "f")]

        class Mix:
            def __init__(self, nch, nt, stat, mov, pass1, second, pass2, func, scale, bias, split):
                self.nch, self.nt = nch, nt
                self.stat, self.mov, self.pass1 = stat, mov, pass1
                self.second, self.pass2 = second, pass2
                self.func, self.scale, self.bias, self.split = func, scale, bias, split
                self.k0 = sum(m.nch * m.nt for m in mixes)
                self.c0 = sum(m.nch for m in mixes)
                self.first_done = mx_first
                self.act_done = mx_act
                self.hi_done = mx_hi
                self.lo_done = mx_lo
                self.second_done = mx_second
                self.evac_read = mx_read
                self.evac_done = mx_evac
                self.stored = mx_st[0 if func == ACT.Sigmoid else 1]
                self.s0 = sum(m.nch // 2 for m in mixes if m.stored is self.stored)
                mixes.append(self)

            def step(self, c, j):
                return self.k0 + c * self.nt + j

            def ch(self, c):
                return self.c0 + c

            def st(self, g):
                return 16 * (self.s0 + g) + 16

        THREE = ((0, 0), (1, 0), (0, 1))
        at_mix = [Mix(S // CW, S // P,
                      lambda part, k, j: qkT[part][:, KC + k, j * P:(j + 1) * P],
                      lambda part, k, c: qkT[part][:, k, bass.ds(c * CW, CW)],
                      THREE, lambda part, j: vp[part][:, j, :], THREE,
                      ACT.Sigmoid, 1.0 / (X_S * X_S * math.sqrt(D)), lambda j: nlogs[:, 0:1], ATT_S)
                  for b in range(B)]
        ff_mix = Mix(NCH, FF // P,
                     lambda part, k, j: w1T[:, k, j * P:(j + 1) * P],
                     lambda part, k, c: xT[part][:, k, bass.ds(c * CW, CW)],
                     ((0, 0), (0, 1)), lambda part, j: w2T[:, j, :], ((0, 0), (1, 0)),
                     ACT.Gelu, 1.0 / X_S, lambda j: b1c[:, j:j + 1], GE_S)
        bk_mix = Mix(NCH, NB // P,
                     lambda part, k, j: kbT[part][:, k, j * P:(j + 1) * P],
                     lambda part, k, c: qsT[part][:, k, bass.ds(c * CW, CW)],
                     THREE, lambda part, j: vb[part][:, j, :], THREE,
                     ACT.Gelu, 1.0 / (QS_S * K_S), None, GE_S)
        bk_tanh, bk_silu = sem("bk_tanh"), sem("bk_silu")

        block = ctx.enter_context(nc.Block())

        end_w = [(w_hi, len(jobs)), (w_lo, len(jobs)), (wp_lo, 1), (rw_lo, 1), (bias_step, 4)]
        end_x = [(ln["lo"], at(2 * NCH - 1))] + [(q, 16 * (NCH // 2) + 16) for q in xn_st] + \
            [(ex["lo"], at(3 * NCH - 1)), (ex["hi"], at(3 * NCH - 1))]
        end_rt = [(rt_done, 1)]
        end_pj = [[(pj[n], at((b + 1) * (S // P) - 1)) for n in ("tlo", "vlo")] for b in range(B)]
        end_sc = [(q, 16 * TT) for q in xr_st]
        end_sh = [(shx["ev"], at(TT - 1))] + [(q, 16 * (TT // 2) + 16) for q in shx_st]
        end_mo = [(rex["ev"], at(NSLOT_T // 2 - 1))] + [(q, 16 * (NSLOT_T // 4) + 16) for q in rex_st]
        end_late = [(w_hi, len(jobs) + len(late_jobs)), (w_lo, len(jobs) + LATE_LO), (kn_step, 3 * KC)]
        end_q4 = [(q4["l2"], at(2 * NCH - 1)), (vb_lo, 1)]

        def end_mix(m):
            return [(m.evac_done, at(m.ch(m.nch - 1)))] + [(q, m.st(m.nch // 2)) for q in m.stored]

        @block.sync
        def _(sp):
            def load(dst, src, name, **how):
                sp.dma_start(dst, src, **how).then_inc(ld[name], 16)

            for q in shx_st + rex_st + xn_st + cb_st + [q for m in mx_st for q in m]:
                sp.sem_inc(q, 16)
            load(st_wq, rows(a["L0_attn_Wq"]), "qk")
            load(st_wk, rows(a["L0_attn_Wk"]), "qk")
            load(st_wo, rows(a["L0_attn_Wo"]), "o_v")
            load(st_wv, rows(a["L0_attn_Wv"]), "o_v")
            load(st_sg, rows(a["L0_ffn_sh_gate_w"]), "sh")
            load(st_su, rows(a["L0_ffn_sh_up_w"]), "sh")
            load(st_sd, rows(a["L0_ffn_sh_down_w"]), "sh")
            load(st_rw, a["L0_ffn_router_weight"], "sh")
            for i in range(2):
                sp.dma_start(xin[:, i, :, :], x_c[i]).then_inc(x_ld[i], 16)
            sp.wait_ge(consts, 1)
            for n, name in enumerate(("L0_attn_bq", "L0_attn_bk")):
                for r in (0, 32):
                    load(bias3[r:r + 1, n * D:(n + 1) * D], row1(a[name]), "small")
            for dst, name in ((bo_b, "L0_attn_bo"), (ls_b, "L0_attn_layerscale"), (b2_b, "L1_ffn_b2"),
                              (eb_b, "L0_ffn_e_bias")):
                load(dst[:, :], spread(row1(a[name]), 0, P), "small")
            load(bvf[:, :], a["L0_attn_bv"].rearrange("(t p) -> p t", p=P), "small", allow_slow_non_contiguous=True)
            load(b1c[:, :], a["L1_ffn_b1"].rearrange("(t p) -> p t", p=P), "small", allow_slow_non_contiguous=True)
            load(st_gate, a["L0_ffn_gate_w"].rearrange("e i d -> i e d"), "gate_up")
            load(st_up, a["L0_ffn_up_w"].rearrange("e i d -> i e d"), "gate_up")
            for t in range(KC):
                load(st_down[:, t, :, :], a["L0_ffn_down_w"][:, t * P:(t + 1) * P, :].rearrange("e h i -> h e i"),
                     "down")

            def next_x(c, i, g, more):
                sp.wait_ge(ln["xn"], at(c))
                sp.dma_start(one(xn_c, c), xn[:, i, :, :]).then_inc(xn_st[i], 16)
                if more:
                    sp.dma_start(xin[:, i, :, :], one(x_c, c + 2)).then_inc(x_ld[i], 16)
            by(sp, NCH, 2, next_x)

            for n in range(0, NSLOT_T, 16):
                sp.dma_start(xg_d[n * P:(n + 16) * P, :].rearrange("(n p) d -> p n d", p=P),
                             spread(xr[:, 0, :].rearrange("p (o d) -> p o d", o=1), 1, 16)).then_inc(zero_st, 16)
            for i in range(2):
                sp.wait_ge(xn_st[i], 16 * (NCH // 2) + 16)
            sp.wait_ge(zero_st, 16 * (NSLOT_T // 16))

            def load_xr(c, i, g, more):
                if not first_step(g):
                    sp.wait_ge(xr_st[i], 16 * TOPK * g)
                sp.dma_start(xr[:, i, :], xn_t[bass.ds(c, 1)].rearrange("o p d -> p (o d)")).then_inc(xr_ld[i], 16)
            by(sp, TT, 4, load_xr, head=4)

            gate(sp, end_mix(at_mix[0]))
            load(st_w[0].rearrange("p (n d) -> p n d", d=D), rows(a["L1_ffn_W1"]), "w12")
            load(st_w[1].rearrange("p (t f) -> p t f", f=FF), rows(a["L1_ffn_W2"]), "w12")

            def store_shared(c, i, g, more):
                sp.wait_ge(shx["ev"], at(c))
                sp.dma_start(sh_t[bass.ds(c, 1)].rearrange("o p d -> p (o d)"), yres[:, i, 0, :]
                             ).then_inc(shx_st[i], 16)
            by(sp, TT, 2, store_shared)

            gate(sp, end_sc)
            gate(sp, end_sh)

            def load_slots(c, r):
                sp.dma_start(xs[:, r, :, :], one(xg_p, c)).then_inc(rex_ld[r], 16)

            def next_slots(c, r):
                sp.wait_ge(rex["xt"], at(c - 4))
                load_slots(c, r)
            for c in range(4):
                load_slots(c, c)
            load(st_k, rows(a["L1_attn_k"]), "bank")
            for c in range(4, 7):
                next_slots(c, c - 4)

            def slots(c, i, g, more):
                if more or i == 0:
                    next_slots(c + 7, (i + 3) % 4)
                sp.wait_ge(rex["ev"], at(c))
                sp.dma_start(one(yg_p, c), yres[:, i % 2, :, :]).then_inc(rex_st[i % 2], 16)
            by(sp, NSLOT_T // 2, 8, slots)
            gate(sp, end_mo)

            sp.dma_start(st_vb, rows(a["L1_attn_v"])).then_inc(ld["vb"], 16)

            def load_shared(c, i):
                sp.dma_start(yg[:, i, TOPK, :], sh_t[bass.ds(c, 1)].rearrange("o p d -> p (o d)")
                             ).then_inc(sh_ld[i], 16)
            load_shared(0, 0)
            load_shared(1, 1)

            def combined(c, i, g, more):
                sp.wait_ge(cb_done, at(c))
                sp.dma_start(moe_t[bass.ds(c, 1)].rearrange("o p d -> p (o d)"), cres[:, i, :]
                             ).then_inc(cb_st[i], 16)
                if more:
                    load_shared(c + 2, i)
            by(sp, TT, 2, combined)
            for i in range(2):
                sp.wait_ge(cb_st[i], 16 * (TT // 2) + 16)
            gate(sp, end_mix(at_mix[1]))

            def store_mix(m, dst_c, base, res):
                def store(c, i, g, more):
                    sp.wait_ge(m.evac_done, at(m.ch(c)))
                    sp.dma_start(one(dst_c, base + c), res(i)).then_inc(m.stored[i], 16)
                return store

            def load_parts(n, i):
                sp.dma_start(gin[i], one(moe_c, n)).then_inc(g_ld[i], 16)
                sp.dma_start(sin[i], one(s0_c, n)).then_inc(q4_ld[i], 16)

            def load_x(n, i):
                sp.dma_start(xin[:, i, :, :], one(x_c, n)).then_inc(q4_ld[i], 16)
            for i in range(2):
                load_parts(i, i)
                load_x(i, i)

            def x1_out(c, i, g, more):
                sp.wait_ge(q4["x1"], at(c))
                sp.dma_start(one(x1_c, c), xin[:, i, :, :]).then_inc(q4_st[i], 16)
                if more:
                    load_parts(c + 2, i)
                    sp.wait_ge(q4["xn"], at(c))
                    sp.wait_ge(q4_st[i], 16 * g + 16)
                    load_x(c + 2, i)
            by(sp, NCH, 2, x1_out)
            for i in range(2):
                sp.wait_ge(q4_st[i], 16 * (NCH // 2))

            by(sp, NCH, 2, store_mix(ff_mix, f_c, 0, lambda i: fbuf[i]))
            gate(sp, end_mix(ff_mix))

            def load2(n, i):
                sp.dma_start(gl[i], one(f_c, n)).then_inc(bk_ld[i], 16)
                sp.dma_start(xl[i], one(x1_c, n)).then_inc(bk_ld[i], 16)
            load2(0, 0)
            load2(1, 1)
            final = store_mix(bk_mix, out_c, 0, lambda i: fbuf[i])

            def out_rows(c, i, g, more):
                final(c, i, g, more)
                if more:
                    load2(c + 2, i)
            by(sp, NCH, 2, out_rows)
            gate(sp, end_mix(bk_mix))

        @block.gpsimd
        def _(pool):
            pool.memset(ident[:, :], 0.0).then_inc(ident_zero, 1)
            pool.wait_ge(ident_zero, 1)
            pool.affine_select(out=ident[:, :], in_=ident[:, :], compare_op=ALU.not_equal, fill=1.0, base=0,
                               pattern=[[-1, P]], channel_multiplier=1).then_inc(ready_id, 1)
            pool.memset(mhalf[:, :], -0.5).then_inc(ready_id, 1)
            pool.memset(before_h[:, :], 1.0).then_inc(ident_zero, 1)
            pool.wait_ge(ident_zero, 2)
            pool.affine_select(out=before_h[:, :], in_=before_h[:, :], compare_op=ALU.is_ge, fill=0.0, base=-1,
                               pattern=[[1, P]], channel_multiplier=-1).then_inc(ready_id, 1)
            pool.memset(ones_h[:, :], 1.0).then_inc(ready_id, 1)
            pool.iota(tile_no[:, :], pattern=[[1, NSLOT_T]], base=0, channel_multiplier=0).then_inc(ready_id, 1)
            pool.wait_ge(ready_id, 5)
            open_(pool, ln["rs"], q4["rs"], q4["rn"], pj["rs"])

            def ln_rows(c, i, g, more):
                pool.wait_ge(ln["ve"], at(c))
                pool.wait_ge(ln["xn"], at(c - 2))
                pool.tensor_tensor(rstd[:, i, :], ve[:, i, :], mhalf[:, :], ALU.pow).then_inc(ln["rs"], 1)
            by(pool, NCH, 2, ln_rows)

            turns = [0]

            def column(src, r, ring):
                pool.tensor_copy(icol[:, r, :], src).then_inc(pool_col, 1)

            def scatter(c, i, g, more):
                if not first_step(g):
                    pool.wait_ge(xr_st[i], 16 * TOPK * g)
                    pool.sem_inc(pool_turn, 1)
                column(slot_i[:, :, bass.ds(c, 1)].rearrange("p k o -> p (k o)"), i, 4)
                pool.wait_ge(xr_ld[i], 16 * g + 16)
                pool.sem_inc(pool_turn, 1)
                pool.wait_ge(pool_col, c + 1)
                pool.sem_inc(pool_turn, 1)
                for k in range(TOPK):
                    pool.indirect_dma_start(out=xg_d, out_offset=bass.IndirectOffsetOnAxis(ap=icol[:, i, k:k + 1], axis=0),
                                            in_=xr[:, i, :], in_offset=None).then_inc(xr_st[i], 16)

            def gather(c, i, g):
                pool.wait_ge(cb_done, at(c - 2))
                pool.sem_inc(pool_turn, 1)
                column(slot_i[:, :, bass.ds(c, 1)].rearrange("p k o -> p (k o)"), i, 2)
                pool.wait_ge(pool_col, TT + c + 1)
                pool.sem_inc(pool_turn, 1)
                for k in range(TOPK):
                    pool.indirect_dma_start(out=yg[:, i, k, :], out_offset=None, in_=yg_d,
                                            in_offset=bass.IndirectOffsetOnAxis(ap=icol[:, i, k:k + 1], axis=0)
                                            ).then_inc(y_ld[i], 16)

            def second_round():
                gate(pool, end_sh)
                pool.wait_ge(tn_sum, 2)
                pool.dma_start(sums_d, thr[:, 0:2]).then_inc(tn_dma, 16)
                pool.wait_ge(tn_dma, 16)
                pool.dma_start(w_sums, spread(sums_d.rearrange("(o q) n -> o q n", o=1), 0, P)
                               ).then_inc(tn_dma, 16)
                pool.wait_ge(ld["bank"], 16)
                for k in range(KC):
                    src = st_k[:, k * KN:(k + 1) * KN, :]
                    pool.tensor_scalar(kn[0][k], src, K_S, None, ALU.mult).then_inc(kn_step, 1)
                    pool.wait_ge(kn_step, 3 * k + 1)
                    pool.tensor_scalar(src, src, K_S, None, ALU.mult).then_inc(kn_step, 1)
                    pool.wait_ge(kn_step, 3 * k + 2)
                    pool.tensor_tensor(kn[1][k], src, kn[0][k], ALU.subtract).then_inc(kn_step, 1)
                pool.wait_ge(tn_step, 1)
                pool.tensor_scalar(thr[:, 0:2], thr[:, 2:4], 1.0 / (FF * D), 1e-8, ALU.mult, ALU.max
                                   ).then_inc(tn_step, 1)
                pool.wait_ge(tn_step, 2)
                pool.tensor_scalar(thr[:, 4:6], thr[:, 0:2], 0.5, None, ALU.mult)
                pool.tensor_scalar(thr[:, 6:8], thr[:, 0:2], -0.5, None, ALU.mult).then_inc(tn_step, 1)
                pool.wait_ge(tn_step, 3)
                for n in range(2):
                    if n:
                        pool.wait_ge(tn_made, 1)
                    pool.tensor_scalar(below, st_w[n], thr[:, 6 + n:7 + n], None, ALU.is_lt).then_inc(tn_step, 1)
                    pool.wait_ge(tn_step, 4 + 2 * n)
                    pool.tensor_scalar(st_w[n], st_w[n], thr[:, 4 + n:5 + n], None, ALU.is_gt).then_inc(tn_step, 1)
                    pool.wait_ge(tn_step, 5 + 2 * n)
                    pool.tensor_tensor(st_w[n], st_w[n], below, ALU.subtract).then_inc(tn_made, 1)

            for b in range(B):
                first_t = b * (S // P)
                if b == 1:
                    second_round()
                    gate(pool, end_mo)
                    gather(0, 0, 0)
                    gather(1, 1, 0)

                def qk_rows(c, i, g, more):
                    pool.wait_ge(pj["ve"], at(first_t + c))
                    pool.wait_ge(pj["qkn"], at(first_t + c - 2))
                    pool.tensor_tensor(rstd[:, i, 0:2], ve[:, i, 0:2], mhalf[:, 0:2], ALU.pow
                                       ).then_inc(pj["rs"], 1)
                by(pool, S // P, 2, qk_rows)
                if b == 0:
                    gate(pool, end_rt)
                    pool.wait_ge(zero_st, 16 * (NSLOT_T // 16))
                    by(pool, TT, 4, scatter, head=4)
                else:
                    def next_gather(c, i, g, more):
                        if more:
                            gather(c + 2, i, None)
                    by(pool, TT, 2, next_gather)

            def second_block(c, i, g, more):
                pool.wait_ge(q4["ve"], at(c))
                pool.wait_ge(q4["xn"], at(c - 2))
                pool.tensor_tensor(rstd[:, i, :], ve[:, i, :], mhalf[:, :], ALU.pow).then_inc(q4["rs"], 1)

            def query_norms(c, i, g, more):
                pool.wait_ge(q4["nn"], at(c))
                pool.wait_ge(q4["qs"], at(c - 2))
                pool.tensor_tensor(rn2[:, i, :], nn2[:, i, :], mhalf[:, :], ALU.pow).then_inc(q4["rn"], 1)

            second_block(0, 0, 0, True)
            second_block(1, 1, 0, True)

            def both(c, i, g, more):
                if more:
                    second_block(c + 2, i, None, None)
                query_norms(c, i, g, more)
            by(pool, NCH, 2, both)

        @block.tensor
        def _(pe):
            pe.wait_ge(ready_id, 5)
            pe.wait_ge(consts, 1)
            open_(pe, ln["mm"], ex["turned"], *(m[n] for m in (shx, rex) for n in ("gu", "tr", "dn")), rex["xt"], q4["t1"], q4["gm"], q4["t2"],
                  pj["mm"], pj["tr"], mx_first, mx_second)

            loaded = set()
            for j, (need, blocks, hi, lo, scale) in enumerate(jobs):
                for n in need:
                    if n not in loaded:
                        pe.wait_ge(ld[n], 16 * {"qk": 2, "o_v": 2, "sh": 4}[n])
                        loaded.add(n)
                if j >= 8:
                    pe.wait_ge(w_lo, j - 7)
                for n, b in enumerate(blocks):
                    mm = pe.transpose(bank[j % 8][:, n * P:(n + 1) * P], b, ident[:, :])
                mm.then_inc(w_turned, 1)

            pe.wait_ge(w_lo, len(jobs))
            pe.wait_ge(nat_lo, 1)
            pe.wait_ge(bv_step, 4)
            for k in range(KC):
                for n, (m, (x, y)) in enumerate([(m, p) for m in range(KC) for p in THREE]):
                    mm = pe.matmul(bank[0][:, k * D:(k + 1) * D], wv[x][:, m, k * P:(k + 1) * P], woT[y][:, m, :],
                                   start=(n == 0), stop=(n == 5))
            mm.then_inc(wp_mm, 1)
            for n, (m, (x, y)) in enumerate([(m, p) for m in range(KC) for p in THREE]):
                mm = pe.matmul(bank[1][0:33, 0:D], bvc[x][:, m, :], woT[y][:, m, :], start=(n == 0), stop=(n == 5))
            mm.then_inc(wp_mm, 1)
            for k in range(KC):
                mm = pe.transpose(bank[2][:, k * E:(k + 1) * E], st_rw[:, k * P:(k + 1) * P], ident[0:E, 0:E])
            mm.then_inc(rw_mm, 1)
            gate(pe, end_w)

            def turn(c, i, b, src, banks, done, free, ready):
                pe.wait_ge(ready[0], ready[1])
                pe.wait_ge(free[0], free[1])
                for m in range(2):
                    for k in range(KC):
                        mm = pe.transpose(banks[b][:, k * D + m * P:k * D + (m + 1) * P],
                                          src[:, 2 * b + m, k * P:(k + 1) * P], ident[:, :])
                mm.then_inc(done, 1)

            def route(c):
                pe.wait_ge(ln["lo"], at(2 * c + 1))
                for m in range(G4):
                    for n, (k, (x, y)) in enumerate([(k, p) for k in range(KC) for p in THREE]):
                        mm = pe.matmul(a_bank[3][:, bass.ds((c * G4 + m) * E, E)],
                                       xT[x][:, k, bass.ds(c * CW + m * P, P)], rwT[y][:, k, :],
                                       start=(n == 0), stop=(n == 5))
                mm.then_inc(rt_mm, 1)

            def turn_x(c, i, g, more):
                for n in range(3):
                    if first_step(c) and n != 1:
                        pe.wait_ge(ld["gate_up" if n == 0 else "down"], 32)
                    pe.wait_ge(ex["lo"], at(3 * c + n - 3))
                    for m, w in enumerate(ex_job(c, n)[0]):
                        mm = pe.transpose(a_bank[n][:, m * P:(m + 1) * P], w, ident[:, :])
                    mm.then_inc(ex["turned"], 1)
                if not first_step(c):
                    route(c - 1)
                for b in range(2):
                    turn(c, i, b, xn[:, i, :, :], s_bank[2 * i:2 * i + 2], ln["mm"],
                         (ln["lo"], at(2 * (c - 2) + b)), (ln["xn"], at(c)))
            by(pe, NCH, 2, turn_x, head=NCH - 2)
            route(NCH - 1)

            pe.wait_ge(rt_sel, 1)
            gate(pe, end_x)
            pe.matmul(a_bank[1][:, :], before_h[:, :], sel_h[:, :], start=True, stop=True)
            pe.matmul(a_bank[2][:, :], ones_h[:, :], sel_h[:, :], start=True, stop=True).then_inc(rt_cnt, 1)

            def turn_inner(m, c, i):
                pe.wait_ge(m["h"], at(c))
                pe.wait_ge(m["lo"], at(c - 2))
                for e in range(2):
                    mm = pe.transpose(h_bank[i][:, e * P:(e + 1) * P], hh[:, i, e * P:(e + 1) * P], ident[:, :])
                mm.then_inc(m["tr"], 1)

            def shared_expert():
                def gate_up(c, i):
                    pe.wait_ge(shx["h"], at(c - 2))
                    for n, (kc, (x, y)) in enumerate([(kc, q) for kc in range(KC) for q in THREE]):
                        mm = pe.matmul(s_bank[i][:, :].rearrange("p (e c) -> p e c", e=2),
                                       xT[x][:, kc, bass.ds(c * P, P)], gu[y][:, E:NE, kc, :],
                                       start=(n == 0), stop=(n == 5))
                    mm.then_inc(shx["gu"], 1)

                def down(c, i):
                    pe.wait_ge(shx["lo"], at(c))
                    pe.wait_ge(shx["ev"], at(c - 2))
                    for n, (e, (x, y)) in enumerate([(e, q) for e in range(2) for q in THREE]):
                        mm = pe.matmul(a_bank[i][:, 0:D], hT[x][:, i, e * P:(e + 1) * P], dn[y][:, E + e, :],
                                       start=(n == 0), stop=(n == 5))
                    mm.then_inc(shx["dn"], 1)

                def step(c, i, g, more):
                    if more:
                        gate_up(c + 2, i)
                    if more or i == 0:
                        turn_inner(shx, c + 1, 1 - i)
                    down(c, i)
                gate_up(0, 0)
                gate_up(1, 1)
                turn_inner(shx, 0, 0)
                by(pe, TT, 2, step)

            def routed_experts():
                def turn_rows(c, r4, g):
                    pe.wait_ge(rex_ld[r4], 16 * g + 16)
                    pe.wait_ge(rex["xl"], at(c - 2))
                    for m in range(2):
                        for k in range(KC):
                            mm = pe.transpose(s_bank[2 + r4 % 2][:, k * D + m * P:k * D + (m + 1) * P],
                                              xs[:, r4, m, k * P:(k + 1) * P], ident[:, :])
                    mm.then_inc(rex["xt"], 1)

                def experts(c, n):
                    _, es = nc.values_load_multi_w_load_instructions(
                        expert_of[0:1, bass.ds(2 * c, 2 * n)], engines=(nc.tensor.engine,), min_val=0, max_val=E - 1,
                        skip_runtime_bounds_check_because="the routing clamps them to 0 .. E - 1")
                    return es

                def gate_up(c, i, es):
                    pe.wait_ge(rex["xl"], at(c))
                    pe.wait_ge(rex["h"], at(c - 2))
                    for m in range(2):
                        for n, (kc, (x, y)) in enumerate([(kc, q) for kc in range(KC) for q in THREE]):
                            mm = pe.matmul(s_bank[i][:, m * D:(m + 1) * D], xgT[x][:, i, kc, m * P:(m + 1) * P],
                                           gu[y][:, bass.ds(es[m], 1), kc, :].rearrange("p o c -> p (o c)"),
                                           start=(n == 0), stop=(n == 5))
                    mm.then_inc(rex["gu"], 1)

                def down(c, i, es):
                    pe.wait_ge(rex["lo"], at(c))
                    pe.wait_ge(rex["ev"], at(c - 2))
                    for m in range(2):
                        for n, (x, y) in enumerate(THREE):
                            mm = pe.matmul(a_bank[i][:, m * D:(m + 1) * D], hT[x][:, i, m * P:(m + 1) * P],
                                           dn[y][:, bass.ds(es[m], 1), :].rearrange("p o h -> p (o h)"),
                                           start=(n == 0), stop=(n == 2))
                    mm.then_inc(rex["dn"], 1)

                body = [None]

                def step(c, i, g, more):
                    if i == 0:
                        body[0] = experts(c, 6 if more else 4)
                    es = body[0]
                    if more or i == 0:
                        turn_rows(c + 3, (i + 3) % 4, g if i == 0 else g + 1)
                    if more or i < 2:
                        gate_up(c + 2, i % 2, es[2 * i + 4:2 * i + 6])
                    if more or i < 3:
                        turn_inner(rex, c + 1, 1 - i % 2)
                    down(c, i % 2, es[2 * i:2 * i + 2])
                first = experts(0, 2)
                for c in range(3):
                    turn_rows(c, c, 0)
                    if c:
                        gate_up(c - 1, c - 1, first[2 * c - 2:2 * c])
                turn_inner(rex, 0, 0)
                by(pe, NSLOT_T // 2, 4, step)

            def mix(m):
                def first(c, j):
                    k = m.step(c, j)
                    pe.wait_ge(m.act_done, at(k - 4))
                    seq = [(kc, q) for kc in range(KC) for q in m.pass1]
                    for n, (kc, (x, y)) in enumerate(seq):
                        mm = pe.matmul(s_bank[j % 4][:, :], m.stat(x, kc, j), m.mov(y, kc, c),
                                       start=(n == 0), stop=(n == len(seq) - 1))
                    mm.then_inc(m.first_done, 1)

                def second(c, i, j):
                    k = m.step(c, j)
                    pe.wait_ge(m.lo_done, at(k))
                    if j == 0:
                        pe.wait_ge(m.evac_read, at(m.ch(c - 2)))
                    for q in range(G4):
                        for n, (x, y) in enumerate(m.pass2):
                            part = (ah, al)[x]
                            mm = pe.matmul(a_bank[2 * i + q // 2][:, (q % 2) * D:(q % 2 + 1) * D],
                                           part[:, j % 4, q * P:(q + 1) * P], m.second(y, j),
                                           start=(j == 0 and n == 0 and q % 2 == 0),
                                           stop=(j == m.nt - 1 and n == len(m.pass2) - 1 and q % 2 == 1),
                                           skip_group_check=True)
                    mm.then_inc(m.second_done, 1)

                def chunk(c, i, g, more):
                    for j in range(m.nt):
                        if j + 2 < m.nt:
                            first(c, j + 2)
                        elif more or i == 0:
                            first(c + 1, j + 2 - m.nt)
                        second(c, i, j)
                first(0, 0)
                first(0, 1)
                by(pe, m.nch, 2, chunk)

            def late_round():
                pe.wait_ge(kn_step, 3 * KC)
                for j, (blocks, hi, lo, scale) in enumerate(late_jobs):
                    if j >= 8:
                        pe.wait_ge(w_lo, len(jobs) + j - 7)
                    if j == LATE_LO:
                        pe.wait_ge(tn_made, 2)
                    for n, w in enumerate(blocks):
                        mm = pe.transpose(bank[j % 8][:, n * P:(n + 1) * P], w, ident[:, :])
                    mm.then_inc(w_turned, 1)

            before = end_rt
            for b in range(B):
                first_t = b * (S // P)
                gate(pe, before)
                if b == 1:
                    late_round()
                    gate(pe, end_late)

                def project(t, i):
                    pe.wait_ge(pj["qkn"], at(first_t + t - 4))
                    pe.matmul(s_bank[i % 4][:, :], ones33[:, :], biasz[:, 0:2 * D], start=True, stop=False)
                    for n, (k, (x, y)) in enumerate([(k, p) for k in range(KC) for p in THREE]):
                        mm = pe.matmul(s_bank[i % 4][:, :], xT[x][:, k, bass.ds(b * S + t * P, P)], wqkT[y][:, k, :],
                                       start=False, stop=(n == 5))
                    pe.wait_ge(pj["vlo"], at(first_t + t - 2))
                    v_ps = a_bank[2 + i % 2][:, 0:D]
                    pe.matmul(v_ps, ones33[:, :], biasz[:, 2 * D:3 * D], start=True, stop=False)
                    for n, (k, (x, y)) in enumerate([(k, p) for k in range(KC) for p in THREE]):
                        mm = pe.matmul(v_ps, xT[x][:, k, bass.ds(b * S + t * P, P)], wpT[y][:, k, :],
                                       start=False, stop=(n == 5))
                    mm.then_inc(pj["mm"], 1)

                def turn_qk(t, i, g, more):
                    if more or i == 0:
                        project(t + 3, i + 3)
                    pe.wait_ge(pj["qkn"], at(first_t + t))
                    pe.wait_ge(pj["tlo"], at(first_t + t - 2))
                    for n in range(2 * KC):
                        mm = pe.transpose(a_bank[i % 2][:, n * P:(n + 1) * P], qkn[:, i % 2, n * P:(n + 1) * P],
                                          ident[:, :])
                    mm.then_inc(pj["tr"], 1)
                for t in range(3):
                    project(t, t)
                by(pe, S // P, 4, turn_qk)
                gate(pe, end_pj[b])
                mix(at_mix[b])
                before = end_mix(at_mix[b])
                if b == 0:
                    gate(pe, before)
                    shared_expert()
                    gate(pe, end_sh)
                    routed_experts()
                    before = end_mo

            gate(pe, before)

            def turn1(c, i):
                for b in range(2):
                    turn(c, i, b, xn[:, i, :, :], s_bank[0:2], q4["t1"],
                         (q4["l1"], at(2 * (c - 1) + b)), (q4["xn"], at(c)))

            def turn2(c, i):
                for b in range(2):
                    turn(c, i, b, qsb[i], s_bank[2:4], q4["t2"],
                         (q4["l2"], at(2 * (c - 1) + b)), (q4["qs"], at(c)))

            def second_block(c, i, g, more):
                pe.wait_ge(q4["l1"], at(2 * c + 1))
                pe.wait_ge(q4["nn"], at(c - 1))
                for m in range(G4):
                    for n, (k, (x, y)) in enumerate([(k, p) for k in range(KC) for p in THREE]):
                        mm = pe.matmul(a_bank[m][:, 0:D], xT[x][:, k, bass.ds(c * CW + m * P, P)], gram[y][:, k, :],
                                       start=(n == 0), stop=(n == 5))
                mm.then_inc(q4["gm"], 1)
                if not first_step(c):
                    turn2(c - 1, 1 - i)
                if more or i == 0:
                    turn1(c + 1, 1 - i)
            for k in range(KC):
                seq = [(m, p) for m in range(NB // P) for p in THREE]
                for n, (m, (x, y)) in enumerate(seq):
                    mm = pe.matmul(a_bank[0][:, k * D:(k + 1) * D], kn[x][m // KN][:, m % KN, k * P:(k + 1) * P],
                                   kn[y][m // KN][:, m % KN, :], start=(n == 0), stop=(n == len(seq) - 1))
            mm.then_inc(gram_mm, 1)
            turn1(0, 0)
            pe.wait_ge(gram_lo, 1)
            by(pe, NCH, 2, second_block, head=2)
            turn2(NCH - 1, 1)

            gate(pe, end_q4)
            mix(ff_mix)
            gate(pe, end_mix(ff_mix))
            mix(bk_mix)

        @block.scalar
        def _(act):
            open_(act, ln["hi"], ex["hi"], *(m[n] for m in (shx, rex) for n in ("sig", "hi", "ev")), rex["xh"], q4["sig"], q4["h1"], q4["qs"], q4["h2"], bk_tanh,
                  pj["qkn"], pj["vhi"], pj["thi"], mx_act)

            def copy(out_ap, in_ap, scale, done):
                act.activation(out_ap, in_ap, ACT.Copy, scale=scale).then_inc(done, 1)

            for j, (need, blocks, hi, lo, scale) in enumerate(jobs):
                act.wait_ge(w_turned, j + 1)
                copy(hi, job_ps(j), scale, w_hi)
                if j == WO_JOBS:
                    act.wait_ge(ld["o_v"], 32)
                    copy(wv[0][:, :, :], st_wv, WQK_S, nat_hi)
            act.wait_ge(wp_mm, 1)
            copy(wpT[0][:, :, :], bank[0][:, :].rearrange("p (k c) -> p k c", k=KC), WP_S / (WQK_S * WO_S), wp_hi)
            act.wait_ge(rw_mm, 1)
            copy(rwT[0][:, :, :], bank[2][:, 0:2 * E].rearrange("p (k c) -> p k c", k=KC), WQK_S, rw_hi)
            def hi_of(c, i, b, banks, dst, scale, turned, done):
                act.wait_ge(turned, at(2 * c + b))
                copy(dst[0][:, :, bass.ds(c * CW + b * D, D)], banks[b][:, :].rearrange("p (k c) -> p k c", k=KC),
                     scale, done)

            gate(act, end_w)

            def hi_x(c, i, g, more):
                for n in range(3):
                    act.wait_ge(ex["turned"], at(3 * c + n))
                    copy(ex_job(c, n)[1][0], a_bank[n][:, :].rearrange("p (k c) -> p k c", k=2), WQK_S, ex["hi"])
                for b in range(2):
                    hi_of(c, i, b, s_bank[2 * i:2 * i + 2], xT, X_S, ln["mm"], ln["hi"])
            by(act, NCH, 2, hi_x)

            gate(act, end_x)
            act.wait_ge(rt_mm, NCH)
            act.activation(scores[:, :], a_bank[3][:, :], ACT.Sigmoid, scale=1.0 / QK_PS).then_inc(rt_sig, 1)

            def sigmoid_gate(m, c, i):
                act.wait_ge(m["gu"], at(c))
                act.wait_ge(m["t1"], at(c - 2))
                act.activation(sg[:, i, :].rearrange("p (e c) -> p e c", e=2),
                               s_bank[i][:, :].rearrange("p (e c) -> p e c", e=2)[:, :, 0:IM],
                               ACT.Sigmoid, scale=1.0 / QK_PS).then_inc(m["sig"], 1)

            def inner_hi(m, c, i):
                act.wait_ge(m["tr"], at(c))
                act.wait_ge(m["dn"], at(c - 2))
                copy(hT[0][:, i, :], h_bank[i][:, 0:D], 1.0, m["hi"])

            def shared_expert():
                def rows_out(c, i, g):
                    act.wait_ge(shx["dn"], at(c))
                    act.wait_ge(shx_st[i], 16 * g + 16)
                    copy(yres[:, i, 0, :], a_bank[i][:, 0:D], 1.0 / (H_S * WQK_S), shx["ev"])

                def step(c, i, g, more):
                    inner_hi(shx, c, i)
                    if more or i == 0:
                        sigmoid_gate(shx, c + 1, 1 - i)
                    if not first_step(c):
                        rows_out(c - 1, 1 - i, g - 1 + i)
                sigmoid_gate(shx, 0, 0)
                by(act, TT, 2, step, head=2)
                rows_out(TT - 1, 1, TT // 2 - 1)

            def routed_experts():
                def rows_hi(c, i):
                    act.wait_ge(rex["xt"], at(c))
                    act.wait_ge(rex["gu"], at(c - 2))
                    copy(xgT[0][:, i, :, :], s_bank[2 + i][:, :].rearrange("p (k c) -> p k c", k=KC), X_S, rex["xh"])

                def rows_out(c, i, g):
                    act.wait_ge(rex["dn"], at(c))
                    act.wait_ge(rex_st[i % 2], 32 * g + 16 * (i // 2) + 16)
                    copy(yres[:, i % 2, :, :], a_bank[i % 2][:, :].rearrange("p (m d) -> p m d", m=2),
                         1.0 / (H_S * WQK_S), rex["ev"])

                def step(c, i, g, more):
                    inner_hi(rex, c, i % 2)
                    if more or i < 3:
                        sigmoid_gate(rex, c + 1, 1 - i % 2)
                    if more or i == 0:
                        rows_hi(c + 3, 1 - i % 2)
                    if not first_step(c):
                        rows_out(c - 1, (i + 3) % 4, g if i else g - 1)
                for c in range(3):
                    rows_hi(c, c % 2)
                sigmoid_gate(rex, 0, 0)
                by(act, NSLOT_T // 2, 4, step, head=4)
                rows_out(NSLOT_T // 2 - 1, 3, NSLOT_T // 8 - 1)

            def store_rows(b, c, i):
                act.wait_ge(mx_evac, at(at_mix[b].ch(c)))
                act.dma_start(one(s0_c, b * (S // CW) + c), xin[:, i, :, :]).then_inc(at_mix[b].stored[i], 16)

            def mix(m, at_chunk=None, store=None):
                def chunk(c, i, g, more):
                    for j in range(m.nt):
                        if j == 2 and at_chunk:
                            at_chunk(c, i, g)
                        if j == 6 and store is not None and not first_step(c):
                            store_rows(store, c - 1, 1 - i)
                        k = m.step(c, j)
                        act.wait_ge(m.first_done, at(k))
                        act.wait_ge(m.lo_done, at(k - 2))
                        act.activation(att[:, j % 2, :], s_bank[j % 4][:, :], m.func,
                                       bias=m.bias(j) if m.bias else 0.0, scale=m.scale).then_inc(m.act_done, 1)
                by(act, m.nch, 2, chunk, head=2 if store is not None else 0)
                if store is not None:
                    store_rows(store, m.nch - 1, 1)

            before = end_rt
            for b in range(B):
                first_t = b * (S // P)
                gate(act, before)
                if b == 1:
                    for j, (blocks, hi, lo, scale) in enumerate(late_jobs):
                        act.wait_ge(w_turned, len(jobs) + j + 1)
                        copy(hi, job_ps(j), scale, w_hi)
                    gate(act, end_late)

                def values_hi(t, i):
                    act.wait_ge(pj["mm"], at(first_t + t))
                    copy(vp[0][:, bass.ds(t, 1), :].rearrange("p o e -> p (o e)"), a_bank[2 + i % 2][:, 0:D],
                         V_S / VP_PS, pj["vhi"])

                def norm_rows(t, i):
                    act.wait_ge(pj["nmr"], at(first_t + t))
                    act.wait_ge(pj["tr"], at(first_t + t - 2))
                    for n in range(2):
                        ins = act.activation(qkn[:, i % 2, n * D:(n + 1) * D], s_bank[i % 4][:, n * D:(n + 1) * D],
                                             ACT.Identity, bias=nmr[:, i % 2, n:n + 1], scale=rstd[:, i % 2, n:n + 1])
                    ins.then_inc(pj["qkn"], 1)

                def rows_hi(t, i, g, more):
                    if more or i < 2:
                        values_hi(t + 2, i + 2)
                    if more or i < 3:
                        norm_rows(t + 1, i + 1)
                    act.wait_ge(pj["tr"], at(first_t + t))
                    copy(qkT[0][:, :, bass.ds(t * P, P)], a_bank[i % 2][:, :].rearrange("p (k c) -> p k c", k=2 * KC),
                         X_S, pj["thi"])
                values_hi(0, 0)
                values_hi(1, 1)
                norm_rows(0, 0)
                by(act, S // P, 4, rows_hi)
                gate(act, end_pj[b])
                mix(at_mix[b], store=b)
                before = end_mix(at_mix[b])
                if b == 0:
                    gate(act, before)
                    shared_expert()
                    gate(act, end_sh)
                    routed_experts()
                    before = end_mo

            gate(act, before)
            def open_gate(c, i, g):
                act.wait_ge(g_ld[i], 16 * g + 16)
                act.wait_ge(q4["m1"], at(c - 2))
                act.activation(sgb[i], gin[i], ACT.Sigmoid).then_inc(q4["sig"], 1)

            def hi_rows(c, i):
                for b in range(2):
                    hi_of(c, i, b, s_bank[0:2], xT, X_S, q4["t1"], q4["h1"])

            def hi_queries(c, i):
                for b in range(2):
                    hi_of(c, i, b, s_bank[2:4], qsT, QS_S, q4["t2"], q4["h2"])

            def second_block(c, i, g, more):
                if more:
                    open_gate(c + 2, i, g + 1)
                if not first_step(c):
                    hi_queries(c - 1, 1 - i)
                if more or i == 0:
                    hi_rows(c + 1, 1 - i)
                act.wait_ge(q4["rn"], at(c))
                act.wait_ge(q4["t2"], at(2 * (c - 2) + 1))
                for m in range(G4):
                    ins = act.activation(qsb[i][:, m, :], xn[:, i, m, :], ACT.Copy, scale=rn2[:, i, m:m + 1])
                ins.then_inc(q4["qs"], 1)
            open_gate(0, 0, 0)
            open_gate(1, 1, 0)
            act.wait_ge(ld["vb"], 16)
            copy(vb[0], st_vb, K_S, vb_hi)
            act.wait_ge(gram_mm, 1)
            copy(gram[0][:, :, :], a_bank[0][:, :].rearrange("p (k c) -> p k c", k=KC), GRAM_S / (K_S * K_S), gram_hi)
            hi_rows(0, 0)
            by(act, NCH, 2, second_block, head=2)
            hi_queries(NCH - 1, 1)

            gate(act, end_q4)
            mix(ff_mix)
            gate(act, end_mix(ff_mix))

            def tanh_half(c, i, g):
                act.wait_ge(bk_ld[i], 32 * g + 32)
                act.wait_ge(bk_silu, at(c - 2))
                act.activation(tbuf[i], gl[i], ACT.Tanh, scale=0.5).then_inc(bk_tanh, 1)
            mix(bk_mix, tanh_half)

        @block.vector
        def _(dve):
            dve.memset(bias3[:, :], 0.0)
            dve.memset(ones33[:, :], X_S)
            dve.memset(onesf[:, :], 1.0)
            dve.memset(xr[:, 0, :], 0.0)
            dve.memset(nlogs[:, :], -math.log(S)).then_inc(consts, 1)
            open_(dve, ex["lo"], *(ln[n] for n in ("mv", "ve", "xn", "lo")),
                  *(pj[n] for n in ("mv", "ve", "nmr", "vlo", "tlo")),
                  *(m[n] for m in (shx, rex) for n in ("t1", "h", "lo")), rex["xl"], cb_step, cb_done,
                  *(q4[n] for n in ("m1", "m2", "x1", "mv", "ve", "xn", "l1", "nn", "l2")), bk_silu,
                  mx_hi, mx_lo, mx_read, mx_evac)

            def low(out_ap, in_ap, scale, hi_ap, done=None):
                ins = dve.scalar_tensor_tensor(out=out_ap, in0=in_ap, scalar=scale, in1=hi_ap, op0=ALU.mult,
                                               op1=ALU.subtract)
                if done is not None:
                    ins.then_inc(done, 1)

            for j, (need, blocks, hi, lo, scale) in enumerate(jobs):
                dve.wait_ge(w_hi, j + 1)
                low(lo, job_ps(j), scale, hi, w_lo)
                if j == WO_JOBS:
                    dve.wait_ge(nat_hi, 1)
                    low(wv[1][:, :, :], st_wv, WQK_S, wv[0][:, :, :], nat_lo)
            dve.wait_ge(consts, 1)
            dve.wait_ge(ld["small"], 16 * 10)
            for t in range(KC):
                dve.tensor_scalar(bvt[:, t, :], onesf[:, 0:33], bvf[:, t:t + 1], WQK_S, ALU.mult, ALU.mult
                                  ).then_inc(bv_step, 1)
            dve.wait_ge(bv_step, 2)
            dve.tensor_copy(bvc[0][:, :, :], bvt[:, :, :]).then_inc(bv_step, 1)
            dve.wait_ge(bv_step, 3)
            low(bvc[1][:, :, :], bvt[:, :, :], 1.0, bvc[0][:, :, :], bv_step)
            dve.wait_ge(wp_hi, 1)
            low(wpT[1][:, :, :], bank[0][:, :].rearrange("p (k c) -> p k c", k=KC), WP_S / (WQK_S * WO_S),
                wpT[0][:, :, :], wp_lo)
            dve.wait_ge(wp_mm, 2)
            for r in (0, 32):
                dve.tensor_scalar(bias3[r:r + 1, 2 * D:3 * D], bank[1][r:r + 1, 0:D],
                                  WP_S / (WQK_S * WQK_S * WO_S), None, ALU.mult).then_inc(bias_step, 1)
            dve.wait_ge(bias_step, 2)
            dve.tensor_scalar(biasz[:, :], bias3[:, :], WQK_S, None, ALU.mult).then_inc(bias_step, 1)
            dve.wait_ge(bias_step, 3)
            low(biasz[32:33, :], bias3[32:33, :], WQK_S, biasz[32:33, :], bias_step)
            dve.wait_ge(rw_hi, 1)
            low(rwT[1][:, :, :], bank[2][:, 0:2 * E].rearrange("p (k c) -> p k c", k=KC), WQK_S, rwT[0][:, :, :],
                rw_lo)
            def low_of(c, i, b, banks, dst, scale, his, done):
                dve.wait_ge(his, at(2 * c + b))
                cols = bass.ds(c * CW + b * D, D)
                low(dst[1][:, :, cols], banks[b][:, :].rearrange("p (k c) -> p k c", k=KC), scale,
                    dst[0][:, :, cols], done)

            gate(dve, end_w)

            def moments(src, n, i, c, q, eps):
                for m in range(n):
                    dve.bn_stats(stat[:, i, m, :], src(m))
                dve.drain()
                for m in range(n):
                    ins = dve.bn_aggr(mv[:, i, m, :], stat[:, i, m, :])
                ins.then_inc(q["mv"], 1)
                dve.wait_ge(q["mv"], at(c))
                dve.tensor_scalar(ve[:, i, 0:n], mv[:, i, 0:n, 1], eps, None, ALU.add).then_inc(q["ve"], 1)

            def norm(src, i, c, q):
                dve.wait_ge(q["rs"], at(c))
                for m in range(G4):
                    ins = dve.tensor_scalar(xn[:, i, m, :], src[:, i, m, :], mv[:, i, m, 0:1], rstd[:, i, m:m + 1],
                                            ALU.subtract, ALU.mult)
                ins.then_inc(q["xn"], 1)

            def x_moments(c, i, g):
                dve.wait_ge(x_ld[i], 16 * g + 16)
                moments(lambda m: xin[:, i, m, :], G4, i, c, ln, EPS)

            def x_norm(c, i, g, more):
                if more or i == 0:
                    x_moments(c + 1, 1 - i, g + i)
                dve.wait_ge(ln["mm"], at(2 * (c - 2) + 1))
                dve.wait_ge(xn_st[i], 16 * (g + 1))
                norm(xin, i, c, ln)
                for n in range(3):
                    dve.wait_ge(ex["hi"], at(3 * c + n))
                    hi, lo = ex_job(c, n)[1]
                    low(lo, a_bank[n][:, :].rearrange("p (k c) -> p k c", k=2), WQK_S, hi, ex["lo"])
                for b in range(2):
                    low_of(c, i, b, s_bank[2 * i:2 * i + 2], xT, X_S, ln["hi"], ln["lo"])
            x_moments(0, 0, 0)
            by(dve, NCH, 2, x_norm)

            gate(dve, end_x)
            dve.wait_ge(rt_sig, 1)
            count = [0]

            def step(ins):
                count[0] += 1
                ins.then_inc(rt_step, 1)
                dve.wait_ge(rt_step, count[0])

            sc3 = scores[:, :].rearrange("p (t e) -> p t e", e=E)
            b3 = biased[:, :].rearrange("p (t e) -> p t e", e=E)
            step(dve.tensor_tensor(b3, sc3, spread(eb_b[:, :].rearrange("p (o e) -> p o e", o=1), 1, TT), ALU.add))
            b4 = biased[:, :].rearrange("p (n e) -> p n e", e=EPG)
            pairs = [(x, y) for x in range(EPG) for y in range(x + 1, EPG)]
            for n, (x, y) in enumerate(pairs):
                ins = dve.tensor_tensor(pair_s[:, :, n], b4[:, :, x], b4[:, :, y], ALU.add)
            step(ins)
            step(dve.tensor_reduce(gs[:, :], pair_s[:, :, :], AXX, ALU.max))

            def ranks(vals, n, beat, rank):
                dve.memset(beat[:, :, 0:n * n:n + 1], 0.0)
                bt = beat[:, :, :].rearrange("p t (x y) -> p t x y", x=n)
                for x in range(n):
                    for lo_, hi_, op in ((0, x, ALU.is_ge), (x + 1, n, ALU.is_gt)):
                        if hi_ > lo_:
                            ins = dve.tensor_tensor(bt[:, :, x, lo_:hi_], vals[:, :, lo_:hi_],
                                                    spread(vals[:, :, x:x + 1], 2, hi_ - lo_), op)
                step(ins)
                step(dve.tensor_reduce(rank, bt, AXX, ALU.add))

            ranks(gs[:, :].rearrange("p (t g) -> p t g", g=GROUPS), GROUPS, gbeat,
                  grank[:, :].rearrange("p (t g) -> p t g", g=GROUPS))
            step(dve.tensor_scalar(gsel[:, :], grank[:, :], GTOP - 0.5, None, ALU.is_lt))
            step(dve.tensor_tensor(masked[:, :].rearrange("p (n e) -> p n e", e=EPG), b4,
                                   spread(gsel[:, :].rearrange("p (n o) -> p n o", o=1), 2, EPG), ALU.mult))
            m3 = masked[:, :].rearrange("p (t e) -> p t e", e=E)
            ranks(m3, E, ebeat, erank[:, :].rearrange("p (t e) -> p t e", e=E))
            dve.tensor_scalar(sel_h[:, :], erank[:, :], TOPK - 0.5, None, ALU.is_lt).then_inc(rt_sel, 1)
            step(dve.scalar_tensor_tensor(out=masked[:, :], in0=erank[:, :], scalar=TOPK - 0.5, in1=scores[:, :],
                                          op0=ALU.is_lt, op1=ALU.mult))
            step(dve.tensor_reduce(esum[:, 0:TT], m3, AXX, ALU.add))
            step(dve.tensor_scalar(esum[:, 0:TT], esum[:, 0:TT], 1e-20, None, ALU.add))
            step(dve.reciprocal(esum[:, TT:2 * TT], esum[:, 0:TT]))
            step(dve.scalar_tensor_tensor(out=b3, in0=m3, scalar=ROUTE_SCALE,
                                          in1=spread(esum[:, TT:2 * TT].rearrange("p (t o) -> p t o", o=1), 2, E),
                                          op0=ALU.mult, op1=ALU.mult))
            dve.wait_ge(rt_cnt, 1)
            total = a_bank[2][:, :].rearrange("p (t e) -> p t e", e=E)
            step(dve.tensor_copy(cnt[0], total))
            src, dst = 0, 1
            d = 1
            while d < TT:
                dve.tensor_copy(cnt[dst][:, 0:d, :], cnt[src][:, 0:d, :])
                step(dve.tensor_tensor(cnt[dst][:, d:TT, :], cnt[src][:, d:TT, :], cnt[src][:, 0:TT - d, :], ALU.add))
                src, dst, d = dst, src, 2 * d
            run = cnt[src]
            step(dve.tensor_tensor(cnt[dst], run, total, ALU.subtract))
            within = a_bank[1][:, :].rearrange("p (t e) -> p t e", e=E)
            step(dve.tensor_scalar(small[0], run[:, TT - 1, :], 1.0 / P, 127.0 / P - 0.5 + 0.5 / P, ALU.mult, ALU.add))
            step(dve.tensor_scalar(small[1], small[0], ROUND, None, ALU.add))
            step(dve.tensor_scalar(small[2], small[1], -ROUND, None, ALU.add))
            step(dve.tensor_copy(small[3], small[2]))
            a_, b_, d = 3, 4, 1
            while d < E:
                dve.tensor_copy(small[b_][:, 0:d], small[a_][:, 0:d])
                step(dve.tensor_tensor(small[b_][:, d:E], small[a_][:, d:E], small[a_][:, 0:E - d], ALU.add))
                a_, b_, d = b_, a_, 2 * d
            ends = small[a_]
            step(dve.tensor_tensor(small[5], ends, small[2], ALU.subtract))
            step(dve.tensor_scalar(small[6], small[5], float(P), None, ALU.mult))
            step(dve.tensor_tensor(cnt[2], cnt[dst], within, ALU.add))
            step(dve.tensor_tensor(cnt[2], cnt[2], spread(small[6].rearrange("p (o e) -> p o e", o=1), 1, TT), ALU.add))
            er3 = erank[:, :].rearrange("p (t e) -> p t e", e=E)
            for k in range(TOPK):
                for n, v in enumerate((cnt[2], b3)):
                    ins = dve.scalar_tensor_tensor(out=picks[n][:, k, :, :], in0=er3, scalar=float(k), in1=v,
                                                   op0=ALU.is_equal, op1=ALU.mult)
            step(ins)
            dve.tensor_reduce(slot_f.rearrange("p (k t) -> p k t", k=TOPK), picks[0], AXX, ALU.add)
            step(dve.tensor_reduce(w4[:, :, :], picks[1], AXX, ALU.add))
            dve.tensor_copy(slot_i[:, :, :], slot_f.rearrange("p (k t) -> p k t", k=TOPK))
            step(dve.tensor_copy(tile_f, tile_no[:, :]))
            step(dve.tensor_tensor(upto, spread(ends[0:1, :].rearrange("p (o e) -> p o e", o=1), 1, NSLOT_T),
                                   spread(tile_f.rearrange("p (j o) -> p j o", o=1), 2, E), ALU.is_le))
            step(dve.tensor_reduce(exp_f, upto, AXX, ALU.add))
            dve.tensor_scalar(expert_of[:, :], exp_f, float(E - 1), None, ALU.min).then_inc(rt_done, 1)

            def inner(m, c, i):
                ps = s_bank[i][:, :].rearrange("p (e c) -> p e c", e=2)
                t3 = t1[:, i, :].rearrange("p (e c) -> p e c", e=2)
                dve.wait_ge(m["sig"], at(c))
                dve.tensor_tensor(t3, sg[:, i, :].rearrange("p (e c) -> p e c", e=2), ps[:, :, 0:IM], ALU.mult
                                  ).then_inc(m["t1"], 1)
                dve.wait_ge(m["t1"], at(c))
                dve.wait_ge(m["tr"], at(c - 2))
                dve.scalar_tensor_tensor(out=hh[:, i, :].rearrange("p (e c) -> p e c", e=2), in0=t3,
                                         scalar=H_S / (QK_PS * QK_PS), in1=ps[:, :, IM:2 * IM],
                                         op0=ALU.mult, op1=ALU.mult).then_inc(m["h"], 1)

            def inner_lo(m, c, i):
                dve.wait_ge(m["hi"], at(c))
                low(hT[1][:, i, :], h_bank[i][:, 0:D], 1.0, hT[0][:, i, :], m["lo"])

            def shared_expert():
                def one_step(c, i, g, more):
                    inner_lo(shx, c, i)
                    if more or i == 0:
                        inner(shx, c + 1, 1 - i)
                inner(shx, 0, 0)
                by(dve, TT, 2, one_step)
                dve.wait_ge(ld["w12"], 32)
                for n in range(2):
                    dve.tensor_reduce(thr[:, n:n + 1], st_w[n], AXX, ALU.add, apply_absolute_value=True
                                      ).then_inc(tn_sum, 1)

            def routed_experts():
                def rows_lo(c, i):
                    dve.wait_ge(rex["xh"], at(c))
                    low(xgT[1][:, i, :, :], s_bank[2 + i][:, :].rearrange("p (k c) -> p k c", k=KC), X_S,
                        xgT[0][:, i, :, :], rex["xl"])

                def one_step(c, i, g, more):
                    inner_lo(rex, c, i % 2)
                    if more or i < 3:
                        inner(rex, c + 1, 1 - i % 2)
                    if more or i == 0:
                        rows_lo(c + 3, 1 - i % 2)
                    if isinstance(c, int) and c == 3:
                        dve.wait_ge(tn_dma, 32)
                        dve.tensor_reduce(thr[:, 2:4], w_sums.rearrange("p q n -> p n q"), AXX, ALU.add
                                          ).then_inc(tn_step, 1)
                for c in range(3):
                    rows_lo(c, c % 2)
                inner(rex, 0, 0)
                by(dve, NSLOT_T // 2, 4, one_step, head=4)

            def combine(c, j):
                if j % 2 == 0:
                    return
                t, r = c * (S // P // 2) + j // 2, j // 2 % 2
                pair = c * (S // P // 4) + j // 4
                dve.wait_ge(sh_ld[r], 16 * pair + 16)
                dve.wait_ge(y_ld[r], 16 * TOPK * pair + 16 * TOPK)
                dve.wait_ge(cb_st[r], 16 * pair + 16)
                acc = yg[:, r, TOPK, :]
                for k in range(TOPK):
                    last = k == TOPK - 1
                    dve.scalar_tensor_tensor(
                        out=cres[:, r, :] if last else acc, in0=yg[:, r, k, :],
                        scalar=w4[:, k, bass.ds(t, 1)], in1=acc, op0=ALU.mult, op1=ALU.add
                    ).then_inc(cb_done if last else cb_step, 1)
                    if not last:
                        dve.wait_ge(cb_step, 3 * t + k + 1 + CR)

            def mix(m, evac, at_chunk=None, at_step=None):
                def split(c, j):
                    k = m.step(c, j)
                    dve.wait_ge(m.act_done, at(k))
                    dve.wait_ge(m.second_done, at(k - 4))
                    dve.tensor_scalar(ah[:, j % 4, :], att[:, j % 2, :], m.split, None, ALU.mult
                                      ).then_inc(m.hi_done, 1)
                    dve.wait_ge(m.hi_done, at(k))
                    low(al[:, j % 4, :], att[:, j % 2, :], m.split, ah[:, j % 4, :], m.lo_done)

                def chunk(c, i, g, more):
                    for j in range(2, m.nt):
                        if j == 4 and at_chunk:
                            at_chunk(c, i, g)
                        split(c, j)
                        if at_step:
                            at_step(c, j)
                    if more or i == 0:
                        for j in range(2):
                            split(c + 1, j)
                            if at_step:
                                at_step(c + 1, j)
                    dve.wait_ge(m.second_done, at(m.step(c, m.nt - 1)))
                    dve.wait_ge(m.stored[i], m.st(g))
                    evac(m, c, i)
                for j in range(2):
                    split(0, j)
                    if at_step:
                        at_step(0, j)
                by(dve, m.nch, 2, chunk)

            def two(ap):
                return spread(ap[:, :].rearrange("p (o d) -> p o d", o=1), 1, 2)

            def half(h, i):
                return a_bank[2 * i + h][:, :].rearrange("p (o d) -> p o d", o=2)

            def evac_attention(m, c, i):
                for h in range(2):
                    ins = dve.scalar_tensor_tensor(out=xin[:, i, 2 * h:2 * h + 2, :], in0=half(h, i),
                                                   scalar=1.0 / (ATT_S * V_S), in1=two(bo_b), op0=ALU.mult,
                                                   op1=ALU.add)
                ins.then_inc(m.evac_read, 1)
                dve.wait_ge(m.evac_read, at(m.ch(c)))
                for h in range(2):
                    ins = dve.tensor_tensor(xin[:, i, 2 * h:2 * h + 2, :], xin[:, i, 2 * h:2 * h + 2, :], two(ls_b),
                                            ALU.mult)
                ins.then_inc(m.evac_done, 1)

            before = end_rt
            for b in range(B):
                first_t = b * (S // P)
                gate(dve, before)
                if b == 1:
                    for j, (blocks, hi, lo, scale) in enumerate(late_jobs[:LATE_LO]):
                        dve.wait_ge(w_hi, len(jobs) + j + 1)
                        low(lo, job_ps(j), scale, hi, w_lo)
                    gate(dve, end_late)

                def row_moments(t, i):
                    dve.wait_ge(pj["mm"], at(first_t + t))
                    dve.wait_ge(pj["qkn"], at(first_t + t - 2))
                    moments(lambda m: s_bank[i % 4][:, m * D:(m + 1) * D], 2, i % 2, first_t + t, pj, EPS * QK_PS * QK_PS)
                    dve.wait_ge(pj["vhi"], at(first_t + t))
                    rows_t = bass.ds(t, 1)
                    low(vp[1][:, rows_t, :].rearrange("p o e -> p (o e)"), a_bank[2 + i % 2][:, 0:D], V_S / VP_PS,
                        vp[0][:, rows_t, :].rearrange("p o e -> p (o e)"), pj["vlo"])

                def shifts(t, i):
                    dve.wait_ge(pj["rs"], at(first_t + t))
                    dve.scalar_tensor_tensor(out=nmr[:, i % 2, 0:2], in0=mv[:, i % 2, 0:2, 0], scalar=-1.0,
                                             in1=rstd[:, i % 2, 0:2], op0=ALU.mult, op1=ALU.mult
                                             ).then_inc(pj["nmr"], 1)

                def rows_lo(t, i, g, more):
                    if more or i < 3:
                        shifts(t + 1, i + 1)
                    if more or i < 2:
                        row_moments(t + 2, i + 2)
                    dve.wait_ge(pj["thi"], at(first_t + t))
                    cols = bass.ds(t * P, P)
                    low(qkT[1][:, :, cols], a_bank[i % 2][:, :].rearrange("p (k c) -> p k c", k=2 * KC), X_S,
                        qkT[0][:, :, cols], pj["tlo"])
                row_moments(0, 0)
                row_moments(1, 1)
                shifts(0, 0)
                by(dve, S // P, 4, rows_lo)
                gate(dve, end_pj[b])
                mix(at_mix[b], evac_attention, at_step=combine if b == 1 else None)
                before = end_mix(at_mix[b])
                if b == 0:
                    gate(dve, before)
                    shared_expert()
                    gate(dve, end_sh)
                    routed_experts()
                    before = end_mo

            gate(dve, before)
            def add_up(c, i, g):
                dve.wait_ge(q4["sig"], at(c))
                dve.tensor_tensor(gin[i], gin[i], sgb[i], ALU.mult).then_inc(q4["m1"], 1)
                dve.wait_ge(q4["m1"], at(c))
                dve.wait_ge(q4_ld[i], 32 * g + 32)
                dve.tensor_tensor(gin[i], gin[i], sin[i], ALU.mult).then_inc(q4["m2"], 1)
                dve.wait_ge(q4["m2"], at(c))
                dve.tensor_tensor(xin[:, i, :, :], xin[:, i, :, :], gin[i], ALU.add).then_inc(q4["x1"], 1)
                dve.wait_ge(q4["x1"], at(c))
                moments(lambda m: xin[:, i, m, :], G4, i, c, q4, EPS)

            def norm_x1(c, i):
                dve.wait_ge(q4["t1"], at(2 * (c - 2) + 1))
                dve.wait_ge(q4["qs"], at(c - 2))
                norm(xin, i, c, q4)

            def lo_rows(c, i):
                for b in range(2):
                    low_of(c, i, b, s_bank[0:2], xT, X_S, q4["h1"], q4["l1"])

            def lo_queries(c, i):
                for b in range(2):
                    low_of(c, i, b, s_bank[2:4], qsT, QS_S, q4["h2"], q4["l2"])

            def second_block(c, i, g, more):
                if more:
                    add_up(c + 2, i, g + 1)
                if more or i == 0:
                    norm_x1(c + 1, 1 - i)
                dve.wait_ge(q4["gm"], at(c))
                dve.wait_ge(q4["rn"], at(c - 2))
                for m in range(G4):
                    ins = dve.tensor_tensor_reduce(out=junk[:, m, :], in0=a_bank[m][:, 0:D], in1=xn[:, i, m, :],
                                                   scale=1.0 / (X_S * GRAM_S * NB), scalar=0.0, op0=ALU.mult,
                                                   op1=ALU.add, accum_out=nn2[:, i, m:m + 1])
                ins.then_inc(q4["nn"], 1)
                if not first_step(c):
                    lo_queries(c - 1, 1 - i)
                if more or i == 0:
                    lo_rows(c + 1, 1 - i)
            add_up(0, 0, 0)
            norm_x1(0, 0)
            add_up(1, 1, 0)
            lo_rows(0, 0)
            dve.wait_ge(vb_hi, 1)
            low(vb[1], st_vb, K_S, vb[0], vb_lo)
            dve.wait_ge(gram_hi, 1)
            low(gram[1][:, :, :], a_bank[0][:, :].rearrange("p (k c) -> p k c", k=KC), GRAM_S / (K_S * K_S),
                gram[0][:, :, :], gram_lo)
            by(dve, NCH, 2, second_block, head=2)
            lo_queries(NCH - 1, 1)

            def evac_ffn(m, c, i):
                for h in range(2):
                    ins = dve.scalar_tensor_tensor(out=fbuf[i][:, 2 * h:2 * h + 2, :], in0=half(h, i),
                                                   scalar=1.0 / GE_S, in1=two(b2_b), op0=ALU.mult, op1=ALU.add)
                ins.then_inc(m.evac_read, 1)
                dve.wait_ge(m.evac_read, at(m.ch(c)))
                dve.sem_inc(m.evac_done, 1)
            gate(dve, end_q4)
            mix(ff_mix, evac_ffn)
            gate(dve, end_mix(ff_mix))

            def silu2(c, i, g):
                dve.wait_ge(bk_tanh, at(c))
                dve.wait_ge(bk_ld[i], 32 * g + 32)
                dve.scalar_tensor_tensor(out=gl[i], in0=tbuf[i], scalar=1.0, in1=gl[i], op0=ALU.add, op1=ALU.mult
                                         ).then_inc(bk_silu, 1)

            def evac_bank(m, c, i):
                dve.wait_ge(bk_silu, at(c))
                for h in range(2):
                    ins = dve.scalar_tensor_tensor(out=gl[i][:, 2 * h:2 * h + 2, :], in0=half(h, i),
                                                   scalar=0.5 / (GE_S * K_S), in1=gl[i][:, 2 * h:2 * h + 2, :],
                                                   op0=ALU.mult, op1=ALU.mult)
                ins.then_inc(m.evac_read, 1)
                dve.wait_ge(m.evac_read, at(m.ch(c)))
                dve.tensor_tensor(fbuf[i], gl[i], xl[i], ALU.add).then_inc(m.evac_done, 1)
            mix(bk_mix, evac_bank, silu2)


_INS = ["L0_attn_x", "L0_attn_Wq", "L0_attn_bq", "L0_attn_Wk", "L0_attn_bk", "L0_attn_Wv", "L0_attn_bv",
        "L0_attn_Wo", "L0_attn_bo", "L0_attn_layerscale", "L0_ffn_router_weight", "L0_ffn_e_bias",
        "L0_ffn_gate_w", "L0_ffn_up_w", "L0_ffn_down_w", "L0_ffn_sh_gate_w", "L0_ffn_sh_up_w",
        "L0_ffn_sh_down_w", "L1_attn_k", "L1_attn_v", "L1_ffn_W1", "L1_ffn_b1", "L1_ffn_W2", "L1_ffn_b2"]


def kernel(**inputs):
    import numpy as _np
    import concourse.bacc as _bacc
    from concourse import mybir as _mybir
    from concourse.bass_utils import run_bass_kernel_spmd as _run

    nc = _bacc.Bacc("TRN2", target_bir_lowering=False, num_devices=1)
    arrays, args = {}, {}
    for name in _INS:
        v = _np.ascontiguousarray(inputs[name])
        arrays[f"in_{name}_dram"] = v
        args[name] = nc.dram_tensor(f"in_{name}_dram", v.shape, _mybir.dt.from_np(v.dtype), kind="ExternalInput").ap()
    result = nc.dram_tensor("out_0_dram", (B, S, D), F32, kind="ExternalOutput").ap()
    build(nc, args, result)
    r = _run(nc, [arrays], core_ids=[0])
    return r.results[0]["out_0_dram"]
```

```python
from contextlib import ExitStack
import math

import concourse.bass as bass
from concourse import mybir

P = 128
D = 256
KC = D // P
B, S = 2, 2048
T = B * S
TT = T // P
G4 = 4
NCH = TT // G4
CW = G4 * P
E = 16
TOPK, GROUPS, GTOP = 4, 4, 2
ROUTE_SCALE = 2.5
EPG = E // GROUPS
NE = E + 2
IM = 128
NSLOT_T = TOPK * T // P + E
NSLOT = NSLOT_T * P
ROUND = 12582912.0
NB = 2048
FF = 1024
EPS = 1e-5

F32 = mybir.dt.float32
F16 = mybir.dt.float16
I32 = mybir.dt.int32
ALU = mybir.AluOpType
ACT = mybir.ActivationFunctionType
AXX = mybir.AxisListType.X

X_S = 64.0
WQK_S = 16.0
WO_S = 64.0
WP_S = 4.0
V_S = 0.25
ATT_S = 2.0 ** 14
H_S = 0.25
K_S = 1024.0
GRAM_S = 64.0
QS_S = 16.0
GE_S = 64.0
QK_PS = X_S * WQK_S
VP_PS = X_S * WP_S


def build(nc, a, out):
    with ExitStack() as ctx:
        def sb(name, shape, dt=F32):
            return ctx.enter_context(nc.sbuf_tensor(name, shape, dt))

        def sem(name):
            return ctx.enter_context(nc.semaphore(name))

        def dram(name, shape, dt=F32):
            return nc.dram_tensor(name, shape, dt, kind="Internal").ap()

        s0_d = dram("s0_d", [T, D])
        xn_d = dram("xn_d", [T, D])
        xg_d = dram("xg_d", [NSLOT, D])
        yg_d = dram("yg_d", [NSLOT, D])
        sh_d = dram("sh_d", [T, D])
        moe_d = dram("moe_d", [T, D])
        x1_d = dram("x1_d", [T, D])
        f_d = dram("f_d", [T, D])
        sums_d = dram("sums_d", [P, 2])

        def chunks(ap):
            return ap.rearrange("(n m p) d -> n p m d", m=G4, p=P)

        x_rows = a["L0_attn_x"].rearrange("b s d -> (b s) d")
        x_c, s0_c, xn_c, moe_c, x1_c, f_c = (chunks(v) for v in (x_rows, s0_d, xn_d, moe_d, x1_d, f_d))
        out_c = chunks(out.rearrange("b s d -> (b s) d"))
        xn_t, sh_t, moe_t = (v.rearrange("(n p) d -> n p d", p=P) for v in (xn_d, sh_d, moe_d))
        xg_p, yg_p = (v.rearrange("(n m p) d -> n p m d", m=2, p=P) for v in (xg_d, yg_d))

        reg_x = sb("reg_x", [P, 8192])
        reg_qk = sb("reg_qk", [P, 8192])
        reg_v = sb("reg_v", [P, 4096])
        reg_e = sb("reg_e", [P, NE * 512 + NE * D])
        reg_w = sb("reg_w", [P, 3072])

        def f16(r, lo, n):
            return r[:, lo:lo + n].bitcast(F16)

        xT = [f16(reg_x, h * 4096, 4096).rearrange("p (k t) -> p k t", k=KC) for h in range(2)]
        qkT = [f16(reg_qk, h * 4096, 4096).rearrange("p (k t) -> p k t", k=2 * KC) for h in range(2)]
        qsT = [f16(reg_qk, h * 4096, 4096).rearrange("p (k t) -> p k t", k=KC) for h in range(2)]
        vp = [f16(reg_v, h * 2048, 2048).rearrange("p (t e) -> p t e", e=D) for h in range(2)]
        vb = vp
        gu = [f16(reg_e, h * NE * 256, NE * 256).rearrange("p (e k c) -> p e k c", k=KC, c=D) for h in range(2)]
        dn = [f16(reg_e, NE * 512 + h * NE * 128, NE * 128).rearrange("p (e h) -> p e h", h=D) for h in range(2)]

        wqkT = [sb(f"wqkT{h}", [P, KC, 2 * D], F16) for h in range(2)]
        woT = [sb(f"woT{h}", [P, KC, D], F16) for h in range(2)]
        wv = [sb(f"wv{h}", [P, KC, D], F16) for h in range(2)]
        wpT = [sb(f"wpT{h}", [P, KC, D], F16) for h in range(2)]
        kbT = [sb(f"kbT{h}", [P, KC, NB], F16) for h in range(2)]
        gram = [sb(f"gram{h}", [P, KC, D], F16) for h in range(2)]
        w1T = sb("w1T", [P, KC, FF], F16)
        w2T = sb("w2T", [P, FF // P, D], F16)
        rwT = [sb(f"rwT{h}", [P, KC, E], F16) for h in range(2)]
        bvf = sb("bvf", [P, KC])
        bvc = [sb(f"bvc{h}", [P, KC, 33], F16) for h in range(2)]
        bias3 = sb("bias3", [33, 3 * D])
        biasz = sb("biasz", [33, 3 * D], F16)
        ones33 = sb("ones33", [33, P], F16)
        onesf = sb("onesf", [P, P])
        ident = sb("ident", [P, P])
        b1c = sb("b1c", [P, FF // P])
        bo_b = sb("bo_b", [P, D])
        ls_b = sb("ls_b", [P, D])
        b2_b = sb("b2_b", [P, D])
        eb_b = sb("eb_b", [P, E])
        nlogs = sb("nlogs", [P, 1])
        mhalf = sb("mhalf", [P, G4])
        thr = sb("thr", [P, 8])
        slot_i = sb("slot_i", [P, TOPK, TT], I32)
        w4 = sb("w4", [P, TOPK, TT])
        expert_of = sb("expert_of", [1, NSLOT_T], I32)
        before_h = sb("before_h", [P, P], F16)
        ones_h = sb("ones_h", [P, P], F16)
        sel_h = sb("sel_h", [P, TT * E], F16)
        tile_no = sb("tile_no", [1, NSLOT_T], I32)
        xr = sb("xr", [P, 4, D])
        icol = sb("icol", [P, 4, TOPK], I32)

        xin = sb("xin", [P, 2, G4, D])
        stat = sb("stat", [P, 2, G4, 6])
        mv = sb("mv", [P, 2, G4, 2])
        ve = sb("ve", [P, 2, G4])
        rstd = sb("rstd", [P, 2, G4])
        nmr = sb("nmr", [P, 2, G4])
        nn2 = sb("nn2", [P, 2, G4])
        rn2 = sb("rn2", [P, 2, G4])
        att = reg_w[:, 0:1024].rearrange("p (r c) -> p r c", c=CW)
        ah = f16(reg_w, 1024, 1024).rearrange("p (r c) -> p r c", c=CW)
        al = f16(reg_w, 2048, 1024).rearrange("p (r c) -> p r c", c=CW)
        xn = reg_w[:, 0:2048].rearrange("p (b m d) -> p b m d", b=2, d=D)
        def inner_buffers(reg):
            return ([reg[:, 512 * i:512 * (i + 1)].rearrange("p (r c) -> p r c", c=D) for i in range(3)] +
                    [[f16(reg, 1536 + 256 * h, 256).rearrange("p (r c) -> p r c", c=D) for h in range(2)]])
        ex_buf, sh_buf = inner_buffers(reg_w), inner_buffers(reg_v)
        xgT = [f16(reg_w, 2048 + 512 * h, 512).rearrange("p (r k c) -> p r k c", r=2, k=KC) for h in range(2)]
        xs = xin[:, :, :, :].rearrange("p a (b m) d -> p (a b) m d", m=2)
        sres = reg_v[:, 2048:2560].rearrange("p (r d) -> p r d", d=D)
        yres = reg_qk[:, 0:1024].rearrange("p (r m d) -> p r m d", r=2, d=D)
        yg = reg_e[:, 6144:8704].rearrange("p (r k d) -> p r k d", r=2, d=D)
        cres = reg_e[:, 8704:9216].rearrange("p (r d) -> p r d", d=D)
        sgc = reg_e[:, 4096:4608].rearrange("p (r d) -> p r d", d=D)
        qkn = reg_w[:, 0:1024].rearrange("p (r c) -> p r c", c=2 * D)
        buf_e = [reg_e[:, i * 1024:(i + 1) * 1024].rearrange("p (m d) -> p m d", d=D) for i in range(8)]
        sin, gin, qsb = buf_e[0:2], buf_e[2:4], buf_e[6:8]
        fbuf, tbuf, gl, xl = buf_e[0:2], buf_e[2:4], buf_e[4:6], buf_e[6:8]
        junk = reg_e[:, 8192:8192 + G4 * D].rearrange("p (m d) -> p m d", d=D)
        st_vb = reg_e[:, 9216:9216 + 4096].rearrange("p (n d) -> p n d", d=D)

        scores, biased, masked, erank = (reg_w[:, 512 * i:512 * (i + 1)] for i in range(4))
        pair_s = reg_w[:, 2048:2816].rearrange("p (n q) -> p n q", q=6)
        xin_f = xin[:, :, :, :].rearrange("p a b c -> p (a b c)")
        gs, grank, gsel = (xin_f[:, 128 * i:128 * (i + 1)] for i in range(3))
        esum = xin_f[:, 384:448]
        gbeat = xin_f[:, 512:1024].rearrange("p (t x) -> p t x", x=GROUPS * GROUPS)
        ebeat = reg_qk[:, :].rearrange("p (t x) -> p t x", x=E * E)
        cnt = [reg_qk[:, 512 * i:512 * (i + 1)].rearrange("p (t e) -> p t e", e=E) for i in range(3)]
        picks = [reg_qk[:, 2048 + 2048 * i:4096 + 2048 * i].rearrange("p (k t e) -> p k t e", k=TOPK, e=E)
                 for i in range(2)]
        slot_f = reg_qk[:, 6144:6272]
        small = [reg_qk[:, 6272 + 16 * i:6288 + 16 * i] for i in range(8)]
        upto = reg_qk[0:1, 2048:2048 + NSLOT_T * E].rearrange("p (j e) -> p j e", e=E)
        tile_f = reg_qk[0:1, 6400:6400 + NSLOT_T]
        exp_f = reg_qk[0:1, 6560:6560 + NSLOT_T]

        bank = [ctx.enter_context(nc.psum_tensor(f"bank{i}", [P, 512], F32)) for i in range(8)]
        s_bank, a_bank = bank[:4], bank[4:]

        st_gate = reg_qk[:, 0:4096].rearrange("p (e d) -> p e d", d=D)
        st_up = reg_qk[:, 4096:8192].rearrange("p (e d) -> p e d", d=D)
        st_down = reg_v[:, :].rearrange("p (t e i) -> p t e i", t=KC, e=E)
        st_sg = reg_x[:, 0:512].rearrange("p (t d) -> p t d", d=D)
        st_su = reg_x[:, 512:1024].rearrange("p (t d) -> p t d", d=D)
        st_sd = reg_x[:, 1024:1536].rearrange("p (t i) -> p t i", i=D)
        st_wq, st_wk, st_wv, st_wo = (reg_x[:, 1536 + 512 * i:2048 + 512 * i].rearrange("p (t d) -> p t d", d=D)
                                      for i in range(4))
        st_rw = reg_x[0:E, 3584:3840]
        st_k = reg_v[:, :].rearrange("p (n d) -> p n d", d=D)
        KN = NB // P // 2
        kn = [[f16(reg_x, h * 4096 + k * 2048, 1024).rearrange("p (n d) -> p n d", d=D) for k in range(KC)]
              for h in range(2)]
        st_w = [reg_qk[:, 1024:3072], reg_qk[:, 3072:5120]]
        below = reg_qk[:, 5120:7168]
        w_sums = reg_qk[:, 7168:7168 + 2 * P].rearrange("p (q n) -> p q n", n=2)

        def rows(ap):
            return ap.rearrange("(t p) d -> p t d", p=P)

        def row1(ap):
            return ap.rearrange("(o d) -> o d", o=1)

        def spread(ap, axis, n):
            shape = list(ap.shape)
            shape[axis] = n
            return ap.broadcast_to(shape)

        def one(ap, n):
            return ap[bass.ds(n, 1)].rearrange("o p m d -> p (o m) d")

        COUNTS_AT = 14

        def first_step(c):
            return isinstance(c, int) and c == 0

        def by(eng, n, m, body, head=0, pauses={}):
            for c in range(head):
                body(c, c % m, c // m, True)
            cuts = [head] + [c for c in pauses if c < n - m] + [n - m]
            for lo, hi in zip(cuts, cuts[1:]):
                if lo in pauses:
                    pauses[lo]()
                if hi > lo:
                    with eng.Fori(lo // m, hi // m) as g:
                        for i in range(m):
                            body(m * g + i, i, g, True)
            if n - m in pauses:
                pauses[n - m]()
            for i in range(m):
                body(n - m + i, i, n // m - 1, False)

        CR = 4

        def at(k):
            return k + 1 + CR

        def open_(eng, *sems):
            for q in sems:
                eng.sem_inc(q, CR)

        def gate(eng, waits):
            for q, count in waits:
                eng.wait_ge(q, count)

        ld = {n: sem("ld_" + n) for n in ("qk", "o_v", "gate_up", "down", "sh", "bank", "w12", "small", "vb")}
        ident_zero = sem("ident_zero")
        ready_id = sem("ready_id")
        consts = sem("consts")
        w_turned = sem("w_turned")
        w_hi = sem("w_hi")
        w_lo = sem("w_lo")
        nat_hi = sem("nat_hi")
        nat_lo = sem("nat_lo")
        ex = {n: sem("ex_" + n) for n in ("turned", "hi", "lo")}
        kn_step = sem("kn_step")
        wp_mm, wp_hi, wp_lo = sem("wp_mm"), sem("wp_hi"), sem("wp_lo")
        bias_step = sem("bias_step")
        gram_mm, gram_hi, gram_lo = sem("gram_mm"), sem("gram_hi"), sem("gram_lo")
        tn_step, tn_sum, tn_dma, tn_made = sem("tn_step"), sem("tn_sum"), sem("tn_dma"), sem("tn_made")
        rw_mm, rw_hi, rw_lo = sem("rw_mm"), sem("rw_hi"), sem("rw_lo")

        jobs = []

        def job(need, blocks, hi, lo, scale):
            jobs.append((need, blocks, hi, lo, scale))

        def blk(x3, t, k):
            return x3[:, t, k * P:(k + 1) * P]

        for n, w in enumerate((st_wq, st_wk)):
            job(("qk",), [blk(w, r, k) for k in range(KC) for r in range(KC)],
                wqkT[0][:, :, n * D:(n + 1) * D], wqkT[1][:, :, n * D:(n + 1) * D], WQK_S)
        job(("o_v",), [blk(st_wo, r, k) for k in range(KC) for r in range(KC)],
            woT[0][:, :, :], woT[1][:, :, :], WO_S)
        WO_JOBS = len(jobs)
        for e in range(2):
            job(("sh",), [blk(w, e, k) for k in range(KC) for w in (st_sg, st_su)],
                gu[0][:, E + e, :, :], gu[1][:, E + e, :, :], WQK_S)
        job(("sh",), [st_sd[:, t, x * P:(x + 1) * P] for x in range(2) for t in range(KC)],
            dn[0][:, E:NE, :], dn[1][:, E:NE, :], WQK_S)

        def ex_job(c, n):
            def e1(ap, e):
                return ap[:, bass.ds(e, 1)]
            if n < 2:
                return ([e1(w, 2 * c + n)[:, 0, k * P:(k + 1) * P] for k in range(KC) for w in (st_gate, st_up)],
                        [gu[h][:, bass.ds(2 * c + n, 1), :, :].rearrange("p o k c -> p (o k) c") for h in range(2)])
            return ([st_down[:, t, bass.ds(2 * c + x, 1), :].rearrange("p o i -> p (o i)")
                     for x in range(2) for t in range(KC)],
                    [dn[h][:, bass.ds(2 * c, 2), :] for h in range(2)])

        late_jobs = []
        for n in range(0, NB // P, 2):
            late_jobs.append(([blk(st_k, n + r, k) for k in range(KC) for r in range(2)],
                              kbT[0][:, :, n * P:(n + 2) * P], kbT[1][:, :, n * P:(n + 2) * P], 1.0))
        LATE_LO = len(late_jobs)
        tern1 = st_w[0].rearrange("p (n d) -> p n d", d=D)
        tern2 = st_w[1].rearrange("p (t f) -> p t f", f=FF)
        for n in range(0, FF // P, 2):
            late_jobs.append(([blk(tern1, n + r, k) for k in range(KC) for r in range(2)],
                              w1T[:, :, n * P:(n + 2) * P], None, 1.0))
        for n in range(0, FF // P, 2):
            late_jobs.append(([tern2[:, t, (n + r) * P:(n + r + 1) * P] for r in range(2) for t in range(KC)],
                              w2T[:, n:n + 2, :], None, 1.0))

        def job_ps(j):
            return bank[j % 8][:, :].rearrange("p (k c) -> p k c", k=2)

        bvt = sb("bvt", [P, KC, 33])
        bv_step = sem("bv_step")
        x_ld = [sem(f"x_ld{i}") for i in range(2)]
        ln = {n: sem("ln_" + n) for n in ("mv", "ve", "rs", "nmr", "xn", "mm", "hi", "lo")}
        rt_mm, rt_sig, rt_step, rt_done = sem("rt_mm"), sem("rt_sig"), sem("rt_step"), sem("rt_done")
        pj = {n: sem(f"pj_{n}") for n in ("mm", "mv", "ve", "rs", "nmr", "qkn", "vhi", "vlo", "tr", "thi", "tlo")}
        steps = ("xt", "xh", "xl", "gu", "sig", "t1", "h", "tr", "hi", "lo", "dn", "ev")
        shx = {n: sem("shx_" + n) for n in steps[3:]}
        rex = {n: sem("rex_" + n) for n in steps}
        shared = (shx, sh_buf, bank[2:4])
        routed = (rex, ex_buf, bank[6:])
        shx_st = [sem(f"shx_st{i}") for i in range(2)]
        rex_st = [sem(f"rex_st{i}") for i in range(2)]
        rex_ld = [sem(f"rex_ld{i}") for i in range(4)]
        xn_st = [sem(f"xn_st{i}") for i in range(2)]
        zero_st = sem("zero_st")
        xr_ld = [sem(f"xr_ld{i}") for i in range(4)]
        xr_st = [sem(f"xr_st{i}") for i in range(4)]
        sh_ld = [sem(f"sh_ld{i}") for i in range(2)]
        y_ld = [sem(f"y_ld{i}") for i in range(2)]
        cb_step, cb_sig, cb_done = sem("cb_step"), sem("cb_sig"), sem("cb_done")
        cb_st = [sem(f"cb_st{i}") for i in range(2)]
        pool_col = sem("pool_col")
        pool_turn = sem("pool_turn")
        rt_sel, rt_cnt = sem("rt_sel"), sem("rt_cnt")
        q4 = {n: sem("q4_" + n) for n in ("m2", "x1", "mv", "ve", "rs", "nmr", "xn", "t1", "h1", "l1",
                                         "gm", "nn", "rn", "qs", "t2", "h2", "l2")}
        g_ld = [sem(f"g_ld{i}") for i in range(2)]
        q4_ld = [sem(f"q4_ld{i}") for i in range(2)]
        q4_st = [sem(f"q4_st{i}") for i in range(2)]
        vb_hi, vb_lo = sem("vb_hi"), sem("vb_lo")
        bk_ld = [sem(f"bk_ld{i}") for i in range(2)]

        mixes = []
        mx_first, mx_act, mx_hi, mx_lo, mx_second, mx_read, mx_evac = (
            sem("mx_" + n) for n in ("first", "act", "hi", "lo", "second", "read", "evac"))
        mx_st = [[sem(f"mx_st{n}{i}") for i in range(2)] for n in ("a", "f")]

        class Mix:
            def __init__(self, nch, nt, stat, mov, pass1, second, pass2, func, scale, bias, split):
                self.nch, self.nt = nch, nt
                self.stat, self.mov, self.pass1 = stat, mov, pass1
                self.second, self.pass2 = second, pass2
                self.func, self.scale, self.bias, self.split = func, scale, bias, split
                self.k0 = sum(m.nch * m.nt for m in mixes)
                self.c0 = sum(m.nch for m in mixes)
                self.first_done = mx_first
                self.act_done = mx_act
                self.hi_done = mx_hi
                self.lo_done = mx_lo
                self.second_done = mx_second
                self.evac_read = mx_read
                self.evac_done = mx_evac
                self.stored = mx_st[0 if func == ACT.Sigmoid else 1]
                self.s0 = sum(m.nch // 2 for m in mixes if m.stored is self.stored)
                mixes.append(self)

            def step(self, c, j):
                return self.k0 + c * self.nt + j

            def ch(self, c):
                return self.c0 + c

            def st(self, g):
                return 16 * (self.s0 + g) + 16

        THREE = ((0, 0), (1, 0), (0, 1))
        at_mix = [Mix(S // CW, S // P,
                      lambda part, k, j: qkT[part][:, KC + k, j * P:(j + 1) * P],
                      lambda part, k, c: qkT[part][:, k, bass.ds(c * CW, CW)],
                      THREE, lambda part, j: vp[part][:, j, :], THREE,
                      ACT.Sigmoid, 1.0 / (X_S * X_S * math.sqrt(D)), lambda j: nlogs[:, 0:1], ATT_S)
                  for b in range(B)]
        ff_mix = Mix(NCH, FF // P,
                     lambda part, k, j: w1T[:, k, j * P:(j + 1) * P],
                     lambda part, k, c: xT[part][:, k, bass.ds(c * CW, CW)],
                     ((0, 0), (0, 1)), lambda part, j: w2T[:, j, :], ((0, 0), (1, 0)),
                     ACT.Gelu, 1.0 / X_S, lambda j: b1c[:, j:j + 1], GE_S)
        bk_mix = Mix(NCH, NB // P,
                     lambda part, k, j: kbT[part][:, k, j * P:(j + 1) * P],
                     lambda part, k, c: qsT[part][:, k, bass.ds(c * CW, CW)],
                     THREE, lambda part, j: vb[part][:, j, :], THREE,
                     ACT.Gelu, 1.0 / (QS_S * K_S), None, GE_S)
        bk_tanh, bk_silu = sem("bk_tanh"), sem("bk_silu")

        block = ctx.enter_context(nc.Block())

        end_w = [(w_hi, len(jobs)), (w_lo, len(jobs)), (wp_lo, 1), (rw_lo, 1), (bias_step, 4)]
        end_x = [(ln["lo"], at(2 * NCH - 1))] + [(q, 16 * (NCH // 2) + 16) for q in xn_st] + \
            [(ex["lo"], at(3 * NCH - 1)), (ex["hi"], at(3 * NCH - 1))]
        end_pj = [[(pj[n], at((b + 1) * (S // P) - 1)) for n in ("tlo", "vlo")] for b in range(B)]
        end_sc = [(q, 16 * TT) for q in xr_st]
        end_sh = [(shx["ev"], at(TT - 1))] + [(q, 16 * (TT // 2) + 16) for q in shx_st]
        end_rt = [(rt_done, 1)] + end_sh
        end_mo = [(rex["ev"], at(NSLOT_T // 2 - 1))] + [(q, 16 * (NSLOT_T // 4) + 16) for q in rex_st]
        end_late = [(w_hi, len(jobs) + len(late_jobs)), (w_lo, len(jobs) + LATE_LO), (kn_step, 3 * KC)]
        end_q4 = [(q4["l2"], at(2 * NCH - 1))]
        VB_N = NB // P // NCH

        def end_mix(m):
            return [(m.evac_done, at(m.ch(m.nch - 1)))] + [(q, m.st(m.nch // 2)) for q in m.stored]

        @block.sync
        def _(sp):
            def load(dst, src, name, **how):
                sp.dma_start(dst, src, **how).then_inc(ld[name], 16)

            for q in shx_st + rex_st + xn_st + cb_st + [q for m in mx_st for q in m]:
                sp.sem_inc(q, 16)
            load(st_wq, rows(a["L0_attn_Wq"]), "qk")
            load(st_wk, rows(a["L0_attn_Wk"]), "qk")
            load(st_wo, rows(a["L0_attn_Wo"]), "o_v")
            load(st_wv, rows(a["L0_attn_Wv"]), "o_v")
            load(st_sg, rows(a["L0_ffn_sh_gate_w"]), "sh")
            load(st_su, rows(a["L0_ffn_sh_up_w"]), "sh")
            load(st_sd, rows(a["L0_ffn_sh_down_w"]), "sh")
            load(st_rw, a["L0_ffn_router_weight"], "sh")
            for i in range(2):
                sp.dma_start(xin[:, i, :, :], x_c[i]).then_inc(x_ld[i], 16)
            sp.wait_ge(consts, 1)
            for n, name in enumerate(("L0_attn_bq", "L0_attn_bk")):
                for r in (0, 32):
                    load(bias3[r:r + 1, n * D:(n + 1) * D], row1(a[name]), "small")
            for dst, name in ((bo_b, "L0_attn_bo"), (ls_b, "L0_attn_layerscale"), (b2_b, "L1_ffn_b2"),
                              (eb_b, "L0_ffn_e_bias")):
                load(dst[:, :], spread(row1(a[name]), 0, P), "small")
            load(bvf[:, :], a["L0_attn_bv"].rearrange("(t p) -> p t", p=P), "small", allow_slow_non_contiguous=True)
            load(b1c[:, :], a["L1_ffn_b1"].rearrange("(t p) -> p t", p=P), "small", allow_slow_non_contiguous=True)
            load(st_gate, a["L0_ffn_gate_w"].rearrange("e i d -> i e d"), "gate_up")
            load(st_up, a["L0_ffn_up_w"].rearrange("e i d -> i e d"), "gate_up")
            for t in range(KC):
                load(st_down[:, t, :, :], a["L0_ffn_down_w"][:, t * P:(t + 1) * P, :].rearrange("e h i -> h e i"),
                     "down")

            def next_x(c, i, g, more):
                sp.wait_ge(ln["xn"], at(c))
                if more:
                    sp.dma_start(xin[:, i, :, :], one(x_c, c + 2)).then_inc(x_ld[i], 16)
                sp.dma_start(one(xn_c, c), xn[:, i, :, :]).then_inc(xn_st[i], 16)
            by(sp, NCH, 2, next_x)

            def store_shared(c, i, g, more):
                sp.wait_ge(shx["ev"], at(c))
                sp.dma_start(sh_t[bass.ds(c, 1)].rearrange("o p d -> p (o d)"), sres[:, i, :]
                             ).then_inc(shx_st[i], 16)
            by(sp, TT, 2, store_shared)

            for n in range(0, NSLOT_T, 16):
                sp.dma_start(xg_d[n * P:(n + 16) * P, :].rearrange("(n p) d -> p n d", p=P),
                             spread(xr[:, 0, :].rearrange("p (o d) -> p o d", o=1), 1, 16)).then_inc(zero_st, 16)
            for i in range(2):
                sp.wait_ge(xn_st[i], 16 * (NCH // 2) + 16)
            sp.wait_ge(zero_st, 16 * (NSLOT_T // 16))

            def load_xr(c, i, g, more):
                if not first_step(g):
                    sp.wait_ge(xr_st[i], 16 * TOPK * g)
                sp.dma_start(xr[:, i, :], xn_t[bass.ds(c, 1)].rearrange("o p d -> p (o d)")).then_inc(xr_ld[i], 16)
            by(sp, TT, 4, load_xr, head=4)

            gate(sp, end_sc)

            def load_slots(c, r):
                sp.dma_start(xs[:, r, :, :], one(xg_p, c)).then_inc(rex_ld[r], 16)

            def next_slots(c, r):
                sp.wait_ge(rex["xt"], at(c - 4))
                load_slots(c, r)
            for c in range(4):
                if c % 2 == 0:
                    sp.wait_ge(at_mix[0].stored[c // 2], at_mix[0].st(S // CW // 2))
                load_slots(c, c)
            gate(sp, end_mix(at_mix[0]))
            for c in range(4, 7):
                next_slots(c, c - 4)
            load(st_w[0].rearrange("p (n d) -> p n d", d=D), rows(a["L1_ffn_W1"]), "w12")
            load(st_w[1].rearrange("p (t f) -> p t f", f=FF), rows(a["L1_ffn_W2"]), "w12")
            load(st_k, rows(a["L1_attn_k"]), "bank")

            def slots(c, i, g, more):
                if more or i == 0:
                    next_slots(c + 7, (i + 3) % 4)
                sp.wait_ge(rex["ev"], at(c))
                sp.dma_start(one(yg_p, c), yres[:, i % 2, :, :]).then_inc(rex_st[i % 2], 16)
            by(sp, NSLOT_T // 2, 8, slots)
            gate(sp, end_mo)

            sp.dma_start(st_vb, rows(a["L1_attn_v"])).then_inc(ld["vb"], 16)

            def load_shared(c, i):
                sp.dma_start(yg[:, i, TOPK, :], sh_t[bass.ds(c, 1)].rearrange("o p d -> p (o d)")
                             ).then_inc(sh_ld[i], 16)
            load_shared(0, 0)
            load_shared(1, 1)

            def load_parts(n, i):
                sp.dma_start(gin[i], one(moe_c, n)).then_inc(g_ld[i], 16)
                sp.dma_start(sin[i], one(s0_c, n)).then_inc(g_ld[i], 16)

            def load_x(n, i):
                sp.dma_start(xin[:, i, :, :], one(x_c, n)).then_inc(q4_ld[i], 16)
            def first_parts():
                for i in range(2):
                    sp.wait_ge(cb_st[i], 16 * G4 + 16)
                for i in range(2):
                    load_parts(i, i)

            def first_x(i):
                sp.wait_ge(at_mix[1].stored[i], at_mix[1].st(S // CW // 2))
                load_x(i, i)

            def combined(c, i, g, more):
                sp.wait_ge(cb_done, at(c))
                sp.dma_start(moe_t[bass.ds(c, 1)].rearrange("o p d -> p (o d)"), cres[:, i, :]
                             ).then_inc(cb_st[i], 16)
                if more:
                    load_shared(c + 2, i)
            by(sp, TT, 2, combined, pauses={TT - 8: first_parts, TT - 2: lambda: first_x(0)})
            first_x(1)
            for i in range(2):
                sp.wait_ge(cb_st[i], 16 * (TT // 2) + 16)
            gate(sp, end_mix(at_mix[1]))

            def store_mix(m, dst_c, base, res):
                def store(c, i, g, more):
                    sp.wait_ge(m.evac_done, at(m.ch(c)))
                    sp.dma_start(one(dst_c, base + c), res(i)).then_inc(m.stored[i], 16)
                return store

            def x1_out(c, i, g, more):
                sp.wait_ge(q4["x1"], at(c))
                sp.dma_start(one(x1_c, c), xin[:, i, :, :]).then_inc(q4_st[i], 16)
                if more:
                    load_parts(c + 2, i)
                    sp.wait_ge(q4["xn"], at(c))
                    sp.wait_ge(q4_st[i], 16 * g + 16)
                    load_x(c + 2, i)
            by(sp, NCH, 2, x1_out)
            for i in range(2):
                sp.wait_ge(q4_st[i], 16 * (NCH // 2))

            by(sp, NCH, 2, store_mix(ff_mix, f_c, 0, lambda i: fbuf[i]))
            gate(sp, end_mix(ff_mix))

            def load2(n, i):
                sp.dma_start(gl[i], one(f_c, n)).then_inc(bk_ld[i], 16)
                sp.dma_start(xl[i], one(x1_c, n)).then_inc(bk_ld[i], 16)
            load2(0, 0)
            load2(1, 1)
            final = store_mix(bk_mix, out_c, 0, lambda i: fbuf[i])

            def out_rows(c, i, g, more):
                final(c, i, g, more)
                if more:
                    load2(c + 2, i)
            by(sp, NCH, 2, out_rows)
            gate(sp, end_mix(bk_mix))

        @block.gpsimd
        def _(pool):
            pool.memset(ident[:, :], 0.0).then_inc(ident_zero, 1)
            pool.wait_ge(ident_zero, 1)
            pool.affine_select(out=ident[:, :], in_=ident[:, :], compare_op=ALU.not_equal, fill=1.0, base=0,
                               pattern=[[-1, P]], channel_multiplier=1).then_inc(ready_id, 1)
            pool.memset(mhalf[:, :], -0.5).then_inc(ready_id, 1)
            pool.memset(before_h[:, :], 1.0).then_inc(ident_zero, 1)
            pool.wait_ge(ident_zero, 2)
            pool.affine_select(out=before_h[:, :], in_=before_h[:, :], compare_op=ALU.is_ge, fill=0.0, base=-1,
                               pattern=[[1, P]], channel_multiplier=-1).then_inc(ready_id, 1)
            pool.memset(ones_h[:, :], 1.0).then_inc(ready_id, 1)
            pool.iota(tile_no[:, :], pattern=[[1, NSLOT_T]], base=0, channel_multiplier=0).then_inc(ready_id, 1)
            pool.wait_ge(ready_id, 5)
            open_(pool, ln["rs"], q4["m2"], q4["rs"], q4["rn"], pj["rs"])

            def ln_rows(c, i, g, more):
                pool.wait_ge(ln["ve"], at(c))
                pool.wait_ge(ln["xn"], at(c - 2))
                pool.tensor_tensor(rstd[:, i, :], ve[:, i, :], mhalf[:, :], ALU.pow).then_inc(ln["rs"], 1)
            by(pool, NCH, 2, ln_rows)

            def column(t, r):
                pool.tensor_copy(icol[:, r, :], slot_i[:, :, bass.ds(t, 1)].rearrange("p k o -> p (k o)")
                                 ).then_inc(pool_col, 1)

            def slots_of(r, k):
                return bass.IndirectOffsetOnAxis(ap=icol[:, r, k:k + 1], axis=0)

            def scatter(c, i, g, more):
                if not first_step(g):
                    pool.wait_ge(xr_st[i], 16 * TOPK * g)
                    pool.sem_inc(pool_turn, 1)
                column(c, i)
                pool.wait_ge(xr_ld[i], 16 * g + 16)
                pool.sem_inc(pool_turn, 1)
                pool.wait_ge(pool_col, c + 1)
                pool.sem_inc(pool_turn, 1)
                for k in range(TOPK):
                    pool.indirect_dma_start(out=xg_d, out_offset=slots_of(i, k), in_=xr[:, i, :], in_offset=None
                                            ).then_inc(xr_st[i], 16)

            def gather(c, i, g):
                if not (isinstance(c, int) and c < 2):
                    pool.wait_ge(cb_step, TOPK * (c - 1) + CR)
                    pool.sem_inc(pool_turn, 1)
                column(c, i)
                pool.wait_ge(pool_col, TT + c + 1)
                pool.sem_inc(pool_turn, 1)
                for k in range(TOPK):
                    pool.indirect_dma_start(out=yg[:, i, k, :], out_offset=None, in_=yg_d, in_offset=slots_of(i, k)
                                            ).then_inc(y_ld[i], 16)

            def second_round():
                gate(pool, end_mix(at_mix[0]))
                pool.wait_ge(tn_sum, 2)
                pool.dma_start(sums_d, thr[:, 0:2]).then_inc(tn_dma, 16)
                pool.wait_ge(tn_dma, 16)
                pool.dma_start(w_sums, spread(sums_d.rearrange("(o q) n -> o q n", o=1), 0, P)
                               ).then_inc(tn_dma, 16)
                pool.wait_ge(ld["bank"], 16)
                for k in range(KC):
                    src = st_k[:, k * KN:(k + 1) * KN, :]
                    pool.tensor_scalar(kn[0][k], src, K_S, None, ALU.mult).then_inc(kn_step, 1)
                    pool.wait_ge(kn_step, 3 * k + 1)
                    pool.tensor_scalar(src, src, K_S, None, ALU.mult).then_inc(kn_step, 1)
                    pool.wait_ge(kn_step, 3 * k + 2)
                    pool.tensor_tensor(kn[1][k], src, kn[0][k], ALU.subtract).then_inc(kn_step, 1)
                pool.wait_ge(tn_step, 1)
                pool.tensor_scalar(thr[:, 0:2], thr[:, 2:4], 1.0 / (FF * D), 1e-8, ALU.mult, ALU.max
                                   ).then_inc(tn_step, 1)
                pool.wait_ge(tn_step, 2)
                pool.tensor_scalar(thr[:, 4:6], thr[:, 0:2], 0.5, None, ALU.mult)
                pool.tensor_scalar(thr[:, 6:8], thr[:, 0:2], -0.5, None, ALU.mult).then_inc(tn_step, 1)
                pool.wait_ge(tn_step, 3)
                for n in range(2):
                    if n:
                        pool.wait_ge(tn_made, 1)
                    pool.tensor_scalar(below, st_w[n], thr[:, 6 + n:7 + n], None, ALU.is_lt).then_inc(tn_step, 1)
                    pool.wait_ge(tn_step, 4 + 2 * n)
                    pool.tensor_scalar(st_w[n], st_w[n], thr[:, 4 + n:5 + n], None, ALU.is_gt).then_inc(tn_step, 1)
                    pool.wait_ge(tn_step, 5 + 2 * n)
                    pool.tensor_tensor(st_w[n], st_w[n], below, ALU.subtract).then_inc(tn_made, 1)

            for b in range(B):
                first_t = b * (S // P)
                if b == 1:
                    second_round()
                    gate(pool, end_mo)
                    gather(0, 0, 0)
                    gather(1, 1, 0)

                def qk_rows(c, i, g, more):
                    pool.wait_ge(pj["ve"], at(first_t + c))
                    pool.wait_ge(pj["qkn"], at(first_t + c - 2))
                    pool.tensor_tensor(rstd[:, i, 0:2], ve[:, i, 0:2], mhalf[:, 0:2], ALU.pow
                                       ).then_inc(pj["rs"], 1)
                by(pool, S // P, 2, qk_rows)
                if b == 0:
                    gate(pool, end_rt)
                    pool.wait_ge(zero_st, 16 * (NSLOT_T // 16))
                    by(pool, TT, 4, scatter, head=4)
                else:
                    def next_gather(c, i, g, more):
                        if more:
                            gather(c + 2, i, None)
                    by(pool, TT, 2, next_gather)

            def second_block(c, i, g, more):
                pool.wait_ge(q4["ve"], at(c))
                pool.wait_ge(q4["xn"], at(c - 2))
                pool.tensor_tensor(rstd[:, i, :], ve[:, i, :], mhalf[:, :], ALU.pow).then_inc(q4["rs"], 1)

            def query_norms(c, i, g, more):
                pool.wait_ge(q4["nn"], at(c))
                pool.wait_ge(q4["qs"], at(c - 2))
                pool.tensor_tensor(rn2[:, i, :], nn2[:, i, :], mhalf[:, :], ALU.pow).then_inc(q4["rn"], 1)

            def gated(c, i, g):
                pool.wait_ge(g_ld[i], 32 * g + 32)
                pool.tensor_tensor(gin[i], gin[i], sin[i], ALU.mult).then_inc(q4["m2"], 1)

            def both(c, i, g, more):
                if more:
                    gated(c + 2, i, g + 1)
                if more or i == 0:
                    second_block(c + 1, 1 - i, None, None)
                if not first_step(c):
                    query_norms(c - 1, 1 - i, None, None)
            gated(0, 0, 0)
            second_block(0, 0, None, None)
            gated(1, 1, 0)
            by(pool, NCH, 2, both, head=2)
            query_norms(NCH - 1, 1, None, None)

        @block.tensor
        def _(pe):
            pe.wait_ge(ready_id, 5)
            pe.wait_ge(consts, 1)
            open_(pe, ln["mm"], ex["turned"], *(m[n] for m in (shx, rex) for n in ("gu", "tr", "dn")), rex["xt"],
                  *(q4[n] for n in ("t1", "gm", "t2")), pj["mm"], pj["tr"], mx_first, mx_second)

            loaded = set()
            for j, (need, blocks, hi, lo, scale) in enumerate(jobs):
                for n in need:
                    if n not in loaded:
                        pe.wait_ge(ld[n], 16 * {"qk": 2, "o_v": 2, "sh": 4}[n])
                        loaded.add(n)
                if j >= 8:
                    pe.wait_ge(w_lo, j - 7)
                for n, b in enumerate(blocks):
                    mm = pe.transpose(bank[j % 8][:, n * P:(n + 1) * P], b, ident[:, :])
                mm.then_inc(w_turned, 1)

            pe.wait_ge(w_lo, len(jobs))
            pe.wait_ge(nat_lo, 1)
            pe.wait_ge(bv_step, 4)
            for k in range(KC):
                for n, (m, (x, y)) in enumerate([(m, p) for m in range(KC) for p in THREE]):
                    mm = pe.matmul(bank[0][:, k * D:(k + 1) * D], wv[x][:, m, k * P:(k + 1) * P], woT[y][:, m, :],
                                   start=(n == 0), stop=(n == 5))
            mm.then_inc(wp_mm, 1)
            for n, (m, (x, y)) in enumerate([(m, p) for m in range(KC) for p in THREE]):
                mm = pe.matmul(bank[1][0:33, 0:D], bvc[x][:, m, :], woT[y][:, m, :], start=(n == 0), stop=(n == 5))
            mm.then_inc(wp_mm, 1)
            for k in range(KC):
                mm = pe.transpose(bank[2][:, k * E:(k + 1) * E], st_rw[:, k * P:(k + 1) * P], ident[0:E, 0:E])
            mm.then_inc(rw_mm, 1)
            gate(pe, end_w)

            def turn(c, i, b, src, banks, done, free, ready):
                pe.wait_ge(ready[0], ready[1])
                pe.wait_ge(free[0], free[1])
                for m in range(2):
                    for k in range(KC):
                        mm = pe.transpose(banks[b][:, k * D + m * P:k * D + (m + 1) * P],
                                          src[:, 2 * b + m, k * P:(k + 1) * P], ident[:, :])
                mm.then_inc(done, 1)

            def route(c):
                pe.wait_ge(ln["lo"], at(2 * c + 1))
                for m in range(G4):
                    for n, (k, (x, y)) in enumerate([(k, p) for k in range(KC) for p in THREE]):
                        mm = pe.matmul(a_bank[3][:, bass.ds((c * G4 + m) * E, E)],
                                       xT[x][:, k, bass.ds(c * CW + m * P, P)], rwT[y][:, k, :],
                                       start=(n == 0), stop=(n == 5))
                mm.then_inc(rt_mm, 1)

            def turn_x(c, i, g, more):
                for n in range(3):
                    if first_step(c) and n != 1:
                        pe.wait_ge(ld["gate_up" if n == 0 else "down"], 32)
                    pe.wait_ge(ex["lo"], at(3 * c + n - 3))
                    for m, w in enumerate(ex_job(c, n)[0]):
                        mm = pe.transpose(a_bank[n][:, m * P:(m + 1) * P], w, ident[:, :])
                    mm.then_inc(ex["turned"], 1)
                if not first_step(c):
                    route(c - 1)
                for b in range(2):
                    turn(c, i, b, xn[:, i, :, :], s_bank[2 * i:2 * i + 2], ln["mm"],
                         (ln["lo"], at(2 * (c - 2) + b)), (ln["xn"], at(c)))
            by(pe, NCH, 2, turn_x, head=NCH - 2)
            route(NCH - 1)

            def counts():
                pe.wait_ge(rt_sel, 1)
                pe.matmul(a_bank[2][:, :], before_h[:, :], sel_h[:, :], start=True, stop=True)
                pe.matmul(a_bank[3][:, :], ones_h[:, :], sel_h[:, :], start=True, stop=True).then_inc(rt_cnt, 1)

            def turn_inner(expert, c, i):
                m, (sg, t1, hh, hT), h_bank = expert
                pe.wait_ge(m["h"], at(c))
                pe.wait_ge(m["lo"], at(c - 2))
                for e in range(2):
                    mm = pe.transpose(h_bank[i][:, e * P:(e + 1) * P], hh[:, i, e * P:(e + 1) * P], ident[:, :])
                mm.then_inc(m["tr"], 1)

            def shared_expert():
                def gate_up(c, i):
                    pe.wait_ge(shx["h"], at(c - 2))
                    for n, (kc, (x, y)) in enumerate([(kc, q) for kc in range(KC) for q in THREE]):
                        mm = pe.matmul(s_bank[i][:, :].rearrange("p (e c) -> p e c", e=2),
                                       xT[x][:, kc, bass.ds(c * P, P)], gu[y][:, E:NE, kc, :],
                                       start=(n == 0), stop=(n == 5))
                    mm.then_inc(shx["gu"], 1)

                def down(c, i):
                    pe.wait_ge(shx["lo"], at(c))
                    pe.wait_ge(shx["ev"], at(c - 2))
                    for n, (e, (x, y)) in enumerate([(e, q) for e in range(2) for q in THREE]):
                        mm = pe.matmul(a_bank[i][:, 0:D], sh_buf[3][x][:, i, e * P:(e + 1) * P], dn[y][:, E + e, :],
                                       start=(n == 0), stop=(n == 5))
                    mm.then_inc(shx["dn"], 1)

                def step(c, i, g, more):
                    if more:
                        gate_up(c + 2, i)
                    if more or i == 0:
                        turn_inner(shared, c + 1, 1 - i)
                    down(c, i)
                gate_up(0, 0)
                gate_up(1, 1)
                turn_inner(shared, 0, 0)
                by(pe, TT, 2, step, pauses={COUNTS_AT: counts})

            def routed_experts():
                def turn_rows(c, r4, g):
                    pe.wait_ge(rex_ld[r4], 16 * g + 16)
                    pe.wait_ge(rex["xl"], at(c - 2))
                    for m in range(2):
                        for k in range(KC):
                            mm = pe.transpose(s_bank[2 + r4 % 2][:, k * D + m * P:k * D + (m + 1) * P],
                                              xs[:, r4, m, k * P:(k + 1) * P], ident[:, :])
                    mm.then_inc(rex["xt"], 1)

                def experts(c, n):
                    _, es = nc.values_load_multi_w_load_instructions(
                        expert_of[0:1, bass.ds(2 * c, 2 * n)], engines=(nc.tensor.engine,), min_val=0, max_val=E - 1,
                        skip_runtime_bounds_check_because="the routing clamps them to 0 .. E - 1")
                    return es

                def gate_up(c, i, es):
                    pe.wait_ge(rex["xl"], at(c))
                    pe.wait_ge(rex["h"], at(c - 2))
                    for m in range(2):
                        for n, (kc, (x, y)) in enumerate([(kc, q) for kc in range(KC) for q in THREE]):
                            mm = pe.matmul(s_bank[i][:, m * D:(m + 1) * D], xgT[x][:, i, kc, m * P:(m + 1) * P],
                                           gu[y][:, bass.ds(es[m], 1), kc, :].rearrange("p o c -> p (o c)"),
                                           start=(n == 0), stop=(n == 5))
                    mm.then_inc(rex["gu"], 1)

                def down(c, i, es):
                    pe.wait_ge(rex["lo"], at(c))
                    pe.wait_ge(rex["ev"], at(c - 2))
                    for m in range(2):
                        for n, (x, y) in enumerate(THREE):
                            mm = pe.matmul(a_bank[i][:, m * D:(m + 1) * D], ex_buf[3][x][:, i, m * P:(m + 1) * P],
                                           dn[y][:, bass.ds(es[m], 1), :].rearrange("p o h -> p (o h)"),
                                           start=(n == 0), stop=(n == 2))
                    mm.then_inc(rex["dn"], 1)

                body = [None]

                def step(c, i, g, more):
                    if i == 0:
                        body[0] = experts(c, 6 if more else 4)
                    es = body[0]
                    if more or i == 0:
                        turn_rows(c + 3, (i + 3) % 4, g if i == 0 else g + 1)
                    if more or i < 2:
                        gate_up(c + 2, i % 2, es[2 * i + 4:2 * i + 6])
                    if more or i < 3:
                        turn_inner(routed, c + 1, 1 - i % 2)
                    down(c, i % 2, es[2 * i:2 * i + 2])
                first = experts(0, 2)
                for c in range(3):
                    turn_rows(c, c, 0)
                    if c:
                        gate_up(c - 1, c - 1, first[2 * c - 2:2 * c])
                turn_inner(routed, 0, 0)
                by(pe, NSLOT_T // 2, 4, step)

            def mix(m):
                def first(c, j):
                    k = m.step(c, j)
                    pe.wait_ge(m.act_done, at(k - 4))
                    seq = [(kc, q) for kc in range(KC) for q in m.pass1]
                    for n, (kc, (x, y)) in enumerate(seq):
                        mm = pe.matmul(s_bank[j % 4][:, :], m.stat(x, kc, j), m.mov(y, kc, c),
                                       start=(n == 0), stop=(n == len(seq) - 1))
                    mm.then_inc(m.first_done, 1)

                def second(c, i, j):
                    k = m.step(c, j)
                    pe.wait_ge(m.lo_done, at(k))
                    if j == 0:
                        pe.wait_ge(m.evac_read, at(m.ch(c - 2)))
                    for q in range(G4):
                        for n, (x, y) in enumerate(m.pass2):
                            part = (ah, al)[x]
                            mm = pe.matmul(a_bank[2 * i + q // 2][:, (q % 2) * D:(q % 2 + 1) * D],
                                           part[:, j % 4, q * P:(q + 1) * P], m.second(y, j),
                                           start=(j == 0 and n == 0 and q % 2 == 0),
                                           stop=(j == m.nt - 1 and n == len(m.pass2) - 1 and q % 2 == 1),
                                           skip_group_check=True)
                    mm.then_inc(m.second_done, 1)

                def chunk(c, i, g, more):
                    for j in range(m.nt):
                        if j + 2 < m.nt:
                            first(c, j + 2)
                        elif more or i == 0:
                            first(c + 1, j + 2 - m.nt)
                        second(c, i, j)
                first(0, 0)
                first(0, 1)
                by(pe, m.nch, 2, chunk)

            def late_round():
                pe.wait_ge(kn_step, 3 * KC)
                for j, (blocks, hi, lo, scale) in enumerate(late_jobs):
                    if j >= 8:
                        pe.wait_ge(w_lo, len(jobs) + j - 7)
                    if j == LATE_LO:
                        pe.wait_ge(tn_made, 2)
                    for n, w in enumerate(blocks):
                        mm = pe.transpose(bank[j % 8][:, n * P:(n + 1) * P], w, ident[:, :])
                    mm.then_inc(w_turned, 1)

            gate(pe, end_x)
            shared_expert()
            before = end_rt
            for b in range(B):
                first_t = b * (S // P)
                gate(pe, before)
                if b == 1:
                    late_round()
                    gate(pe, end_late)

                def project(t, i):
                    pe.wait_ge(pj["qkn"], at(first_t + t - 4))
                    pe.matmul(s_bank[i % 4][:, :], ones33[:, :], biasz[:, 0:2 * D], start=True, stop=False)
                    for n, (k, (x, y)) in enumerate([(k, p) for k in range(KC) for p in THREE]):
                        mm = pe.matmul(s_bank[i % 4][:, :], xT[x][:, k, bass.ds(b * S + t * P, P)], wqkT[y][:, k, :],
                                       start=False, stop=(n == 5))
                    pe.wait_ge(pj["vlo"], at(first_t + t - 2))
                    v_ps = a_bank[2 + i % 2][:, 0:D]
                    pe.matmul(v_ps, ones33[:, :], biasz[:, 2 * D:3 * D], start=True, stop=False)
                    for n, (k, (x, y)) in enumerate([(k, p) for k in range(KC) for p in THREE]):
                        mm = pe.matmul(v_ps, xT[x][:, k, bass.ds(b * S + t * P, P)], wpT[y][:, k, :],
                                       start=False, stop=(n == 5))
                    mm.then_inc(pj["mm"], 1)

                def turn_qk(t, i, g, more):
                    if more or i == 0:
                        project(t + 3, i + 3)
                    pe.wait_ge(pj["qkn"], at(first_t + t))
                    pe.wait_ge(pj["tlo"], at(first_t + t - 2))
                    for n in range(2 * KC):
                        mm = pe.transpose(a_bank[i % 2][:, n * P:(n + 1) * P], qkn[:, i % 2, n * P:(n + 1) * P],
                                          ident[:, :])
                    mm.then_inc(pj["tr"], 1)
                for t in range(3):
                    project(t, t)
                by(pe, S // P, 4, turn_qk)
                gate(pe, end_pj[b])
                mix(at_mix[b])
                before = end_mix(at_mix[b])
                if b == 0:
                    pe.wait_ge(mx_act, at(at_mix[0].step(S // CW - 1, S // P - 1)))
                    routed_experts()
                    before = end_mo

            pe.wait_ge(mx_evac, at(at_mix[1].ch(S // CW - 2)))

            def turn1(c, i):
                for b in range(2):
                    turn(c, i, b, xn[:, i, :, :], s_bank[0:2], q4["t1"],
                         (q4["l1"], at(2 * (c - 1) + b)), (q4["xn"], at(c)))

            def turn2(c, i):
                for b in range(2):
                    turn(c, i, b, qsb[i], s_bank[2:4], q4["t2"],
                         (q4["l2"], at(2 * (c - 1) + b)), (q4["qs"], at(c)))

            def second_block(c, i, g, more):
                pe.wait_ge(q4["l1"], at(2 * c + 1))
                pe.wait_ge(q4["nn"], at(c - 1))
                for m in range(G4):
                    for n, (k, (x, y)) in enumerate([(k, p) for k in range(KC) for p in THREE]):
                        mm = pe.matmul(a_bank[m][:, 0:D], xT[x][:, k, bass.ds(c * CW + m * P, P)], gram[y][:, k, :],
                                       start=(n == 0), stop=(n == 5))
                mm.then_inc(q4["gm"], 1)
                if more or i == 0:
                    turn1(c + 1, 1 - i)
                if not first_step(c):
                    turn2(c - 1, 1 - i)
            for k in range(KC):
                seq = [(m, p) for m in range(NB // P) for p in THREE]
                for n, (m, (x, y)) in enumerate(seq):
                    mm = pe.matmul(a_bank[0][:, k * D:(k + 1) * D], kn[x][m // KN][:, m % KN, k * P:(k + 1) * P],
                                   kn[y][m // KN][:, m % KN, :], start=(n == 0), stop=(n == len(seq) - 1))
            mm.then_inc(gram_mm, 1)
            turn1(0, 0)
            pe.wait_ge(gram_lo, 1)
            by(pe, NCH, 2, second_block, head=2)
            turn2(NCH - 1, 1)

            gate(pe, end_q4)
            mix(ff_mix)
            pe.wait_ge(vb_lo, NCH)
            mix(bk_mix)

        @block.scalar
        def _(act):
            open_(act, ln["xn"], ln["hi"], ex["hi"], *(m[n] for m in (shx, rex) for n in ("sig", "hi", "ev")),
                  rex["xh"], *(pj[n] for n in ("qkn", "vhi", "thi")), mx_act, cb_sig,
                  *(q4[n] for n in ("xn", "h1", "qs", "h2")), vb_hi, bk_tanh)

            def copy(out_ap, in_ap, scale, done):
                act.activation(out_ap, in_ap, ACT.Copy, scale=scale).then_inc(done, 1)

            for j, (need, blocks, hi, lo, scale) in enumerate(jobs):
                act.wait_ge(w_turned, j + 1)
                copy(hi, job_ps(j), scale, w_hi)
                if j == WO_JOBS:
                    act.wait_ge(ld["o_v"], 32)
                    copy(wv[0][:, :, :], st_wv, WQK_S, nat_hi)
            act.wait_ge(wp_mm, 1)
            copy(wpT[0][:, :, :], bank[0][:, :].rearrange("p (k c) -> p k c", k=KC), WP_S / (WQK_S * WO_S), wp_hi)
            act.wait_ge(rw_mm, 1)
            copy(rwT[0][:, :, :], bank[2][:, 0:2 * E].rearrange("p (k c) -> p k c", k=KC), WQK_S, rw_hi)
            def hi_of(c, i, b, banks, dst, scale, turned, done):
                act.wait_ge(turned, at(2 * c + b))
                copy(dst[0][:, :, bass.ds(c * CW + b * D, D)], banks[b][:, :].rearrange("p (k c) -> p k c", k=KC),
                     scale, done)

            gate(act, end_w)

            def norm(i, done):
                for m in range(G4):
                    ins = act.activation(xn[:, i, m, :], xin[:, i, m, :], ACT.Identity, bias=nmr[:, i, m:m + 1],
                                         scale=rstd[:, i, m:m + 1])
                ins.then_inc(done, 1)

            def hi_x(c, i, g, more):
                act.wait_ge(ln["nmr"], at(c))
                act.wait_ge(ln["mm"], at(2 * (c - 2) + 1))
                act.wait_ge(xn_st[i], 16 * g + 16)
                norm(i, ln["xn"])
                for n in range(3):
                    act.wait_ge(ex["turned"], at(3 * c + n))
                    copy(ex_job(c, n)[1][0], a_bank[n][:, :].rearrange("p (k c) -> p k c", k=2), WQK_S, ex["hi"])
                for b in range(2):
                    hi_of(c, i, b, s_bank[2 * i:2 * i + 2], xT, X_S, ln["mm"], ln["hi"])
            by(act, NCH, 2, hi_x)

            gate(act, end_x)
            act.wait_ge(rt_mm, NCH)
            act.activation(scores[:, :], a_bank[3][:, :], ACT.Sigmoid, scale=1.0 / QK_PS).then_inc(rt_sig, 1)

            def sigmoid_gate(expert, c, i):
                m, (sg, t1, hh, hT), h_bank = expert
                act.wait_ge(m["gu"], at(c))
                act.wait_ge(m["t1"], at(c - 2))
                act.activation(sg[:, i, :].rearrange("p (e c) -> p e c", e=2),
                               s_bank[i][:, :].rearrange("p (e c) -> p e c", e=2)[:, :, 0:IM],
                               ACT.Sigmoid, scale=1.0 / QK_PS).then_inc(m["sig"], 1)

            def inner_hi(expert, c, i):
                m, (sg, t1, hh, hT), h_bank = expert
                act.wait_ge(m["tr"], at(c))
                act.wait_ge(m["dn"], at(c - 2))
                copy(hT[0][:, i, :], h_bank[i][:, 0:D], 1.0, m["hi"])

            def shared_expert():
                def rows_out(c, i, g):
                    act.wait_ge(shx["dn"], at(c))
                    act.wait_ge(shx_st[i], 16 * g + 16)
                    copy(sres[:, i, :], a_bank[i][:, 0:D], 1.0 / (H_S * WQK_S), shx["ev"])

                def step(c, i, g, more):
                    inner_hi(shared, c, i)
                    if more or i == 0:
                        sigmoid_gate(shared, c + 1, 1 - i)
                    if not first_step(c):
                        rows_out(c - 1, 1 - i, g - 1 + i)
                sigmoid_gate(shared, 0, 0)
                by(act, TT, 2, step, head=2)
                rows_out(TT - 1, 1, TT // 2 - 1)

            def routed_experts():
                def rows_hi(c, i):
                    act.wait_ge(rex["xt"], at(c))
                    act.wait_ge(rex["gu"], at(c - 2))
                    copy(xgT[0][:, i, :, :], s_bank[2 + i][:, :].rearrange("p (k c) -> p k c", k=KC), X_S, rex["xh"])

                def rows_out(c, i, g):
                    act.wait_ge(rex["dn"], at(c))
                    act.wait_ge(rex_st[i % 2], 32 * g + 16 * (i // 2) + 16)
                    copy(yres[:, i % 2, :, :], a_bank[i % 2][:, :].rearrange("p (m d) -> p m d", m=2),
                         1.0 / (H_S * WQK_S), rex["ev"])

                def step(c, i, g, more):
                    inner_hi(routed, c, i % 2)
                    if more or i < 3:
                        sigmoid_gate(routed, c + 1, 1 - i % 2)
                    if more or i == 0:
                        rows_hi(c + 3, 1 - i % 2)
                    if not first_step(c):
                        rows_out(c - 1, (i + 3) % 4, g if i else g - 1)
                for c in range(3):
                    rows_hi(c, c % 2)
                sigmoid_gate(routed, 0, 0)
                by(act, NSLOT_T // 2, 4, step, head=4)
                rows_out(NSLOT_T // 2 - 1, 3, NSLOT_T // 8 - 1)

            def experts_sigmoid(t, r):
                act.wait_ge(cb_step, TOPK * (t + 1) + CR)
                act.wait_ge(cb_done, at(t - 2))
                act.activation(sgc[:, r, :], cres[:, r, :], ACT.Sigmoid).then_inc(cb_sig, 1)

            def sigmoid_step(c, j):
                if j % 2 == 0 and not (first_step(c) and j < 4):
                    experts_sigmoid(c * (S // P // 2) + j // 2 - 2, j // 2 % 2)

            def store_rows(b, c, i):
                act.wait_ge(mx_evac, at(at_mix[b].ch(c)))
                act.dma_start(one(s0_c, b * (S // CW) + c), xin[:, i, :, :]).then_inc(at_mix[b].stored[i], 16)

            def mix(m, at_chunk=None, store=None, at_step=None):
                def chunk(c, i, g, more):
                    for j in range(m.nt):
                        if j == 6 and at_chunk:
                            at_chunk(c, i, g)
                        if j == 6 and store is not None and not first_step(c):
                            store_rows(store, c - 1, 1 - i)
                        if at_step:
                            at_step(c, j)
                        k = m.step(c, j)
                        act.wait_ge(m.first_done, at(k))
                        act.wait_ge(m.lo_done, at(k - 2))
                        act.activation(att[:, j % 2, :], s_bank[j % 4][:, :], m.func,
                                       bias=m.bias(j) if m.bias else 0.0, scale=m.scale).then_inc(m.act_done, 1)
                by(act, m.nch, 2, chunk, head=2 if store is not None else 0)
                if at_step:
                    for j in range(0, 4, 2):
                        at_step(m.nch, j)
                if store is not None:
                    store_rows(store, m.nch - 1, 1)

            shared_expert()
            before = end_rt
            for b in range(B):
                first_t = b * (S // P)
                gate(act, before)
                if b == 1:
                    for j, (blocks, hi, lo, scale) in enumerate(late_jobs):
                        act.wait_ge(w_turned, len(jobs) + j + 1)
                        copy(hi, job_ps(j), scale, w_hi)
                    gate(act, end_late)

                def values_hi(t, i):
                    act.wait_ge(pj["mm"], at(first_t + t))
                    copy(vp[0][:, bass.ds(t, 1), :].rearrange("p o e -> p (o e)"), a_bank[2 + i % 2][:, 0:D],
                         V_S / VP_PS, pj["vhi"])

                def norm_rows(t, i):
                    act.wait_ge(pj["nmr"], at(first_t + t))
                    act.wait_ge(pj["tr"], at(first_t + t - 2))
                    for n in range(2):
                        ins = act.activation(qkn[:, i % 2, n * D:(n + 1) * D], s_bank[i % 4][:, n * D:(n + 1) * D],
                                             ACT.Identity, bias=nmr[:, i % 2, n:n + 1], scale=rstd[:, i % 2, n:n + 1])
                    ins.then_inc(pj["qkn"], 1)

                def rows_hi(t, i, g, more):
                    if more or i < 2:
                        values_hi(t + 2, i + 2)
                    if more or i < 3:
                        norm_rows(t + 1, i + 1)
                    act.wait_ge(pj["tr"], at(first_t + t))
                    copy(qkT[0][:, :, bass.ds(t * P, P)], a_bank[i % 2][:, :].rearrange("p (k c) -> p k c", k=2 * KC),
                         X_S, pj["thi"])
                values_hi(0, 0)
                values_hi(1, 1)
                norm_rows(0, 0)
                by(act, S // P, 4, rows_hi)
                gate(act, end_pj[b])
                mix(at_mix[b], store=b, at_step=sigmoid_step if b == 1 else None)
                before = end_mix(at_mix[b])
                if b == 0:
                    routed_experts()
                    before = end_mo

            gate(act, before)
            def hi_rows(c, i):
                for b in range(2):
                    hi_of(c, i, b, s_bank[0:2], xT, X_S, q4["t1"], q4["h1"])

            def hi_queries(c, i):
                for b in range(2):
                    hi_of(c, i, b, s_bank[2:4], qsT, QS_S, q4["t2"], q4["h2"])

            def norm_x1(c, i):
                act.wait_ge(q4["nmr"], at(c))
                act.wait_ge(q4["t1"], at(2 * (c - 2) + 1))
                act.wait_ge(q4["nn"], at(c - 2))
                act.wait_ge(q4["qs"], at(c - 2))
                norm(i, q4["xn"])

            def queries(c, i):
                act.wait_ge(q4["rn"], at(c))
                act.wait_ge(q4["t2"], at(2 * (c - 2) + 1))
                for m in range(G4):
                    ins = act.activation(qsb[i][:, m, :], xn[:, i, m, :], ACT.Copy, scale=rn2[:, i, m:m + 1])
                ins.then_inc(q4["qs"], 1)

            def second_block(c, i, g, more):
                hi_rows(c, i)
                if not (isinstance(c, int) and c < 2):
                    hi_queries(c - 2, i)
                if not first_step(c):
                    queries(c - 1, 1 - i)
                if more or i == 0:
                    norm_x1(c + 1, 1 - i)
            norm_x1(0, 0)
            act.wait_ge(gram_mm, 1)
            copy(gram[0][:, :, :], a_bank[0][:, :].rearrange("p (k c) -> p k c", k=KC), GRAM_S / (K_S * K_S), gram_hi)
            by(act, NCH, 2, second_block, head=2)
            hi_queries(NCH - 2, 0)
            queries(NCH - 1, 1)
            hi_queries(NCH - 1, 1)

            gate(act, end_q4)

            def bank_hi(c, i, g):
                act.wait_ge(ld["vb"], 16)
                rows_c = bass.ds(c * VB_N, VB_N)
                copy(vb[0][:, rows_c, :], st_vb[:, rows_c, :], K_S, vb_hi)
            mix(ff_mix, bank_hi)

            def tanh_half(c, i, g):
                act.wait_ge(bk_ld[i], 32 * g + 32)
                act.wait_ge(bk_silu, at(c - 2))
                act.activation(tbuf[i], gl[i], ACT.Tanh, scale=0.5).then_inc(bk_tanh, 1)
            mix(bk_mix, tanh_half)

        @block.vector
        def _(dve):
            dve.memset(bias3[:, :], 0.0)
            dve.memset(ones33[:, :], X_S)
            dve.memset(onesf[:, :], 1.0)
            dve.memset(xr[:, 0, :], 0.0)
            dve.memset(nlogs[:, :], -math.log(S)).then_inc(consts, 1)
            open_(dve, ex["lo"], *(ln[n] for n in ("mv", "ve", "nmr", "lo")),
                  *(pj[n] for n in ("mv", "ve", "nmr", "vlo", "tlo")),
                  *(m[n] for m in (shx, rex) for n in ("t1", "h", "lo")), rex["xl"], cb_step, cb_done,
                  *(q4[n] for n in ("x1", "mv", "ve", "nmr", "l1", "nn", "l2")), bk_silu,
                  mx_hi, mx_lo, mx_read, mx_evac)

            def low(out_ap, in_ap, scale, hi_ap, done=None):
                ins = dve.scalar_tensor_tensor(out=out_ap, in0=in_ap, scalar=scale, in1=hi_ap, op0=ALU.mult,
                                               op1=ALU.subtract)
                if done is not None:
                    ins.then_inc(done, 1)

            for j, (need, blocks, hi, lo, scale) in enumerate(jobs):
                dve.wait_ge(w_hi, j + 1)
                low(lo, job_ps(j), scale, hi, w_lo)
                if j == WO_JOBS:
                    dve.wait_ge(nat_hi, 1)
                    low(wv[1][:, :, :], st_wv, WQK_S, wv[0][:, :, :], nat_lo)
            dve.wait_ge(consts, 1)
            dve.wait_ge(ld["small"], 16 * 10)
            for t in range(KC):
                dve.tensor_scalar(bvt[:, t, :], onesf[:, 0:33], bvf[:, t:t + 1], WQK_S, ALU.mult, ALU.mult
                                  ).then_inc(bv_step, 1)
            dve.wait_ge(bv_step, 2)
            dve.tensor_copy(bvc[0][:, :, :], bvt[:, :, :]).then_inc(bv_step, 1)
            dve.wait_ge(bv_step, 3)
            low(bvc[1][:, :, :], bvt[:, :, :], 1.0, bvc[0][:, :, :], bv_step)
            def moments(src, n, i, c, q, eps):
                for m in range(n):
                    dve.bn_stats(stat[:, i, m, :], src(m))
                dve.drain()
                for m in range(n):
                    ins = dve.bn_aggr(mv[:, i, m, :], stat[:, i, m, :])
                ins.then_inc(q["mv"], 1)
                dve.wait_ge(q["mv"], at(c))
                dve.tensor_scalar(ve[:, i, 0:n], mv[:, i, 0:n, 1], eps, None, ALU.add).then_inc(q["ve"], 1)

            def x_moments(c, i, g):
                dve.wait_ge(x_ld[i], 16 * g + 16)
                moments(lambda m: xin[:, i, m, :], G4, i, c, ln, EPS)

            x_moments(0, 0, 0)

            dve.wait_ge(wp_hi, 1)
            low(wpT[1][:, :, :], bank[0][:, :].rearrange("p (k c) -> p k c", k=KC), WP_S / (WQK_S * WO_S),
                wpT[0][:, :, :], wp_lo)
            dve.wait_ge(wp_mm, 2)
            for r in (0, 32):
                dve.tensor_scalar(bias3[r:r + 1, 2 * D:3 * D], bank[1][r:r + 1, 0:D],
                                  WP_S / (WQK_S * WQK_S * WO_S), None, ALU.mult).then_inc(bias_step, 1)
            dve.wait_ge(bias_step, 2)
            dve.tensor_scalar(biasz[:, :], bias3[:, :], WQK_S, None, ALU.mult).then_inc(bias_step, 1)
            dve.wait_ge(bias_step, 3)
            low(biasz[32:33, :], bias3[32:33, :], WQK_S, biasz[32:33, :], bias_step)
            dve.wait_ge(rw_hi, 1)
            low(rwT[1][:, :, :], bank[2][:, 0:2 * E].rearrange("p (k c) -> p k c", k=KC), WQK_S, rwT[0][:, :, :],
                rw_lo)
            def low_of(c, i, b, banks, dst, scale, his, done):
                dve.wait_ge(his, at(2 * c + b))
                cols = bass.ds(c * CW + b * D, D)
                low(dst[1][:, :, cols], banks[b][:, :].rearrange("p (k c) -> p k c", k=KC), scale,
                    dst[0][:, :, cols], done)

            gate(dve, end_w)

            def shifts(c, i, q):
                dve.wait_ge(q["rs"], at(c))
                dve.wait_ge(q["xn"], at(c - 2))
                dve.scalar_tensor_tensor(out=nmr[:, i, :], in0=mv[:, i, :, 0], scalar=-1.0, in1=rstd[:, i, :],
                                         op0=ALU.mult, op1=ALU.mult).then_inc(q["nmr"], 1)

            def x_norm(c, i, g, more):
                shifts(c, i, ln)
                if more or i == 0:
                    x_moments(c + 1, 1 - i, g + i)
                for n in range(3):
                    dve.wait_ge(ex["hi"], at(3 * c + n))
                    hi, lo = ex_job(c, n)[1]
                    low(lo, a_bank[n][:, :].rearrange("p (k c) -> p k c", k=2), WQK_S, hi, ex["lo"])
                for b in range(2):
                    low_of(c, i, b, s_bank[2 * i:2 * i + 2], xT, X_S, ln["hi"], ln["lo"])
            by(dve, NCH, 2, x_norm)

            gate(dve, end_x)
            count = [0]

            def step(ins):
                count[0] += 1
                ins.then_inc(rt_step, 1)
                dve.wait_ge(rt_step, count[0])

            def ranks(vals, n, beat, rank, xs, ts):
                dve.memset(beat[:, :, 0:n * n:n + 1], 0.0)
                bt = beat[:, :, :].rearrange("p t (x y) -> p t x y", x=n)
                for x in range(n):
                    for lo_, hi_, op in ((0, x, ALU.is_ge), (x + 1, n, ALU.is_gt)):
                        if hi_ > lo_:
                            ins = dve.tensor_tensor(bt[:, :, x, lo_:hi_], vals[:, :, lo_:hi_],
                                                    spread(vals[:, :, x:x + 1], 2, hi_ - lo_), op)
                    if x % xs == xs - 1 and x < n - 1:
                        yield
                step(ins)
                for t in range(0, TT, ts):
                    ins = dve.tensor_reduce(rank[:, t:t + ts, :], bt[:, t:t + ts, :, :], AXX, ALU.add)
                    if t + ts < TT:
                        yield
                step(ins)

            def routing():
                dve.wait_ge(rt_sig, 1)
                sc3 = scores[:, :].rearrange("p (t e) -> p t e", e=E)
                b3 = biased[:, :].rearrange("p (t e) -> p t e", e=E)
                step(dve.tensor_tensor(b3, sc3, spread(eb_b[:, :].rearrange("p (o e) -> p o e", o=1), 1, TT), ALU.add))
                yield
                b4 = biased[:, :].rearrange("p (n e) -> p n e", e=EPG)
                pairs = [(x, y) for x in range(EPG) for y in range(x + 1, EPG)]
                for n, (x, y) in enumerate(pairs):
                    ins = dve.tensor_tensor(pair_s[:, :, n], b4[:, :, x], b4[:, :, y], ALU.add)
                step(ins)
                step(dve.tensor_reduce(gs[:, :], pair_s[:, :, :], AXX, ALU.max))

                yield
                yield from ranks(gs[:, :].rearrange("p (t g) -> p t g", g=GROUPS), GROUPS, gbeat,
                                 grank[:, :].rearrange("p (t g) -> p t g", g=GROUPS), GROUPS, TT)
                yield
                step(dve.tensor_scalar(gsel[:, :], grank[:, :], GTOP - 0.5, None, ALU.is_lt))
                step(dve.tensor_tensor(masked[:, :].rearrange("p (n e) -> p n e", e=EPG), b4,
                                       spread(gsel[:, :].rearrange("p (n o) -> p n o", o=1), 2, EPG), ALU.mult))
                m3 = masked[:, :].rearrange("p (t e) -> p t e", e=E)
                yield
                yield from ranks(m3, E, ebeat, erank[:, :].rearrange("p (t e) -> p t e", e=E), 3, TT // 4)
                dve.tensor_scalar(sel_h[:, :], erank[:, :], TOPK - 0.5, None, ALU.is_lt).then_inc(rt_sel, 1)
                yield
                step(dve.scalar_tensor_tensor(out=masked[:, :], in0=erank[:, :], scalar=TOPK - 0.5, in1=scores[:, :],
                                              op0=ALU.is_lt, op1=ALU.mult))
                step(dve.tensor_reduce(esum[:, 0:TT], m3, AXX, ALU.add))
                yield
                step(dve.tensor_scalar(esum[:, 0:TT], esum[:, 0:TT], 1e-20, None, ALU.add))
                step(dve.reciprocal(esum[:, TT:2 * TT], esum[:, 0:TT]))
                step(dve.scalar_tensor_tensor(out=b3, in0=m3, scalar=ROUTE_SCALE,
                                              in1=spread(esum[:, TT:2 * TT].rearrange("p (t o) -> p t o", o=1), 2, E),
                                              op0=ALU.mult, op1=ALU.mult))
                yield
                dve.wait_ge(rt_cnt, 1)
                total = a_bank[3][:, :].rearrange("p (t e) -> p t e", e=E)
                step(dve.tensor_copy(cnt[0], total))
                src, dst = 0, 1
                d = 1
                while d < TT:
                    dve.tensor_copy(cnt[dst][:, 0:d, :], cnt[src][:, 0:d, :])
                    step(dve.tensor_tensor(cnt[dst][:, d:TT, :], cnt[src][:, d:TT, :], cnt[src][:, 0:TT - d, :],
                                           ALU.add))
                    if d in (2, 8):
                        yield
                    src, dst, d = dst, src, 2 * d
                yield
                run = cnt[src]
                step(dve.tensor_tensor(cnt[dst], run, total, ALU.subtract))
                within = a_bank[2][:, :].rearrange("p (t e) -> p t e", e=E)
                yield
                step(dve.tensor_scalar(small[0], run[:, TT - 1, :], 1.0 / P, 127.0 / P - 0.5 + 0.5 / P, ALU.mult,
                                       ALU.add))
                step(dve.tensor_scalar(small[1], small[0], ROUND, None, ALU.add))
                step(dve.tensor_scalar(small[2], small[1], -ROUND, None, ALU.add))
                step(dve.tensor_copy(small[3], small[2]))
                a_, b_, d = 3, 4, 1
                while d < E:
                    dve.tensor_copy(small[b_][:, 0:d], small[a_][:, 0:d])
                    step(dve.tensor_tensor(small[b_][:, d:E], small[a_][:, d:E], small[a_][:, 0:E - d], ALU.add))
                    a_, b_, d = b_, a_, 2 * d
                yield
                ends = small[a_]
                step(dve.tensor_tensor(small[5], ends, small[2], ALU.subtract))
                step(dve.tensor_scalar(small[6], small[5], float(P), None, ALU.mult))
                step(dve.tensor_tensor(cnt[2], cnt[dst], within, ALU.add))
                first_slot = spread(small[6].rearrange("p (o e) -> p o e", o=1), 1, TT)
                step(dve.tensor_tensor(cnt[2], cnt[2], first_slot, ALU.add))
                yield
                er3 = erank[:, :].rearrange("p (t e) -> p t e", e=E)
                for k in range(TOPK):
                    for n, v in enumerate((cnt[2], b3)):
                        ins = dve.scalar_tensor_tensor(out=picks[n][:, k, :, :], in0=er3, scalar=float(k), in1=v,
                                                       op0=ALU.is_equal, op1=ALU.mult)
                    if k < TOPK - 1:
                        yield
                step(ins)
                yield
                dve.tensor_reduce(slot_f.rearrange("p (k t) -> p k t", k=TOPK), picks[0], AXX, ALU.add)
                step(dve.tensor_reduce(w4[:, :, :], picks[1], AXX, ALU.add))
                yield
                dve.tensor_copy(slot_i[:, :, :], slot_f.rearrange("p (k t) -> p k t", k=TOPK))
                step(dve.tensor_copy(tile_f, tile_no[:, :]))
                step(dve.tensor_tensor(upto, spread(ends[0:1, :].rearrange("p (o e) -> p o e", o=1), 1, NSLOT_T),
                                       spread(tile_f.rearrange("p (j o) -> p j o", o=1), 2, E), ALU.is_le))
                yield
                step(dve.tensor_reduce(exp_f, upto, AXX, ALU.add))
                dve.tensor_scalar(expert_of[:, :], exp_f, float(E - 1), None, ALU.min).then_inc(rt_done, 1)

            def inner(expert, c, i):
                m, (sg, t1, hh, hT), h_bank = expert
                ps = s_bank[i][:, :].rearrange("p (e c) -> p e c", e=2)
                t3 = t1[:, i, :].rearrange("p (e c) -> p e c", e=2)
                dve.wait_ge(m["sig"], at(c))
                dve.tensor_tensor(t3, sg[:, i, :].rearrange("p (e c) -> p e c", e=2), ps[:, :, 0:IM], ALU.mult
                                  ).then_inc(m["t1"], 1)
                dve.wait_ge(m["t1"], at(c))
                dve.wait_ge(m["tr"], at(c - 2))
                dve.scalar_tensor_tensor(out=hh[:, i, :].rearrange("p (e c) -> p e c", e=2), in0=t3,
                                         scalar=H_S / (QK_PS * QK_PS), in1=ps[:, :, IM:2 * IM],
                                         op0=ALU.mult, op1=ALU.mult).then_inc(m["h"], 1)

            def inner_lo(expert, c, i):
                m, (sg, t1, hh, hT), h_bank = expert
                dve.wait_ge(m["hi"], at(c))
                low(hT[1][:, i, :], h_bank[i][:, 0:D], 1.0, hT[0][:, i, :], m["lo"])

            def shared_expert():
                def one_step(c, i, g, more):
                    inner_lo(shared, c, i)
                    if more or i == 0:
                        inner(shared, c + 1, 1 - i)
                inner(shared, 0, 0)
                stages = routing()
                for c in range(TT):
                    one_step(c, c % 2, c // 2, c < TT - 2)
                    next(stages, None)
                for _ in stages:
                    pass

            def routed_experts():
                def rows_lo(c, i):
                    dve.wait_ge(rex["xh"], at(c))
                    low(xgT[1][:, i, :, :], s_bank[2 + i][:, :].rearrange("p (k c) -> p k c", k=KC), X_S,
                        xgT[0][:, i, :, :], rex["xl"])

                def one_step(c, i, g, more):
                    inner_lo(routed, c, i % 2)
                    if more or i < 3:
                        inner(routed, c + 1, 1 - i % 2)
                    if more or i == 0:
                        rows_lo(c + 3, 1 - i % 2)
                    if isinstance(c, int) and c in (4, 5):
                        dve.wait_ge(ld["w12"], 32)
                        dve.tensor_reduce(thr[:, c - 4:c - 3], st_w[c - 4], AXX, ALU.add, apply_absolute_value=True
                                          ).then_inc(tn_sum, 1)
                    if isinstance(c, int) and c == 11:
                        dve.wait_ge(tn_dma, 32)
                        dve.tensor_reduce(thr[:, 2:4], w_sums.rearrange("p q n -> p n q"), AXX, ALU.add
                                          ).then_inc(tn_step, 1)
                for c in range(3):
                    rows_lo(c, c % 2)
                inner(routed, 0, 0)
                by(dve, NSLOT_T // 2, 4, one_step, head=12)

            def experts_silu(t, r):
                dve.wait_ge(cb_sig, at(t))
                dve.tensor_tensor(cres[:, r, :], cres[:, r, :], sgc[:, r, :], ALU.mult).then_inc(cb_done, 1)

            def combine(c, j):
                if j % 2 == 0:
                    return
                t, r = c * (S // P // 2) + j // 2, j // 2 % 2
                pair = c * (S // P // 4) + j // 4
                if not first_step(t):
                    experts_silu(t - 1, 1 - r)
                dve.wait_ge(sh_ld[r], 16 * pair + 16)
                dve.wait_ge(y_ld[r], 16 * TOPK * pair + 16 * TOPK)
                dve.wait_ge(cb_st[r], 16 * pair + 16)
                acc = yg[:, r, TOPK, :]
                for k in range(TOPK):
                    last = k == TOPK - 1
                    dve.scalar_tensor_tensor(
                        out=cres[:, r, :] if last else acc, in0=yg[:, r, k, :],
                        scalar=w4[:, k, bass.ds(t, 1)], in1=acc, op0=ALU.mult, op1=ALU.add).then_inc(cb_step, 1)
                    if not last:
                        dve.wait_ge(cb_step, TOPK * t + k + 1 + CR)

            def mix(m, evac, at_chunk=None, at_step=None):
                def split(c, j):
                    k = m.step(c, j)
                    dve.wait_ge(m.act_done, at(k))
                    dve.wait_ge(m.second_done, at(k - 4))
                    dve.tensor_scalar(ah[:, j % 4, :], att[:, j % 2, :], m.split, None, ALU.mult
                                      ).then_inc(m.hi_done, 1)
                    dve.wait_ge(m.hi_done, at(k))
                    low(al[:, j % 4, :], att[:, j % 2, :], m.split, ah[:, j % 4, :], m.lo_done)

                def chunk(c, i, g, more):
                    for j in range(2, m.nt):
                        if j == 7 and at_chunk:
                            at_chunk(c, i, g)
                        split(c, j)
                        if at_step:
                            at_step(c, j)
                    if more or i == 0:
                        for j in range(2):
                            split(c + 1, j)
                            if at_step:
                                at_step(c + 1, j)
                    dve.wait_ge(m.second_done, at(m.step(c, m.nt - 1)))
                    dve.wait_ge(m.stored[i], m.st(g))
                    evac(m, c, i)
                for j in range(2):
                    split(0, j)
                    if at_step:
                        at_step(0, j)
                by(dve, m.nch, 2, chunk)

            def two(ap):
                return spread(ap[:, :].rearrange("p (o d) -> p o d", o=1), 1, 2)

            def half(h, i):
                return a_bank[2 * i + h][:, :].rearrange("p (o d) -> p o d", o=2)

            def evac_attention(m, c, i):
                for h in range(2):
                    ins = dve.scalar_tensor_tensor(out=xin[:, i, 2 * h:2 * h + 2, :], in0=half(h, i),
                                                   scalar=1.0 / (ATT_S * V_S), in1=two(bo_b), op0=ALU.mult,
                                                   op1=ALU.add)
                ins.then_inc(m.evac_read, 1)
                dve.wait_ge(m.evac_read, at(m.ch(c)))
                for h in range(2):
                    ins = dve.tensor_tensor(xin[:, i, 2 * h:2 * h + 2, :], xin[:, i, 2 * h:2 * h + 2, :], two(ls_b),
                                            ALU.mult)
                ins.then_inc(m.evac_done, 1)

            shared_expert()
            before = end_rt
            for b in range(B):
                first_t = b * (S // P)
                gate(dve, before)
                if b == 1:
                    for j, (blocks, hi, lo, scale) in enumerate(late_jobs[:LATE_LO]):
                        dve.wait_ge(w_hi, len(jobs) + j + 1)
                        low(lo, job_ps(j), scale, hi, w_lo)
                    gate(dve, end_late)

                def row_moments(t, i):
                    dve.wait_ge(pj["mm"], at(first_t + t))
                    dve.wait_ge(pj["qkn"], at(first_t + t - 2))
                    moments(lambda m: s_bank[i % 4][:, m * D:(m + 1) * D], 2, i % 2, first_t + t, pj,
                            EPS * QK_PS * QK_PS)
                    dve.wait_ge(pj["vhi"], at(first_t + t))
                    rows_t = bass.ds(t, 1)
                    low(vp[1][:, rows_t, :].rearrange("p o e -> p (o e)"), a_bank[2 + i % 2][:, 0:D], V_S / VP_PS,
                        vp[0][:, rows_t, :].rearrange("p o e -> p (o e)"), pj["vlo"])

                def shift_qk(t, i):
                    dve.wait_ge(pj["rs"], at(first_t + t))
                    dve.scalar_tensor_tensor(out=nmr[:, i % 2, 0:2], in0=mv[:, i % 2, 0:2, 0], scalar=-1.0,
                                             in1=rstd[:, i % 2, 0:2], op0=ALU.mult, op1=ALU.mult
                                             ).then_inc(pj["nmr"], 1)

                def rows_lo(t, i, g, more):
                    if more or i < 3:
                        shift_qk(t + 1, i + 1)
                    if more or i < 2:
                        row_moments(t + 2, i + 2)
                    dve.wait_ge(pj["thi"], at(first_t + t))
                    cols = bass.ds(t * P, P)
                    low(qkT[1][:, :, cols], a_bank[i % 2][:, :].rearrange("p (k c) -> p k c", k=2 * KC), X_S,
                        qkT[0][:, :, cols], pj["tlo"])
                row_moments(0, 0)
                row_moments(1, 1)
                shift_qk(0, 0)
                by(dve, S // P, 4, rows_lo)
                gate(dve, end_pj[b])
                mix(at_mix[b], evac_attention, at_step=combine if b == 1 else None)
                if b == 1:
                    experts_silu(TT - 1, (TT - 1) % 2)
                before = end_mix(at_mix[b])
                if b == 0:
                    routed_experts()
                    before = end_mo

            def add_up(c, i, g):
                dve.wait_ge(q4["m2"], at(c))
                dve.wait_ge(q4_ld[i], 16 * g + 16)
                dve.tensor_tensor(xin[:, i, :, :], xin[:, i, :, :], gin[i], ALU.add).then_inc(q4["x1"], 1)
                dve.wait_ge(q4["x1"], at(c))
                moments(lambda m: xin[:, i, m, :], G4, i, c, q4, EPS)

            def lo_rows(c, i):
                for b in range(2):
                    low_of(c, i, b, s_bank[0:2], xT, X_S, q4["h1"], q4["l1"])

            def lo_queries(c, i):
                for b in range(2):
                    low_of(c, i, b, s_bank[2:4], qsT, QS_S, q4["h2"], q4["l2"])

            def second_block(c, i, g, more):
                if more or i == 0:
                    shifts(c + 1, 1 - i, q4)
                if more:
                    add_up(c + 2, i, g + 1)
                dve.wait_ge(q4["gm"], at(c))
                dve.wait_ge(q4["rn"], at(c - 2))
                for m in range(G4):
                    ins = dve.tensor_tensor_reduce(out=junk[:, m, :], in0=a_bank[m][:, 0:D], in1=xn[:, i, m, :],
                                                   scale=1.0 / (X_S * GRAM_S * NB), scalar=0.0, op0=ALU.mult,
                                                   op1=ALU.add, accum_out=nn2[:, i, m:m + 1])
                ins.then_inc(q4["nn"], 1)
                if more or i == 0:
                    lo_rows(c + 1, 1 - i)
                if not first_step(c):
                    lo_queries(c - 1, 1 - i)
            add_up(0, 0, 0)
            gate(dve, before)
            for i in range(2):
                dve.wait_ge(cb_st[i], 16 * (TT // 2) + 16)
            shifts(0, 0, q4)
            add_up(1, 1, 0)
            lo_rows(0, 0)
            dve.wait_ge(gram_hi, 1)
            low(gram[1][:, :, :], a_bank[0][:, :].rearrange("p (k c) -> p k c", k=KC), GRAM_S / (K_S * K_S),
                gram[0][:, :, :], gram_lo)
            by(dve, NCH, 2, second_block, head=2)
            lo_queries(NCH - 1, 1)

            def evac_ffn(m, c, i):
                for h in range(2):
                    ins = dve.scalar_tensor_tensor(out=fbuf[i][:, 2 * h:2 * h + 2, :], in0=half(h, i),
                                                   scalar=1.0 / GE_S, in1=two(b2_b), op0=ALU.mult, op1=ALU.add)
                ins.then_inc(m.evac_read, 1)
                dve.wait_ge(m.evac_read, at(m.ch(c)))
                dve.sem_inc(m.evac_done, 1)
            gate(dve, end_q4)

            def bank_lo(c, i, g):
                dve.wait_ge(vb_hi, at(c))
                rows_c = bass.ds(c * VB_N, VB_N)
                low(vb[1][:, rows_c, :], st_vb[:, rows_c, :], K_S, vb[0][:, rows_c, :], vb_lo)
            mix(ff_mix, evac_ffn, bank_lo)

            def silu2(c, i, g):
                dve.wait_ge(bk_tanh, at(c))
                dve.wait_ge(bk_ld[i], 32 * g + 32)
                dve.scalar_tensor_tensor(out=gl[i], in0=tbuf[i], scalar=1.0, in1=gl[i], op0=ALU.add, op1=ALU.mult
                                         ).then_inc(bk_silu, 1)

            def evac_bank(m, c, i):
                dve.wait_ge(bk_silu, at(c))
                for h in range(2):
                    ins = dve.scalar_tensor_tensor(out=gl[i][:, 2 * h:2 * h + 2, :], in0=half(h, i),
                                                   scalar=0.5 / (GE_S * K_S), in1=gl[i][:, 2 * h:2 * h + 2, :],
                                                   op0=ALU.mult, op1=ALU.mult)
                ins.then_inc(m.evac_read, 1)
                dve.wait_ge(m.evac_read, at(m.ch(c)))
                dve.tensor_tensor(fbuf[i], gl[i], xl[i], ALU.add).then_inc(m.evac_done, 1)
            mix(bk_mix, evac_bank, silu2)


_INS = ["L0_attn_x", "L0_attn_Wq", "L0_attn_bq", "L0_attn_Wk", "L0_attn_bk", "L0_attn_Wv", "L0_attn_bv",
        "L0_attn_Wo", "L0_attn_bo", "L0_attn_layerscale", "L0_ffn_router_weight", "L0_ffn_e_bias",
        "L0_ffn_gate_w", "L0_ffn_up_w", "L0_ffn_down_w", "L0_ffn_sh_gate_w", "L0_ffn_sh_up_w",
        "L0_ffn_sh_down_w", "L1_attn_k", "L1_attn_v", "L1_ffn_W1", "L1_ffn_b1", "L1_ffn_W2", "L1_ffn_b2"]


def kernel(**inputs):
    import numpy as _np
    import concourse.bacc as _bacc
    from concourse import mybir as _mybir
    from concourse.bass_utils import run_bass_kernel_spmd as _run

    nc = _bacc.Bacc("TRN2", target_bir_lowering=False, num_devices=1)
    arrays, args = {}, {}
    for name in _INS:
        v = _np.ascontiguousarray(inputs[name])
        arrays[f"in_{name}_dram"] = v
        args[name] = nc.dram_tensor(f"in_{name}_dram", v.shape, _mybir.dt.from_np(v.dtype), kind="ExternalInput").ap()
    result = nc.dram_tensor("out_0_dram", (B, S, D), F32, kind="ExternalOutput").ap()
    build(nc, args, result)
    r = _run(nc, [arrays], core_ids=[0])
    return r.results[0]["out_0_dram"]
```
